# Optimizing a Trainium2 kernel written in Bass

```python
import numpy as np
import jax
import jax.numpy as jnp

def _softmax(x, axis=-1):
    return jax.nn.softmax(x, axis=axis)

def _gelu(x):
    return jax.nn.gelu(x, approximate=True)

def _silu(x):
    return jax.nn.silu(x)

def _sigmoid(x):
    return jax.nn.sigmoid(x)

def _layernorm(x, axis=-1, eps=1e-05):
    m = jnp.mean(x, axis=axis, keepdims=True)
    v = jnp.var(x, axis=axis, keepdims=True)
    return (x - m) / jnp.sqrt(v + eps)

def _scatter_add(tgt, idx, src, axis=0):
    return tgt.at[idx].add(src)

def _segment_sum(src, seg, n):
    return jax.ops.segment_sum(src, seg, n)
kernel_name = 'mk_early_fusion_d1_tok_img1024_r4_a51727'

def setup_inputs(seed: int=0):
    np.random.seed(seed)
    _w = jnp.asarray

    def _rec_inputs():
        import jax
        import jax.numpy as jnp
        _rk = jax.random.key(seed)
        x = -0.00016672 + 0.999947 * jax.random.normal(jax.random.fold_in(_rk, 1), (16, 3, 96, 96), jnp.float32)
        txt = -0.000312475 + 0.578156 * jax.random.normal(jax.random.fold_in(_rk, 2), (16, 77, 256), jnp.float32)
        return (x, txt)
    x, txt = _rec_inputs()

    def _L0_tok_setup():
        import jax, jax.numpy as jnp
        import numpy as np
        IMAGE_SIZE = 96
        PATCH = 16
        N_EMBD = 256
        C = 3
        N_PATCHES = (IMAGE_SIZE // PATCH) ** 2
        PATCH_DIM = C * PATCH * PATCH
        key = jax.random.key(seed)
        kx, kw, kb, kp = jax.random.split(key, 4)
        B = 64
        x = jax.random.normal(kx, (B, C, IMAGE_SIZE, IMAGE_SIZE), dtype=jnp.float32)
        bound = 1.0 / np.sqrt(PATCH_DIM)
        W = jax.random.uniform(kw, (N_EMBD, PATCH_DIM), minval=-bound, maxval=bound, dtype=jnp.float32)
        b = jax.random.uniform(kb, (N_EMBD,), minval=-bound, maxval=bound, dtype=jnp.float32)
        pos_embd = jax.random.normal(kp, (1, N_PATCHES, N_EMBD), dtype=jnp.float32) * 0.02
        return {'x': x, 'W': W, 'b': b, 'pos_embd': pos_embd}
    _L0_tok_all = _L0_tok_setup()
    _L0_tok_in = {k: v for k, v in _L0_tok_all.items() if k in ('W', 'b', 'pos_embd')}
    del _L0_tok_all

    def _L0_attn_setup():
        import jax, jax.numpy as jnp
        import numpy as np
        D_MODEL = 256
        STATE = 64
        HEADS = 8
        EXPAND = 2
        INNER = EXPAND * D_MODEL
        HEAD_DIM = INNER // HEADS
        PROJ_OUT = 2 * INNER + 2 * STATE + HEADS
        BATCH, SEQ = (2, 256)
        EPS = 1e-05

        def _layer_norm(x, gamma, beta):
            mu = jnp.mean(x, axis=-1, keepdims=True)
            xc = x - mu
            var = jnp.mean(xc * xc, axis=-1, keepdims=True)
            return xc * jax.lax.rsqrt(var + EPS) * gamma + beta

        def _mamba2(u, W_in, b_in, A_log, D_skip, dt_bias, W_out, b_out):
            B, L, _ = u.shape
            zxbcdt = u @ W_in + b_in
            z = zxbcdt[..., :INNER]
            xs = zxbcdt[..., INNER:2 * INNER].reshape(B, L, HEADS, HEAD_DIM)
            Bm = zxbcdt[..., 2 * INNER:2 * INNER + STATE]
            Cm = zxbcdt[..., 2 * INNER + STATE:2 * INNER + 2 * STATE]
            dt = jax.nn.softplus(zxbcdt[..., 2 * INNER + 2 * STATE:] + dt_bias)
            A = -jnp.exp(A_log)
            decay = jnp.exp(dt * A)
            dtx = dt[..., None] * xs

            def step(h, inp):
                dec_t, dtx_t, B_t, C_t = inp
                h = dec_t[:, :, None, None] * h + dtx_t[..., None] * B_t[:, None, None, :]
                y = jnp.einsum('bhpn,bn->bhp', h, C_t)
                return (h, y)
            h0 = jnp.zeros((B, HEADS, HEAD_DIM, STATE), u.dtype)
            scan_in = (jnp.moveaxis(decay, 1, 0), jnp.moveaxis(dtx, 1, 0), jnp.moveaxis(Bm, 1, 0), jnp.moveaxis(Cm, 1, 0))
            _, ys = jax.lax.scan(step, h0, scan_in)
            y = jnp.moveaxis(ys, 0, 1)
            y = y + D_skip[None, None, :, None] * xs
            y = y.reshape(B, L, INNER) * jax.nn.silu(z)
            return y @ W_out + b_out
        key = jax.random.key(seed)
        ks = jax.random.split(key, 6)
        g = lambda k, shape, sc: jax.random.normal(k, shape, jnp.float32) * sc
        return {'input_tensor': jax.random.normal(ks[0], (BATCH, SEQ, D_MODEL), jnp.float32), 'ln_gamma': jnp.ones((D_MODEL,), jnp.float32), 'ln_beta': jnp.zeros((D_MODEL,), jnp.float32), 'W_in': g(ks[1], (D_MODEL, PROJ_OUT), 0.02), 'b_in': jnp.zeros((PROJ_OUT,), jnp.float32), 'A_log': jnp.log(jnp.arange(1, HEADS + 1, dtype=jnp.float32)), 'D_skip': jnp.ones((HEADS,), jnp.float32), 'dt_bias': g(ks[2], (HEADS,), 0.1), 'W_out': g(ks[3], (INNER, D_MODEL), 0.02), 'b_out': jnp.zeros((D_MODEL,), jnp.float32)}
    _L0_attn_all = _L0_attn_setup()
    _L0_attn_in = {k: v for k, v in _L0_attn_all.items() if k in ('ln_gamma', 'ln_beta', 'W_in', 'b_in', 'A_log', 'D_skip', 'dt_bias', 'W_out', 'b_out')}
    del _L0_attn_all

    def _L0_ffn_setup():
        import jax, jax.numpy as jnp
        import numpy as np
        B, S, D, F, E = (2, 512, 256, 1024, 8)
        LN_EPS = 1e-05

        def _layer_norm(x, gamma, beta):
            mu = jnp.mean(x, axis=-1, keepdims=True)
            var = jnp.mean(jnp.square(x - mu), axis=-1, keepdims=True)
            return (x - mu) * jax.lax.rsqrt(var + LN_EPS) * gamma + beta
        key = jax.random.key(seed)
        ks = jax.random.split(key, 8)

        def xavier(k, shape):
            fan_in, fan_out = (shape[-1], shape[-2])
            a = jnp.sqrt(6.0 / (fan_in + fan_out))
            return jax.random.uniform(k, shape, jnp.float32, -a, a)
        return {'tgt': jax.random.normal(ks[0], (B, S, D), jnp.float32), 'Wr': xavier(ks[1], (E, D)), 'br': jnp.zeros((E,), jnp.float32), 'W1': xavier(ks[2], (E, F, D)), 'b1': jnp.zeros((E, F), jnp.float32), 'W2': xavier(ks[3], (E, D, F)), 'b2': jnp.zeros((E, D), jnp.float32), 'gamma': jnp.ones((D,), jnp.float32), 'beta': jnp.zeros((D,), jnp.float32)}
    _L0_ffn_all = _L0_ffn_setup()
    _L0_ffn_in = {k: v for k, v in _L0_ffn_all.items() if k in ('Wr', 'br', 'W1', 'b1', 'W2', 'b2', 'gamma', 'beta')}
    del _L0_ffn_all
    return {'x': x, 'txt': txt, 'L0_tok_W': _L0_tok_in['W'], 'L0_tok_b': _L0_tok_in['b'], 'L0_tok_pos_embd': _L0_tok_in['pos_embd'], 'L0_attn_ln_gamma': _L0_attn_in['ln_gamma'], 'L0_attn_ln_beta': _L0_attn_in['ln_beta'], 'L0_attn_W_in': _L0_attn_in['W_in'], 'L0_attn_b_in': _L0_attn_in['b_in'], 'L0_attn_A_log': _L0_attn_in['A_log'], 'L0_attn_D_skip': _L0_attn_in['D_skip'], 'L0_attn_dt_bias': _L0_attn_in['dt_bias'], 'L0_attn_W_out': _L0_attn_in['W_out'], 'L0_attn_b_out': _L0_attn_in['b_out'], 'L0_ffn_Wr': _L0_ffn_in['Wr'], 'L0_ffn_br': _L0_ffn_in['br'], 'L0_ffn_W1': _L0_ffn_in['W1'], 'L0_ffn_b1': _L0_ffn_in['b1'], 'L0_ffn_W2': _L0_ffn_in['W2'], 'L0_ffn_b2': _L0_ffn_in['b2'], 'L0_ffn_gamma': _L0_ffn_in['gamma'], 'L0_ffn_beta': _L0_ffn_in['beta']}

def reference(x, txt, L0_tok_W, L0_tok_b, L0_tok_pos_embd, L0_attn_ln_gamma, L0_attn_ln_beta, L0_attn_W_in, L0_attn_b_in, L0_attn_A_log, L0_attn_D_skip, L0_attn_dt_bias, L0_attn_W_out, L0_attn_b_out, L0_ffn_Wr, L0_ffn_br, L0_ffn_W1, L0_ffn_b1, L0_ffn_W2, L0_ffn_b2, L0_ffn_gamma, L0_ffn_beta):
    import jax
    import jax.numpy as jnp

    def _L0_tok_ref(x, W, b, pos_embd):
        import jax, jax.numpy as jnp
        import numpy as np
        IMAGE_SIZE = 96
        PATCH = 16
        N_EMBD = 256
        C = 3
        N_PATCHES = (IMAGE_SIZE // PATCH) ** 2
        PATCH_DIM = C * PATCH * PATCH
        B, Cc, H, Wd = x.shape
        p = PATCH
        Hp, Wp = (H // p, Wd // p)
        patches = x.reshape(B, Cc, Hp, p, Wp, p)
        patches = patches.transpose(0, 2, 4, 1, 3, 5)
        patches = patches.reshape(B, Hp * Wp, Cc * p * p)
        out = jnp.einsum('bnd,ed->bne', patches, W) + b + pos_embd
        return out

    def _L0_attn_ref(input_tensor, ln_gamma, ln_beta, W_in, b_in, A_log, D_skip, dt_bias, W_out, b_out):
        import jax, jax.numpy as jnp
        import numpy as np
        D_MODEL = 256
        STATE = 64
        HEADS = 8
        EXPAND = 2
        INNER = EXPAND * D_MODEL
        HEAD_DIM = INNER // HEADS
        PROJ_OUT = 2 * INNER + 2 * STATE + HEADS
        BATCH, SEQ = (2, 256)
        EPS = 1e-05

        def _layer_norm(x, gamma, beta):
            mu = jnp.mean(x, axis=-1, keepdims=True)
            xc = x - mu
            var = jnp.mean(xc * xc, axis=-1, keepdims=True)
            return xc * jax.lax.rsqrt(var + EPS) * gamma + beta

        def _mamba2(u, W_in, b_in, A_log, D_skip, dt_bias, W_out, b_out):
            B, L, _ = u.shape
            zxbcdt = u @ W_in + b_in
            z = zxbcdt[..., :INNER]
            xs = zxbcdt[..., INNER:2 * INNER].reshape(B, L, HEADS, HEAD_DIM)
            Bm = zxbcdt[..., 2 * INNER:2 * INNER + STATE]
            Cm = zxbcdt[..., 2 * INNER + STATE:2 * INNER + 2 * STATE]
            dt = jax.nn.softplus(zxbcdt[..., 2 * INNER + 2 * STATE:] + dt_bias)
            A = -jnp.exp(A_log)
            decay = jnp.exp(dt * A)
            dtx = dt[..., None] * xs

            def step(h, inp):
                dec_t, dtx_t, B_t, C_t = inp
                h = dec_t[:, :, None, None] * h + dtx_t[..., None] * B_t[:, None, None, :]
                y = jnp.einsum('bhpn,bn->bhp', h, C_t)
                return (h, y)
            h0 = jnp.zeros((B, HEADS, HEAD_DIM, STATE), u.dtype)
            scan_in = (jnp.moveaxis(decay, 1, 0), jnp.moveaxis(dtx, 1, 0), jnp.moveaxis(Bm, 1, 0), jnp.moveaxis(Cm, 1, 0))
            _, ys = jax.lax.scan(step, h0, scan_in)
            y = jnp.moveaxis(ys, 0, 1)
            y = y + D_skip[None, None, :, None] * xs
            y = y.reshape(B, L, INNER) * jax.nn.silu(z)
            return y @ W_out + b_out
        normed = _layer_norm(input_tensor, ln_gamma, ln_beta)
        out = _mamba2(normed, W_in, b_in, A_log, D_skip, dt_bias, W_out, b_out)
        return input_tensor + out

    def _L0_ffn_ref(tgt, Wr, br, W1, b1, W2, b2, gamma, beta):
        import jax, jax.numpy as jnp
        import numpy as np
        B, S, D, F, E = (2, 512, 256, 1024, 8)
        LN_EPS = 1e-05

        def _layer_norm(x, gamma, beta):
            mu = jnp.mean(x, axis=-1, keepdims=True)
            var = jnp.mean(jnp.square(x - mu), axis=-1, keepdims=True)
            return (x - mu) * jax.lax.rsqrt(var + LN_EPS) * gamma + beta
        logits = jnp.einsum('bsd,ed->bse', tgt, Wr) + br
        top_v, top_i = jax.lax.top_k(logits, 2)
        top_w = jax.nn.softmax(top_v, axis=-1)
        n_exp = logits.shape[-1]
        router_w = jnp.sum(jax.nn.one_hot(top_i, n_exp, dtype=top_w.dtype) * top_w[..., None], axis=-2)
        h = jnp.einsum('bsd,efd->bsef', tgt, W1) + b1
        h = jax.nn.relu(h)
        o = jnp.einsum('bsef,edf->bsed', h, W2) + b2
        tgt2 = jnp.einsum('bsed,bse->bsd', o, router_w)
        return _layer_norm(tgt + tgt2, gamma, beta)
    h = _L0_tok_ref(x, L0_tok_W, L0_tok_b, L0_tok_pos_embd)
    h = jnp.concatenate([h, txt], axis=1)
    h = h + _L0_attn_ref(_layernorm(h, axis=-1), L0_attn_ln_gamma, L0_attn_ln_beta, L0_attn_W_in, L0_attn_b_in, L0_attn_A_log, L0_attn_D_skip, L0_attn_dt_bias, L0_attn_W_out, L0_attn_b_out)
    h = h + _L0_ffn_ref(_layernorm(h, axis=-1), L0_ffn_Wr, L0_ffn_br, L0_ffn_W1, L0_ffn_b1, L0_ffn_W2, L0_ffn_b2, L0_ffn_gamma, L0_ffn_beta)
    return h

_drawn_inputs = setup_inputs


def setup_inputs(seed=0):
    import zlib

    import numpy as np

    out = dict(_drawn_inputs(seed))
    spreads = {'L0_attn_ln_gamma': (1.0, 0.6),
     'L0_attn_ln_beta': (0.0, 0.8),
     'L0_attn_b_in': (0.0, 0.447),
     'L0_attn_D_skip': (1.0, 0.6),
     'L0_attn_b_out': (0.0, 0.1),
     'L0_ffn_br': (0.0, 0.1),
     'L0_ffn_b1': (0.0, 0.319),
     'L0_ffn_b2': (0.0, 0.282),
     'L0_ffn_gamma': (1.0, 0.2),
     'L0_ffn_beta': (0.0, 0.1)}
    factors = {'L0_attn_A_log': 8.0, 'L0_attn_dt_bias': 8.0}
    for name, (base, spread) in spreads.items():
        noise = np.random.default_rng([zlib.crc32(name.encode()), seed]).standard_normal(out[name].shape)
        drawn = base * np.exp(spread * noise) if base else spread * noise
        out[name] = jnp.asarray(drawn.astype(out[name].dtype))
    for name, factor in factors.items():
        out[name] = (out[name] * factor).astype(out[name].dtype)
    return out
```

```python
from contextlib import ExitStack

import numpy as np
import concourse.bass as bass
from concourse import mybir

F32 = mybir.dt.float32
F32R = mybir.dt.float32r
U32 = mybir.dt.uint32
ALU = mybir.AluOpType
ACT = mybir.ActivationFunctionType

BATCH, IMG, TXT, DIM = 16, 36, 77, 256
LEN = IMG + TXT
TOK = BATCH * LEN
PATCH = 768
INNER, STATE, HEADS, HEAD = 512, 64, 8, 64
PROJ = 2 * INNER + 2 * STATE + HEADS
EXPERTS, HIDDEN = 8, 1024
EPS = 1e-5
P = 128
KP = PATCH // P
KD = DIM // P
KI = INNER // P
KF = HIDDEN // P
CHUNKS = 4
CH = TOK // CHUNKS
HALF = BATCH * IMG // 2
HPB = 4
RING = 2
WPIECE = 1024
WPIECES = (KD * HIDDEN + KF * DIM) // WPIECE
RAWS = 2
HRING = 4
OFREE = 2 * CHUNKS
LAG = 2
STEPS = [(par, c, f) for par in range(2) for c in range(CHUNKS) for f in range(KF)]
DM = 17
C_Z, C_X, C_BC, C_DT = 0, INNER, 2 * INNER, 2 * INNER + 2 * STATE


def build(nc, d, out):
    with ExitStack() as ctx:
        def sem(name):
            return ctx.enter_context(nc.semaphore(name))

        top = [16512]

        def place(name, shape, dt=F32, at=None):
            size = 4
            for n in shape[1:]:
                size *= n
            size = -(-size // 32) * 32
            where = top[0] if at is None else at[0]
            t = nc.alloc_sbuf_tensor_at(name, list(shape), dt, offset=where)
            if at is None:
                top[0] += size
            else:
                at[0] += size
            return t

        h_all = place("h_all", [LEN, BATCH * DIM])
        hn_all = place("hn_all", [LEN, BATCH * DIM])
        thi = place("thi", [P, KD, TOK], F32R)
        tlo = place("tlo", [P, KD, TOK], F32R)
        ident = place("ident", [P, P])
        delta = place("delta", [LEN, HPB * LEN])
        iota8 = place("iota8", [LEN, BATCH * EXPERTS])
        rowmask = place("rowmask", [LEN, 1])
        over_b = [top[0]]
        bx = place("bx", [LEN, INNER])
        bz = place("bz", [LEN, INNER])
        tmp = place("tmp", [P, KD, CH], at=over_b)
        posb = place("posb", [IMG, DIM])
        tokb = place("tokb", [IMG, DIM])
        bout = place("bout", [LEN, DIM])
        fgam = place("fgam", [LEN, DIM])
        fbet = place("fbet", [LEN, DIM])
        b_bc = place("b_bc", [P, 1])
        gam_t = place("gam_t", [P, KD])
        bet_t = place("bet_t", [P, KD])
        b1_t = place("b1_t", [P, EXPERTS * KF])
        b2_t = place("b2_t", [P, EXPERTS * KD])
        rows8 = place("rows8", [LEN, 5 * HEADS])
        bdt = place("bdt", [LEN, HEADS])
        exp_a = place("exp_a", [LEN, HEADS])
        wr = place("wr", [P, KD, EXPERTS])
        mhalf = place("mhalf", [LEN, BATCH])
        stats = place("stats", [LEN, BATCH * 6])
        mv = place("mv", [LEN, BATCH * 2])
        mv2 = place("mv2", [LEN, BATCH * 2])
        ve = place("ve", [LEN, BATCH])
        rstd = place("rstd", [LEN, BATCH])
        rstd2 = place("rstd2", [LEN, BATCH])
        dt_all = place("dt_all", [LEN, BATCH * HEADS])
        dec_all = place("dec_all", [LEN, BATCH * HEADS])
        logit = place("logit", [LEN, BATCH * EXPERTS])
        mx8 = place("mx8", [LEN, BATCH * 8])
        ix8 = place("ix8", [LEN, BATCH * 8], U32)
        t128 = [place(f"t128_{i}", [LEN, BATCH * HEADS]) for i in range(6)]
        t16 = [place(f"t16_{i}", [LEN, BATCH]) for i in range(6)]
        rw_t = place("rw_t", [P, LEN])
        raw = place("raw", [P, RAWS, WPIECE])
        phase = top[0]

        a = [phase]
        xs_all = place("xs_all", [LEN, BATCH * INNER], at=a)
        sz_all = place("sz_all", [LEN, BATCH * INNER], at=a)
        s_all = place("s_all", [LEN, BATCH * LEN], at=a)
        w_out = place("w_out", [P, KI, DIM], at=a)
        work = a[0]
        a = [work]
        w_in = place("w_in", [P, KD, PROJ], at=a)
        nslot = [place(f"nslot{i}", [LEN, DIM], at=a) for i in range(RING)]
        nt = [place(f"nt{i}", [P, KD, LEN], at=a) for i in range(RING)]
        bct = [place(f"bct{i}", [P, LEN], at=a) for i in range(RING)]
        ct = [place(f"ct{i}", [STATE, LEN], at=a) for i in range(RING)]
        zt = [place(f"zt{i}", [LEN, INNER], at=a) for i in range(RING)]
        assert a[0] <= nc.sbuf_top
        b = [phase]
        patch = place("patch", [P, KP, BATCH * IMG], at=b)
        w_tok = place("w_tok", [P, KP, DIM], at=b)
        emb_t = place("emb_t", [P, KD, BATCH * IMG], at=b)
        a = [work]
        decs = [place(f"decs{i}", [LEN, HEADS], at=a) for i in range(RING)]
        dtx = [place(f"dtx{i}", [LEN, INNER], at=a) for i in range(RING)]
        xsd = [place(f"xsd{i}", [LEN, INNER], at=a) for i in range(RING)]
        gm = [place(f"gm{i}", [LEN, HEADS * LEN], at=a) for i in range(RING)]
        yb = [place(f"yb{i}", [LEN, INNER], at=a) for i in range(RING)]
        yt = [place(f"yt{i}", [P, KI, LEN], at=a) for i in range(RING)]
        tslot = [place(f"tslot{i}", [LEN, DIM], at=a) for i in range(RING)]
        tt = [place(f"tt{i}", [P, KD, LEN], at=a) for i in range(RING)]
        est = [place(f"est{i}", [LEN, 6], at=a) for i in range(RING)]
        emv = [place(f"emv{i}", [LEN, 2], at=a) for i in range(RING)]
        eve = [place(f"eve{i}", [LEN, 1], at=a) for i in range(RING)]
        ers = [place(f"ers{i}", [LEN, 1], at=a) for i in range(RING)]
        assert a[0] <= nc.sbuf_top, (a[0], nc.sbuf_top)

        a = [phase]
        whi = [place(f"whi{i}", [P, WPIECES * WPIECE], F32R, at=a) for i in range(2)]
        wlo = [place(f"wlo{i}", [P, WPIECES * WPIECE], F32R, at=a) for i in range(2)]
        over_h = [a[0]]
        aslot = [place(f"aslot{i}", [P, KD, LEN], at=over_h) for i in range(RING)]
        hid = place("hid", [P, HRING, CH], at=a)
        hhi = place("hhi", [P, HRING, CH], F32R, at=a)
        hlo = place("hlo", [P, HRING, CH], F32R, at=a)
        acc = place("acc", [P, KD, TOK], at=a)
        rwb = place("rwb", [P, 2, TOK], at=a)
        assert a[0] <= nc.sbuf_top, (a[0], nc.sbuf_top)

        bank = [ctx.enter_context(nc.psum_tensor(f"bank{i}", [P, 512], F32)) for i in range(6)]
        pair = ctx.enter_context(nc.psum_tensor("pair", [P, 2, 512], F32))
        bank += [pair[:, 0, :], pair[:, 1, :]]
        rw_dram = nc.dram_tensor("rw_dram", [EXPERTS, TOK], F32).ap()

        settled = sem("settled")
        ld_tok, ld_h, ld_proj, ld_ssm, ld_row = (sem(n) for n in ("ld_tok", "ld_h", "ld_proj", "ld_ssm", "ld_row"))
        emb_mm, emb_sb, img_t, img_rows = (sem(n) for n in ("emb_mm", "emb_sb", "img_t", "img_rows"))
        ln, pw, res_done, bdt_done, expa_done = (sem(n) for n in ("ln", "pw", "res_done", "bdt_done", "expa_done"))
        ns_done, t_done, nt_done, bc_mm, dt_mm, xs_mm, z_mm, s_mm = (
            sem(n) for n in ("ns_done", "t_done", "nt_done", "bc_mm", "dt_mm", "xs_mm", "z_mm", "s_mm"))
        bc_ev, c_ev, dt_ev, xs_ev, z_ev, sz_done, s_ev = (
            sem(n) for n in ("bc_ev", "c_ev", "dt_ev", "xs_ev", "z_ev", "sz_done", "s_ev"))
        dm, em, dec_done, mixed = (sem(n) for n in ("dm", "em", "dec_done", "mixed"))
        prep_done, b_mm, scan_done, g_done, y_mm, ya_done, y2_done, t4_mm, yt_done, o_mm, h1_done = (
            sem(n) for n in ("prep_done", "b_mm", "scan_done", "g_done", "y_mm", "ya_done", "y2_done", "t4_mm",
                             "yt_done", "o_mm", "h1_done"))
        st_done, ag_done, ve_done, pow_done, tg_done, t2_mm, tc_done, tt_done, hi_done, lo_done, l_mm, lg_done, mxd, mi_done = (
            sem(n) for n in ("st_done", "ag_done", "ve_done", "pow_done", "tg_done", "t2_mm", "tc_done", "tt_done",
                             "hi_done", "lo_done", "l_mm", "lg_done", "mxd", "mi_done"))
        rt, rt_exp, rt_t, rt_sb, rt_out = (sem(n) for n in ("rt", "rt_exp", "rt_t", "rt_sb", "rt_out"))
        raw_in = [sem(f"raw_in{i}") for i in range(RAWS)]
        rw_in = [sem(f"rw_in{i}") for i in range(2)]
        whi_done, wlo_done, m1_mm, hhi_done, hlo_done, m2_step, o_ev, acc_zero, acc_done = (
            sem(n) for n in ("whi_done", "wlo_done", "m1_mm", "hhi_done", "hlo_done", "m2_step", "o_ev", "acc_zero",
                             "acc_done"))
        hb_done, as_done, f_t, u_done, fs_done, fin, out_done = (
            sem(n) for n in ("hb_done", "as_done", "f_t", "u_done", "fs_done", "fin", "out_done"))

        block = ctx.enter_context(nc.Block())

        def settle(eng):
            eng.sem_inc(settled, 1)

        def cols(b, n=DIM):
            return bass.ds(b * n, n)

        def pairs(eng, first, last, body):
            n = (last - first) // 2
            with eng.Fori(0, n) as p:
                for s in range(2):
                    body(p * 2 + (first + s), (first + s) % 2)
            for b in range(first + 2 * n, last):
                body(b, b % 2)

        def skewed(eng, stages, order):
            lags = [lag for lag, _ in stages]
            lo, hi = min(order), max(order)
            first, last = hi, BATCH + lo
            if (last - first) % 2:
                last -= 1

            def turn(i, ipar):
                for lag, f in stages:
                    if not isinstance(i, int) or 0 <= i - lag < BATCH:
                        f(i - lag, (ipar - lag) % 2)

            for i in range(lo, first):
                turn(i, i % 2)
            with eng.Fori(0, (last - first) // 2) as p:
                for s in range(2):
                    turn(p * 2 + (first + s), (first + s) % 2)
            for i in range(last, BATCH + hi):
                turn(i, i % 2)
            assert set(lags) <= set(order)

        LAGS = (-1, 0, 1, 2, 3)

        @block.sync
        def _(sp):
            sp.dma_start(patch[:, :, :], d["patch"]).then_inc(ld_tok, 16)
            sp.dma_start(w_tok[:, :, :], d["w_tok"]).then_inc(ld_tok, 16)
            sp.dma_start(ident[:, :], d["ident"]).then_inc(ld_tok, 16)
            sp.dma_start(h_all[IMG:LEN, :].rearrange("p (b c) -> p b c", b=BATCH),
                         d["txt"].rearrange("b t c -> t b c")).then_inc(ld_h, 16)
            sp.dma_start(w_in[:, :, :], d["w_in"]).then_inc(ld_proj, 16)
            sp.dma_start(b_bc[:, :], d["b_bc"]).then_inc(ld_proj, 16)
            sp.dma_start(gam_t[:, :], d["gam_t"]).then_inc(ld_proj, 16)
            sp.dma_start(bet_t[:, :], d["bet_t"]).then_inc(ld_proj, 16)
            sp.dma_start(delta[:, :], d["delta"]).then_inc(ld_ssm, 16)
            sp.dma_start(w_out[:, :, :], d["w_out"]).then_inc(ld_ssm, 16)
            sp.dma_start(wr[:, :, :], d["wr"]).then_inc(ld_ssm, 16)
            sp.dma_start(iota8[:, :], d["iota8"]).then_inc(ld_ssm, 16)
            sp.dma_start(b1_t[:, :], d["b1_t"]).then_inc(ld_ssm, 16)
            sp.dma_start(b2_t[:, :], d["b2_t"]).then_inc(ld_ssm, 16)

            with sp.Fori(0, EXPERTS // 2) as g:
                for half in range(2):
                    e = g * 2 + half
                    for q in range(WPIECES):
                        sp.wait_ge(wlo_done, e * WPIECES + (q + 1))
                        sp.dma_start(raw[:, q % RAWS, :],
                                     d["experts"][bass.ds(e, 1), :, q * WPIECE:(q + 1) * WPIECE].rearrange(
                                         "e p n -> (e p) n")).then_inc(raw_in[q % RAWS], 16)
                    if half == 0:
                        sp.wait_ge(rt_out, 16)
                        sp.wait_ge(mixed, 1)
                    sp.wait_ge(o_ev, e * CHUNKS + CHUNKS)
                    sp.dma_start(rwb[:, half, :], rw_dram[bass.ds(e, 1), :].partition_broadcast(P)
                                 ).then_inc(rw_in[half], 16)

            dst = out.rearrange("b t c -> t b c")
            for c in range(CHUNKS):
                sp.wait_ge(fin, (c + 1))
                sp.dma_start(dst[:, 4 * c:4 * c + 4, :],
                             h_all[:, c * 4 * DIM:(c + 1) * 4 * DIM].rearrange("p (b c) -> p b c", b=4)
                             ).then_inc(out_done, 16)
            sp.wait_ge(out_done, 16 * CHUNKS)

        @block.tensor
        def _(pe):
            pe.wait_ge(ld_tok, 48)
            for q in range(2 * KD):
                e, half = q // 2, q % 2
                for k in range(KP):
                    mm = pe.matmul(bank[q][:, 0:HALF], w_tok[:, k, e * P:(e + 1) * P],
                                   patch[:, k, half * HALF:(half + 1) * HALF], start=(k == 0), stop=(k == KP - 1))
                mm.then_inc(emb_mm, 1)
            pe.wait_ge(emb_sb, 2 * KD)
            for g in range(BATCH // 2):
                if g >= 4:
                    pe.wait_ge(img_rows, g - 3)
                for j in range(2 * KD):
                    bb, e = j // KD, j % KD
                    mm = pe.transpose(bank[4 + g % 4][0:IMG, j * P:(j + 1) * P],
                                      emb_t[:, e, (2 * g + bb) * IMG:(2 * g + bb + 1) * IMG], ident[:, :])
                mm.then_inc(img_t, 1)

            for s in (t_done, s_mm):
                pe.sem_inc(s, RING)
            pe.wait_ge(img_rows, BATCH // 2)
            pe.wait_ge(ld_proj, 64)

            def turn_rows(b, s):
                pe.wait_ge(ns_done, b + 1)
                pe.wait_ge(nt_done, b + 1)
                for k in range(KD):
                    mm = pe.transpose(bank[s][:, k * P:k * P + LEN], nslot[s][:, k * P:(k + 1) * P],
                                      ident[0:LEN, 0:LEN])
                mm.then_inc(t_done, 1)

            def project(b, s, ahead=True):
                pe.wait_ge(nt_done, b + 1 + RING)
                pe.wait_ge(bc_ev, b + 1)
                for k in range(KD):
                    mm = pe.matmul(bank[2][:, 0:LEN], w_in[:, k, C_BC:C_DT], nt[s][:, k, :],
                                   start=(k == 0), stop=(k == KD - 1))
                mm.then_inc(bc_mm, 1)
                pe.wait_ge(s_ev, b + 1)
                for k in range(KD):
                    mm = pe.matmul(bank[3][0:LEN, 256:256 + HEADS], nt[s][:, k, :], w_in[:, k, C_DT:PROJ],
                                   start=(k == 0), stop=(k == KD - 1))
                mm.then_inc(dt_mm, 1)
                pe.wait_ge(xs_ev, b + 1)
                for k in range(KD):
                    mm = pe.matmul(bank[4][0:LEN, :], nt[s][:, k, :], w_in[:, k, C_X:C_BC],
                                   start=(k == 0), stop=(k == KD - 1))
                mm.then_inc(xs_mm, 1)
                if ahead:
                    turn_rows(b + 1, 1 - s)
                pe.wait_ge(z_ev, b + 1)
                for k in range(KD):
                    mm = pe.matmul(bank[5][0:LEN, :], nt[s][:, k, :], w_in[:, k, C_Z:C_X],
                                   start=(k == 0), stop=(k == KD - 1))
                mm.then_inc(z_mm, 1)
                pe.wait_ge(c_ev, b + 1)
                pe.wait_ge(dt_ev, b + 1)
                pe.matmul(bank[3][0:LEN, 0:LEN], bct[s][0:STATE, :], ct[s][:, :],
                          start=True, stop=True).then_inc(s_mm, 1)

            turn_rows(0, 0)
            pairs(pe, 0, BATCH - 2, project)
            project(BATCH - 2, 0)
            project(BATCH - 1, 1, ahead=False)

            pe.wait_ge(ld_ssm, 96)
            for s in (b_mm, y_mm, t4_mm, t2_mm, o_mm, l_mm):
                pe.sem_inc(s, RING)
            pe.wait_ge(s_ev, BATCH + 1)
            pe.wait_ge(dt_ev, BATCH)
            pe.wait_ge(xs_ev, BATCH + 1)
            pe.wait_ge(z_ev, BATCH + 1)
            pe.wait_ge(bc_ev, BATCH + 1)

            def spread_decays(b, s):
                pe.wait_ge(prep_done, b + 1)
                pe.wait_ge(scan_done, b + 1)
                for h in range(HEADS):
                    mm = pe.transpose(pair[0:LEN, h // HPB, h % HPB * LEN:(h % HPB + 1) * LEN],
                                      decs[s][:, h:h + 1].to_broadcast([LEN, LEN]), ident[0:LEN, 0:LEN])
                mm.then_inc(b_mm, 1)

            def turn_target(b, s):
                pe.wait_ge(tg_done, b + 1)
                pe.wait_ge(tt_done, b + 1)
                for k in range(KD):
                    mm = pe.transpose(bank[3][:, k * P:k * P + LEN], tslot[s][:, k * P:(k + 1) * P],
                                      ident[0:LEN, 0:LEN])
                mm.then_inc(t2_mm, 1)

            def mix(b, s):
                pe.wait_ge(g_done, b + 1)
                pe.wait_ge(ya_done, b + 2)
                for h in range(HEADS):
                    mm = pe.matmul(bank[0][0:LEN, h * HEAD:(h + 1) * HEAD], gm[s][:, h * LEN:(h + 1) * LEN],
                                   dtx[s][:, h * HEAD:(h + 1) * HEAD], start=True, stop=True)
                mm.then_inc(y_mm, 1)

            def project_out(b, s):
                pe.wait_ge(yt_done, b + 1 + 1)
                pe.wait_ge(h1_done, b + 1)
                for k in range(KI):
                    mm = pe.matmul(bank[2][0:LEN, 0:DIM], yt[s][:, k, :], w_out[:, k, :],
                                   start=(k == 0), stop=(k == KI - 1))
                mm.then_inc(o_mm, 1)

            def logits(b, s):
                pe.wait_ge(tt_done, b + 1 + 1)
                pe.wait_ge(lg_done, b + 1)
                for k in range(KD):
                    mm = pe.matmul(bank[4][0:LEN, 0:EXPERTS], tt[s][:, k, :], wr[:, k, :],
                                   start=(k == 0), stop=(k == KD - 1))
                mm.then_inc(l_mm, 1)

            def turn_gated(b, s):
                pe.wait_ge(y2_done, b + 1)
                pe.wait_ge(yt_done, b + 1)
                for k in range(KI):
                    mm = pe.transpose(bank[1][:, k * P:k * P + LEN], yb[s][:, k * P:(k + 1) * P],
                                      ident[0:LEN, 0:LEN])
                mm.then_inc(t4_mm, 1)

            skewed(pe, [(0, spread_decays), (3, turn_target), (1, mix), (2, project_out), (3, logits),
                        (1, turn_gated)], LAGS)

            pe.wait_ge(rt, 11)
            pe.transpose(bank[5][:, 0:LEN], t128[4][:, :], ident[0:LEN, 0:LEN]).then_inc(rt_t, 1)

            pe.sem_inc(m2_step, HRING)
            pe.wait_ge(rt_sb, 1)
            pe.wait_ge(lo_done, BATCH + RING)

            def first_product(k, j, par, c, f):
                pe.wait_ge(hhi_done, k + 1)
                n = 0
                for w, x in ((whi, thi), (whi, tlo), (wlo, thi)):
                    for kk in range(KD):
                        at = kk * HIDDEN + f * P
                        mm = pe.matmul(bank[j % HRING][:, 0:CH], w[par][:, at:at + P],
                                       x[:, kk, c * CH:(c + 1) * CH], start=(n == 0), stop=(n == 3 * KD - 1))
                        n += 1
                mm.then_inc(m1_mm, 1)

            def second_product(k, j, par, c, f):
                pe.wait_ge(hlo_done, k + 1)
                for dt in range(KD):
                    for n, (w, x) in enumerate(((whi, hhi), (whi, hlo), (wlo, hhi))):
                        at = KD * HIDDEN + f * DIM + dt * P
                        mm = pe.matmul(bank[4 + 2 * (c % 2) + dt][:, 0:CH], w[par][:, at:at + P],
                                       x[:, j % HRING, :], start=(f == 0 and n == 0),
                                       stop=(f == KF - 1 and n == 2))
                mm.then_inc(m2_step, 1)

            with pe.Fori(0, EXPERTS // 2) as g:
                for j in range(len(STEPS) + LAG):
                    if j < len(STEPS):
                        par, c, f = STEPS[j]
                        if c == 0 and f == 0:
                            pe.wait_ge(wlo_done, g * (2 * WPIECES) + (par * WPIECES + WPIECES // 2 + RAWS))
                        first_product(g * len(STEPS) + j, j, par, c, f)
                    if j >= LAG:
                        par, c, f = STEPS[j - LAG]
                        if c == 0 and f == 0:
                            pe.wait_ge(wlo_done, g * (2 * WPIECES) + (par * WPIECES + WPIECES + RAWS))
                        if f == 0:
                            pe.wait_ge(o_ev, g * (2 * CHUNKS) + (par * CHUNKS + c + OFREE - 1))
                        second_product(g * len(STEPS) + (j - LAG), j - LAG, par, c, f)

            pe.sem_inc(f_t, RING)
            pe.wait_ge(hhi_done, EXPERTS * CHUNKS * KF + HRING)

            def turn_sum(b, s):
                pe.wait_ge(as_done, b + 1)
                pe.wait_ge(u_done, b + 1)
                for k in range(KD):
                    mm = pe.transpose(bank[s][0:LEN, k * P:(k + 1) * P], aslot[s][:, k, :], ident[:, :])
                mm.then_inc(f_t, 1)

            pairs(pe, 0, BATCH, turn_sum)

        @block.scalar
        def _(act):
            act.dma_start(posb[:, :], d["pos"]).then_inc(ld_h, 16)
            act.dma_start(tokb[:, :], d["tok_b"].partition_broadcast(IMG)).then_inc(ld_h, 16)
            act.dma_start(bout[:, :], d["b_out"].partition_broadcast(LEN)).then_inc(ld_row, 16)
            act.dma_start(rows8[:, :], d["rows8"].partition_broadcast(LEN)).then_inc(ld_row, 16)
            act.dma_start(bx[:, :], d["b_x"].partition_broadcast(LEN)).then_inc(ld_row, 16)
            act.dma_start(bz[:, :], d["b_z"].partition_broadcast(LEN)).then_inc(ld_row, 16)
            act.dma_start(rowmask[:, :], d["rowmask"]).then_inc(ld_row, 16)
            act.dma_start(fgam[:, :], d["f_gam"].partition_broadcast(LEN)).then_inc(ld_row, 16)
            act.dma_start(fbet[:, :], d["f_bet"].partition_broadcast(LEN)).then_inc(ld_row, 16)
            for q in range(2 * KD):
                e, half = q // 2, q % 2
                act.wait_ge(emb_mm, q + 1)
                act.activation(emb_t[:, e, half * HALF:(half + 1) * HALF], bank[q][:, 0:HALF],
                               ACT.Copy).then_inc(emb_sb, 1)
            act.wait_ge(ld_row, 112)
            act.activation(exp_a[:, :], rows8[:, 2 * HEADS:3 * HEADS], ACT.Exp).then_inc(expa_done, 1)

            act.sem_inc(nt_done, RING)
            for s in (bc_ev, s_ev):
                act.sem_inc(s, 1)
            act.wait_ge(ld_proj, 64)

            def norm_t(b, s):
                act.wait_ge(t_done, b + 1 + RING)
                act.wait_ge(s_mm, b + 1)
                for k in range(KD):
                    i = act.activation(nt[s][:, k, :], bank[s][:, k * P:k * P + LEN], ACT.Identity,
                                       bias=bet_t[:, k:k + 1], scale=gam_t[:, k:k + 1])
                i.then_inc(nt_done, 1)

            def evacuate(b, s, ahead=True):
                act.wait_ge(bc_mm, b + 1)
                act.wait_ge(s_mm, b + 1)
                act.activation(bct[s][:, :], bank[2][:, 0:LEN], ACT.Identity, bias=b_bc[:, 0:1]).then_inc(bc_ev, 1)
                act.wait_ge(bc_ev, b + 1 + 1)
                act.activation(ct[s][:, :], bct[s][STATE:P, :], ACT.Copy).then_inc(c_ev, 1)
                if ahead:
                    norm_t(b + 1, 1 - s)
                act.wait_ge(s_mm, b + 1 + RING)
                settle(act)
                act.activation(s_all[:, bass.ds(b * LEN, LEN)], bank[3][0:LEN, 0:LEN], ACT.Copy).then_inc(s_ev, 1)
                act.wait_ge(z_ev, b + 1 + 1)
                settle(act)
                act.activation(sz_all[:, cols(b, INNER)], zt[s][:, :], ACT.Silu).then_inc(sz_done, 1)

            act.sem_inc(sz_done, RING)
            norm_t(0, 0)
            pairs(act, 0, BATCH - 2, evacuate)
            evacuate(BATCH - 2, 0)
            evacuate(BATCH - 1, 1, ahead=False)

            act.wait_ge(dm, 2)
            act.activation(t128[2][:, :], t128[0][:, :], ACT.Exp).then_inc(em, 1)
            act.wait_ge(dm, DM)
            act.activation(dec_all[:, :], t128[3][:, :], ACT.Exp, bias=rowmask[:, 0:1], scale=-1.0).then_inc(dec_done, 1)

            for s in (tt_done, yt_done):
                act.sem_inc(s, 1)
            act.sem_inc(tc_done, RING)

            def keep_target(b, s):
                act.wait_ge(tg_done, b + 1)
                settle(act)
                act.activation(hn_all[:, cols(b)], tslot[s][:, :], ACT.Copy).then_inc(tc_done, 1)
                act.wait_ge(t2_mm, b + 1 + RING)
                act.wait_ge(l_mm, b + 1)
                act.wait_ge(lo_done, b + 1)
                act.activation(tt[s][:, :, :], bank[3][:, 0:KD * P].rearrange("p (k c) -> p k c", k=KD)[:, :, 0:LEN],
                               ACT.Copy).then_inc(tt_done, 1)
                act.wait_ge(tt_done, b + 1 + 1)
                settle(act)
                act.activation(thi[:, :, bass.ds(b * LEN, LEN)], tt[s][:, :, :], ACT.Copy).then_inc(hi_done, 1)

            def gated_t(b, s):
                act.wait_ge(t4_mm, b + 1 + RING)
                act.wait_ge(o_mm, b + 1)
                act.activation(yt[s][:, :, :], bank[1][:, :].rearrange("p (k c) -> p k c", k=KI)[:, :, 0:LEN],
                               ACT.Copy).then_inc(yt_done, 1)

            skewed(act, [(3, keep_target), (1, gated_t)], LAGS)

            act.wait_ge(rt, 1)
            act.activation(t16[1][:, :], t16[0][:, :], ACT.Exp).then_inc(rt_exp, 1)
            act.wait_ge(rt_t, 1)
            act.activation(rw_t[:, :], bank[5][:, 0:LEN], ACT.Copy).then_inc(rt_sb, 1)
            act.wait_ge(rt_sb, 1)
            act.dma_start(rw_dram.rearrange("e (b t) -> b e t", b=BATCH), rw_t[:, :]).then_inc(rt_out, 16)

            act.sem_inc(hhi_done, HRING)
            act.wait_ge(mixed, 1)
            with act.Fori(0, EXPERTS // 2) as g:
                for j, (par, c, f) in enumerate(STEPS):
                    k = g * len(STEPS) + j
                    bias = b1_t[:, bass.ds(g * (2 * KF) + (par * KF + f), 1)]
                    act.wait_ge(m1_mm, k + 1)
                    act.wait_ge(m2_step, k + 1)
                    settle(act)
                    act.activation(hid[:, j % HRING, :], bank[j % HRING][:, 0:CH], ACT.Relu, bias=bias)
                    act.activation(hhi[:, j % HRING, :], bank[j % HRING][:, 0:CH], ACT.Relu,
                                   bias=bias).then_inc(hhi_done, 1)

            act.wait_ge(acc_done, EXPERTS * CHUNKS)

            def slot_sum(b, s):
                act.wait_ge(f_t, b + 1)
                settle(act)
                act.activation(aslot[s][:, :, :], acc[:, :, bass.ds(b * LEN, LEN)], ACT.Copy).then_inc(as_done, 1)

            pairs(act, 0, BATCH, slot_sum)

        @block.vector
        def _(dve):
            dve.memset(mhalf[:, :], -0.5).then_inc(ln, 1)
            dve.wait_ge(ld_h, 48)
            dve.tensor_tensor(posb[:, :], posb[:, :], tokb[:, :], ALU.add).then_inc(ln, 1)
            dve.wait_ge(ln, 2)
            for g in range(BATCH // 2):
                dve.wait_ge(img_t, g + 1)
                dve.tensor_tensor(h_all[0:IMG, 2 * g * DIM:(2 * g + 2) * DIM].rearrange("p (b c) -> p b c", b=2),
                                  bank[4 + g % 4][0:IMG, :].rearrange("p (b c) -> p b c", b=2),
                                  posb[:, :].unsqueeze(1).to_broadcast([IMG, 2, DIM]),
                                  ALU.add).then_inc(img_rows, 1)
            dve.wait_ge(img_rows, BATCH // 2)

            def mean_var(rows, out_mv, base):
                with dve.Fori(0, BATCH) as b:
                    dve.bn_stats(stats[:, bass.ds(b * 6, 6)], rows[:, cols(b)]).then_inc(ln, 1)
                dve.wait_ge(ln, base + BATCH)
                for b in range(BATCH):
                    dve.bn_aggr(out_mv[:, 2 * b:2 * b + 2], stats[:, 6 * b:6 * b + 6]).then_inc(ln, 1)
                dve.wait_ge(ln, base + 2 * BATCH)
                dve.tensor_scalar(ve[:, :], out_mv[:, 1:2 * BATCH:2], EPS, None, ALU.add).then_inc(ln, 1)
                return base + 2 * BATCH + 1

            n = mean_var(h_all, mv, 2)
            dve.wait_ge(pw, 1)
            with dve.Fori(0, BATCH) as b:
                dve.tensor_scalar(hn_all[:, cols(b)], h_all[:, cols(b)], mv[:, bass.ds(b * 2, 1)],
                                  rstd[:, bass.ds(b, 1)], ALU.subtract, ALU.mult).then_inc(ln, 1)
            n += BATCH
            dve.wait_ge(ln, n)
            n = mean_var(hn_all, mv2, n)
            dve.wait_ge(ld_row, 112)
            dve.tensor_tensor(bdt[:, :], rows8[:, 0:HEADS], rows8[:, HEADS:2 * HEADS], ALU.add).then_inc(bdt_done, 1)
            dve.wait_ge(bdt_done, 1)
            dve.wait_ge(pw, 2)

            for s in (xs_ev, z_ev):
                dve.sem_inc(s, 1)

            def norm_rows(b, s):
                dve.wait_ge(t_done, b + 1)
                dve.tensor_scalar(nslot[s][:, :], hn_all[:, cols(b)], mv2[:, bass.ds(b * 2, 1)],
                                  rstd2[:, bass.ds(b, 1)], ALU.subtract, ALU.mult).then_inc(ns_done, 1)

            def add_biases(b, s, ahead=True):
                if ahead:
                    norm_rows(b + 1, 1 - s)
                dve.wait_ge(dt_mm, b + 1)
                dve.tensor_tensor(dt_all[:, cols(b, HEADS)], bank[3][0:LEN, 256:256 + HEADS], bdt[:, :],
                                  ALU.add).then_inc(dt_ev, 1)
                dve.wait_ge(xs_mm, b + 1)
                dve.tensor_tensor(xs_all[:, cols(b, INNER)], bank[4][0:LEN, :], bx[:, :], ALU.add).then_inc(xs_ev, 1)
                dve.wait_ge(z_mm, b + 1)
                dve.wait_ge(sz_done, b + 1)
                dve.tensor_tensor(zt[s][:, :], bank[5][0:LEN, :], bz[:, :], ALU.add).then_inc(z_ev, 1)

            norm_rows(0, 0)
            pairs(dve, 0, BATCH - 2, add_biases)
            add_biases(BATCH - 2, 0)
            add_biases(BATCH - 1, 1, ahead=False)

            count = [0]

            def step(i):
                count[0] += 1
                i.then_inc(dm, 1)
                dve.wait_ge(dm, count[0])

            x, neg, e_, q, q2 = dt_all, t128[0], t128[2], t128[4], t128[5]
            dve.wait_ge(dt_ev, BATCH)
            step(dve.tensor_scalar(t128[1][:, :], x[:, :], 0.0, None, ALU.max))
            step(dve.scalar_tensor_tensor(neg[:, :], x[:, :], -1.0, x[:, :], ALU.mult, ALU.min))
            dve.wait_ge(em, 1)
            step(dve.tensor_scalar(t128[3][:, :], e_[:, :], 2.0, None, ALU.add))
            step(dve.reciprocal(neg[:, :], t128[3][:, :]))
            step(dve.tensor_tensor(q[:, :], e_[:, :], neg[:, :], ALU.mult))
            step(dve.tensor_tensor(q2[:, :], q[:, :], q[:, :], ALU.mult))
            step(dve.tensor_scalar(t128[3][:, :], q2[:, :], 1.0 / 17, None, ALU.mult))
            for odd in range(15, 1, -2):
                step(dve.scalar_tensor_tensor(t128[3][:, :], t128[3][:, :], 1.0 / odd, q2[:, :], ALU.add, ALU.mult))
            step(dve.scalar_tensor_tensor(t128[3][:, :], t128[3][:, :], 1.0, q[:, :], ALU.add, ALU.mult))
            step(dve.scalar_tensor_tensor(dt_all[:, :], t128[3][:, :], 2.0, t128[1][:, :], ALU.mult, ALU.add))
            dve.wait_ge(expa_done, 1)
            step(dve.tensor_tensor(t128[3][:, :].rearrange("p (b h) -> p b h", h=HEADS),
                                   dt_all[:, :].rearrange("p (b h) -> p b h", h=HEADS),
                                   exp_a[:, :].unsqueeze(1).to_broadcast([LEN, BATCH, HEADS]), ALU.mult))
            assert count[0] == DM

            dve.wait_ge(ld_ssm, 96)
            for s in (scan_done, h1_done, lg_done):
                dve.sem_inc(s, 1)
            for s in (ya_done, lo_done):
                dve.sem_inc(s, RING)
            dve.wait_ge(s_ev, BATCH + 1)

            def scan(b, s):
                dve.wait_ge(b_mm, b + 1 + RING)
                dve.wait_ge(y_mm, b + 1)
                for h in range(HEADS // HPB):
                    at = slice(h * HPB * LEN, (h + 1) * HPB * LEN)
                    i = dve.tensor_tensor_scan(gm[s][:, at], pair[0:LEN, h, 0:HPB * LEN], delta[:, :], 0.0,
                                               ALU.mult, ALU.add)
                i.then_inc(scan_done, 1)

            def add_skip(b, s):
                dve.wait_ge(y_mm, b + 1 + RING)
                dve.wait_ge(prep_done, b + 1)
                dve.wait_ge(t4_mm, b + 1)
                dve.tensor_tensor(yb[s][:, :], bank[0][0:LEN, :], xsd[s][:, :], ALU.add).then_inc(ya_done, 1)

            def weigh(b, s):
                dve.wait_ge(scan_done, b + 1 + 1)
                g3 = gm[s][:, :].rearrange("p (h t) -> p h t", h=HEADS)
                dve.tensor_tensor(g3, g3, s_all[:, bass.ds(b * LEN, LEN)].unsqueeze(1).to_broadcast([LEN, HEADS, LEN]),
                                  ALU.mult).then_inc(g_done, 1)

            def add_residual(b, s):
                dve.wait_ge(o_mm, b + 1 + RING)
                dve.tensor_tensor(h_all[:, cols(b)], bank[2][0:LEN, 0:DIM], h_all[:, cols(b)],
                                  ALU.add).then_inc(h1_done, 1)
                dve.wait_ge(h1_done, b + 1 + 1)
                settle(dve)
                dve.bn_stats(est[s][:, :], h_all[:, cols(b)]).then_inc(st_done, 1)
                dve.wait_ge(st_done, b + 1)
                settle(dve)
                dve.bn_aggr(emv[s][:, :], est[s][:, :]).then_inc(ag_done, 1)
                dve.wait_ge(ag_done, b + 1)
                dve.tensor_scalar(eve[s][:, :], emv[s][:, 1:2], EPS, None, ALU.add).then_inc(ve_done, 1)

            def split_low(b, s):
                dve.wait_ge(hi_done, b + 1)
                at = bass.ds(b * LEN, LEN)
                dve.tensor_tensor(tlo[:, :, at], tt[s][:, :, :], thi[:, :, at].bitcast(F32),
                                  ALU.subtract).then_inc(lo_done, 1)

            def add_router_bias(b, s):
                dve.wait_ge(l_mm, b + 1 + RING)
                at = cols(b, EXPERTS)
                dve.tensor_tensor(logit[:, at], bank[4][0:LEN, 0:EXPERTS], rows8[:, 4 * HEADS:5 * HEADS],
                                  ALU.add).then_inc(lg_done, 1)

            def norm_target(b, s):
                dve.wait_ge(pow_done, b + 1)
                dve.wait_ge(t2_mm, b + 1)
                dve.wait_ge(tc_done, b + 1)
                dve.tensor_scalar(tslot[s][:, :], h_all[:, cols(b)], emv[s][:, 0:1], ers[s][:, :],
                                  ALU.subtract, ALU.mult).then_inc(tg_done, 1)

            skewed(dve, [(0, scan), (1, add_skip), (0, weigh), (2, add_residual), (3, split_low), (3, add_router_bias),
                         (2, norm_target)], LAGS)

            dve.wait_ge(lg_done, BATCH + 1)
            for b in range(BATCH):
                at = slice(b * EXPERTS, (b + 1) * EXPERTS)
                dve.max(mx8[:, at], logit[:, at]).then_inc(mxd, 1)
            dve.wait_ge(mxd, BATCH)
            for b in range(BATCH):
                at = slice(b * EXPERTS, (b + 1) * EXPERTS)
                dve.max_index(ix8[:, at], mx8[:, at], logit[:, at]).then_inc(mi_done, 1)
            dve.wait_ge(mi_done, BATCH)
            first, second = mx8[:, 0:8 * BATCH:8], mx8[:, 1:8 * BATCH:8]
            dve.tensor_tensor(t16[0][:, :], second, first, ALU.subtract).then_inc(rt, 1)
            dve.tensor_copy(t16[4][:, :], ix8[:, 0:8 * BATCH:8]).then_inc(rt, 1)
            dve.tensor_copy(t16[5][:, :], ix8[:, 1:8 * BATCH:8]).then_inc(rt, 1)
            dve.wait_ge(rt_exp, 1)
            dve.tensor_scalar(t16[2][:, :], t16[1][:, :], 1.0, None, ALU.add).then_inc(rt, 1)
            dve.wait_ge(rt, 4)
            dve.reciprocal(t16[3][:, :], t16[2][:, :]).then_inc(rt, 1)
            dve.wait_ge(rt, 5)
            dve.tensor_tensor(t16[2][:, :], t16[1][:, :], t16[3][:, :], ALU.mult).then_inc(rt, 1)
            dve.wait_ge(rt, 6)

            def by_batch(t):
                return t[:, :].rearrange("p (b e) -> p b e", e=EXPERTS)

            def per_expert(t):
                return t[:, :].unsqueeze(2).to_broadcast([LEN, BATCH, EXPERTS])

            dve.tensor_tensor(by_batch(t128[0]), by_batch(iota8), per_expert(t16[4]), ALU.is_equal).then_inc(rt, 1)
            dve.tensor_tensor(by_batch(t128[1]), by_batch(iota8), per_expert(t16[5]), ALU.is_equal).then_inc(rt, 1)
            dve.wait_ge(rt, 8)
            dve.tensor_tensor(by_batch(t128[2]), by_batch(t128[0]), per_expert(t16[3]), ALU.mult).then_inc(rt, 1)
            dve.tensor_tensor(by_batch(t128[3]), by_batch(t128[1]), per_expert(t16[2]), ALU.mult).then_inc(rt, 1)
            dve.wait_ge(rt, 10)
            dve.tensor_tensor(t128[4][:, :], t128[2][:, :], t128[3][:, :], ALU.add).then_inc(rt, 1)

            dve.sem_inc(o_ev, OFREE)
            dve.wait_ge(mixed, 1)
            dve.wait_ge(acc_zero, 1)

            def gather(g, par, c):
                n = g * (2 * CHUNKS) + (par * CHUNKS + c)
                at = slice(c * CH, (c + 1) * CH)
                dve.wait_ge(m2_step, n * KF + (KF + HRING))
                for dt in range(KD):
                    i = dve.scalar_tensor_tensor(tmp[:, dt, :], bank[4 + 2 * (c % 2) + dt][:, 0:CH],
                                                 b2_t[:, bass.ds(g * (2 * KD) + (par * KD + dt), 1)],
                                                 rwb[:, par, at], ALU.add, ALU.mult)
                i.then_inc(o_ev, 1)
                dve.wait_ge(o_ev, n + (1 + OFREE))
                dve.tensor_tensor(acc[:, :, at], acc[:, :, at], tmp[:, :, :], ALU.add).then_inc(acc_done, 1)

            with dve.Fori(0, EXPERTS // 2) as g:
                for j, (par, c, f) in enumerate(STEPS):
                    dve.wait_ge(hhi_done, g * len(STEPS) + (j + 1 + HRING))
                    dve.tensor_tensor(hlo[:, j % HRING, :], hid[:, j % HRING, :],
                                      hhi[:, j % HRING, :].bitcast(F32), ALU.subtract).then_inc(hlo_done, 1)
                    if f == LAG and j > KF:
                        gather(g, *STEPS[j - KF][:2])
                    if c == 0 and f == 0:
                        dve.wait_ge(rw_in[par], g * 16 + 16)
                gather(g, 1, CHUNKS - 1)

            dve.sem_inc(u_done, RING)
            dve.wait_ge(acc_done, EXPERTS * CHUNKS)

            def add_sum(b, s):
                dve.wait_ge(f_t, b + 1 + RING)
                dve.tensor_tensor(hn_all[:, cols(b)], bank[s][0:LEN, 0:DIM], hn_all[:, cols(b)],
                                  ALU.add).then_inc(u_done, 1)

            pairs(dve, 0, BATCH, add_sum)
            dve.wait_ge(u_done, BATCH + RING)
            n = mean_var(hn_all, mv, n)
            dve.wait_ge(pw, 3)
            for c in range(CHUNKS):
                at = slice(4 * c * DIM, (4 * c + 4) * DIM)
                for b in range(4 * c, 4 * c + 4):
                    dve.tensor_scalar(hn_all[:, b * DIM:(b + 1) * DIM], hn_all[:, b * DIM:(b + 1) * DIM],
                                      mv[:, 2 * b:2 * b + 1], rstd[:, b:b + 1], ALU.subtract,
                                      ALU.mult).then_inc(fs_done, 1)
                dve.wait_ge(fs_done, 5 * c + 4)
                x4 = hn_all[:, at].rearrange("p (b c) -> p b c", b=4)
                dve.tensor_tensor(x4, x4, fgam[:, :].unsqueeze(1).to_broadcast([LEN, 4, DIM]),
                                  ALU.mult).then_inc(fs_done, 1)

        @block.gpsimd
        def _(pool):
            def power(i, dst, value):
                pool.wait_ge(ln, value)
                pool.tensor_tensor(dst[:, :], ve[:, :], mhalf[:, :], ALU.pow).then_inc(pw, 1)

            one = 2 * BATCH + 1
            power(1, rstd, 2 + one)
            pool.wait_ge(ln, 2 + one + BATCH)
            pool.wait_ge(ld_row, 112)
            pool.tensor_tensor(h_all[:, :], h_all[:, :], hn_all[:, :], ALU.add).then_inc(res_done, 1)
            power(2, rstd2, 2 + one + BATCH + one)
            pool.wait_ge(res_done, 1)
            h3 = h_all[:, :].rearrange("p (b c) -> p b c", b=BATCH)
            pool.tensor_tensor(h3, h3, bout[:, :].unsqueeze(1).to_broadcast([LEN, BATCH, DIM]),
                               ALU.add).then_inc(res_done, 1)

            pool.wait_ge(dec_done, 1)
            pool.wait_ge(s_mm, BATCH + RING)
            pool.wait_ge(sz_done, BATCH + RING)
            pool.wait_ge(xs_ev, BATCH + 1)

            def by_head(t):
                return t.rearrange("p (h c) -> p h c", h=HEADS)

            def prepare(b, s):
                pool.wait_ge(b_mm, b + 1)
                pool.wait_ge(y_mm, b + 1)
                pool.wait_ge(ya_done, b + 1)
                settle(pool)
                pool.tensor_copy(decs[s][:, :], dec_all[:, cols(b, HEADS)])
                x = by_head(xs_all[:, cols(b, INNER)])
                pool.tensor_tensor(by_head(dtx[s][:, :]), x,
                                   dt_all[:, cols(b, HEADS)].unsqueeze(2).to_broadcast([LEN, HEADS, HEAD]), ALU.mult)
                pool.tensor_tensor(by_head(xsd[s][:, :]), x,
                                   rows8[:, 3 * HEADS:4 * HEADS].unsqueeze(2).to_broadcast([LEN, HEADS, HEAD]),
                                   ALU.mult).then_inc(prep_done, 1)

            def gate(b, s):
                pool.wait_ge(ya_done, b + 1 + RING)
                pool.tensor_tensor(yb[s][:, :], yb[s][:, :], sz_all[:, cols(b, INNER)], ALU.mult).then_inc(y2_done, 1)

            def inverse_root(b, s):
                pool.wait_ge(ve_done, b + 1)
                pool.tensor_tensor(ers[s][:, :], eve[s][:, :], mhalf[:, 0:1], ALU.pow).then_inc(pow_done, 1)

            skewed(pool, [(1, gate), (-1, prepare), (2, inverse_root)], LAGS)

            pool.wait_ge(l_mm, BATCH + RING)
            pool.wait_ge(mi_done, BATCH)
            pool.wait_ge(lo_done, BATCH + RING)
            pool.wait_ge(tc_done, BATCH + RING)
            pool.wait_ge(y2_done, BATCH)
            pool.wait_ge(pow_done, BATCH)
            pool.drain().then_inc(mixed, 1)

            pool.memset(acc[:, :, :], 0.0).then_inc(acc_zero, 1)
            pool.sem_inc(wlo_done, RAWS)
            with pool.Fori(0, EXPERTS // 2) as g:
                for par in range(2):
                    pool.wait_ge(o_ev, g * (2 * CHUNKS) + (par * CHUNKS + CHUNKS))
                    for q in range(WPIECES):
                        at = slice(q * WPIECE, (q + 1) * WPIECE)
                        pool.wait_ge(raw_in[q % RAWS], g * (16 * 2 * WPIECES // RAWS)
                                     + 16 * ((par * WPIECES + q) // RAWS + 1))
                        settle(pool)
                        pool.tensor_copy(whi[par][:, at], raw[:, q % RAWS, :]).then_inc(whi_done, 1)
                        pool.wait_ge(whi_done, g * (2 * WPIECES) + (par * WPIECES + q + 1))
                        pool.tensor_tensor(wlo[par][:, at], raw[:, q % RAWS, :], whi[par][:, at].bitcast(F32),
                                           ALU.subtract).then_inc(wlo_done, 1)

            pool.tensor_tensor(h3, h3, fbet[:, :].unsqueeze(1).to_broadcast([LEN, BATCH, DIM]),
                               ALU.add).then_inc(hb_done, 1)
            power(3, rstd, 2 + one + BATCH + one + one)
            pool.wait_ge(hb_done, 1)
            for c in range(CHUNKS):
                at = slice(4 * c * DIM, (4 * c + 4) * DIM)
                pool.wait_ge(fs_done, 5 * c + 5)
                pool.tensor_tensor(h_all[:, at], h_all[:, at], hn_all[:, at], ALU.add).then_inc(fin, 1)


def kernel(x, txt, L0_tok_W, L0_tok_b, L0_tok_pos_embd, L0_attn_ln_gamma, L0_attn_ln_beta, L0_attn_W_in,
           L0_attn_b_in, L0_attn_A_log, L0_attn_D_skip, L0_attn_dt_bias, L0_attn_W_out, L0_attn_b_out, L0_ffn_Wr,
           L0_ffn_br, L0_ffn_W1, L0_ffn_b1, L0_ffn_W2, L0_ffn_b2, L0_ffn_gamma, L0_ffn_beta):
    import concourse.bacc as bacc
    from concourse.bass_utils import run_bass_kernel_spmd

    def tiles(w, k):
        return np.asarray(w).reshape(k, P, -1).transpose(1, 0, 2)

    side = 16
    per = 96 // side
    patches = np.asarray(x).reshape(BATCH, 3, per, side, per, side).transpose(1, 3, 5, 0, 2, 4)
    w1 = np.asarray(L0_ffn_W1).transpose(0, 2, 1).reshape(EXPERTS, KD, P, HIDDEN).transpose(0, 2, 1, 3)
    w2 = np.asarray(L0_ffn_W2).transpose(0, 2, 1).reshape(EXPERTS, KF, P, DIM).transpose(0, 2, 1, 3)
    b_in = np.asarray(L0_attn_b_in)
    eye = np.eye(P, dtype=np.float32)
    arrays = {
        "patch": tiles(patches.reshape(PATCH, BATCH * IMG), KP),
        "w_tok": tiles(np.asarray(L0_tok_W).T, KP),
        "txt": txt,
        "pos": np.asarray(L0_tok_pos_embd)[0],
        "tok_b": L0_tok_b,
        "w_in": tiles(L0_attn_W_in, KD),
        "w_out": tiles(L0_attn_W_out, KI),
        "wr": tiles(np.asarray(L0_ffn_Wr).T, KD),
        "b_bc": b_in[C_BC:C_DT].reshape(P, 1),
        "b_x": b_in[C_X:C_BC],
        "b_z": b_in[C_Z:C_X],
        "b_out": L0_attn_b_out,
        "gam_t": np.asarray(L0_attn_ln_gamma).reshape(KD, P).T,
        "bet_t": np.asarray(L0_attn_ln_beta).reshape(KD, P).T,
        "rows8": np.concatenate([b_in[C_DT:], np.asarray(L0_attn_dt_bias), np.asarray(L0_attn_A_log),
                                 np.asarray(L0_attn_D_skip), np.asarray(L0_ffn_br)]),
        "experts": np.concatenate([w1.reshape(EXPERTS, P, -1), w2.reshape(EXPERTS, P, -1)], axis=2),
        "b1_t": np.asarray(L0_ffn_b1).reshape(EXPERTS * KF, P).T,
        "b2_t": np.asarray(L0_ffn_b2).reshape(EXPERTS * KD, P).T,
        "f_gam": L0_ffn_gamma,
        "f_bet": L0_ffn_beta,
        "ident": eye,
        "delta": np.tile(eye[:LEN, :LEN], (1, HPB)),
        "iota8": np.tile(np.arange(EXPERTS, dtype=np.float32), (LEN, BATCH)),
        "rowmask": np.where(np.arange(LEN) == 0, -1e30, 0.0).astype(np.float32).reshape(LEN, 1),
    }
    arrays = {f"in_{k}": np.ascontiguousarray(v) for k, v in arrays.items()}
    nc = bacc.Bacc("TRN2", target_bir_lowering=False, num_devices=1)
    d = {k[3:]: nc.dram_tensor(k, v.shape, F32, kind="ExternalInput").ap() for k, v in arrays.items()}
    out = nc.dram_tensor("out", (BATCH, LEN, DIM), F32, kind="ExternalOutput").ap()
    build(nc, d, out)
    r = run_bass_kernel_spmd(nc, [arrays], core_ids=[0])
    return r.results[0]["out"]
```

```python
from contextlib import ExitStack

import numpy as np
import concourse.bass as bass
from concourse import mybir

F32 = mybir.dt.float32
BF16 = mybir.dt.bfloat16
U32 = mybir.dt.uint32
ALU = mybir.AluOpType
ACT = mybir.ActivationFunctionType
AXIS_X = mybir.AxisListType.X

BATCH, IMG, TXT, DIM = 16, 36, 77, 256
LEN = IMG + TXT
TOK = BATCH * LEN
PATCH = 768
INNER, STATE, HEADS, HEAD = 512, 64, 8, 64
PROJ = 2 * INNER + 2 * STATE + HEADS
EXPERTS, HIDDEN = 8, 1024
EPS = 1e-5
P = 128
KP = PATCH // P
KD = DIM // P
KI = INNER // P
KF = HIDDEN // P
TOP = 2
TILES = (TOP * TOK + EXPERTS * (P - 1)) // P
MOST = -(-TOK // P) - 1
WSIZE = KD * HIDDEN + KF * DIM
BIAS_ROWS = EXPERTS * (HIDDEN + DIM) // P
W_FIRST = 2
HALVES = 2
HH = HIDDEN // HALVES
KH = HH // P
CHUNKS = 8
PER = BATCH // CHUNKS
HALF = BATCH * IMG // 2
HPB = 4
RING = 2
RT_PICKED = 6
DM = 17
C_Z, C_X, C_BC, C_DT = 0, INNER, 2 * INNER, 2 * INNER + 2 * STATE


def build(nc, d, out):
    with ExitStack() as ctx:
        def sem(name):
            return ctx.enter_context(nc.semaphore(name))

        top = [16512]

        def place(name, shape, dt=F32, at=None):
            size = 4
            for n in shape[1:]:
                size *= n
            size = -(-size // 32) * 32
            where = top[0] if at is None else at[0]
            t = nc.alloc_sbuf_tensor_at(name, list(shape), dt, offset=where)
            if at is None:
                top[0] += size
            else:
                at[0] += size
            return t

        ident = place("ident", [P, P])
        iota8 = place("iota8", [LEN, BATCH * EXPERTS])
        zeros = place("zeros", [P, DIM])
        rowmask = place("rowmask", [LEN, 1])
        fgam = place("fgam", [LEN, DIM])
        fbet = place("fbet", [LEN, DIM])
        b_bc = place("b_bc", [P, 1])
        gam_t = place("gam_t", [P, KD])
        bet_t = place("bet_t", [P, KD])
        rows8 = place("rows8", [LEN, 5 * HEADS])
        bdt = place("bdt", [LEN, HEADS])
        exp_a = place("exp_a", [LEN, HEADS])
        wr = place("wr", [P, KD, EXPERTS])
        mhalf = place("mhalf", [LEN, BATCH])
        stats = place("stats", [LEN, BATCH * 6])
        mv = place("mv", [LEN, BATCH * 2])
        ve = place("ve", [LEN, BATCH])
        rstd = place("rstd", [LEN, BATCH])
        dt_all = place("dt_all", [LEN, BATCH * HEADS])
        dec_all = place("dec_all", [LEN, BATCH * HEADS])
        logit = place("logit", [LEN, BATCH * EXPERTS])
        mx8 = place("mx8", [LEN, BATCH * 8])
        ix8 = place("ix8", [LEN, BATCH * 8], U32)
        t128 = [place(f"t128_{i}", [LEN, BATCH * HEADS]) for i in range(6)]
        t16 = [place(f"t16_{i}", [LEN, BATCH]) for i in range(6)]
        small = place("small", [LEN, MOST + TILES])
        before = place("before", [LEN, 2 * LEN])
        grid = place("grid", [LEN, TILES * EXPERTS])
        r8 = [place(f"r8_{i}", [LEN, EXPERTS]) for i in range(7)]
        tile_row = place("tile_row", [LEN, TILES])
        tile_slot = place("tile_slot", [LEN, TILES], U32)
        placef = [place(f"placef{i}", [LEN, BATCH]) for i in range(TOP)]
        place_of = [place(f"place_of{i}", [LEN, BATCH], U32) for i in range(TOP)]
        bias3 = place("bias3", [3, EXPERTS, HIDDEN + DIM], BF16)
        ones3 = place("ones3", [3, P], BF16)
        dead = top[0]
        hn_all = place("hn_all", [LEN, BATCH * DIM])
        h_all = place("h_all", [LEN, BATCH * DIM])
        delta = place("delta", [LEN, HPB * LEN])
        bx = place("bx", [LEN, INNER])
        bz = place("bz", [LEN, INNER])
        posb = place("posb", [IMG, DIM])
        tokb = place("tokb", [IMG, DIM])
        bout = place("bout", [LEN, DIM])
        phase = top[0]

        a = [phase]
        xs_all = place("xs_all", [LEN, BATCH * INNER], at=a)
        sz_all = place("sz_all", [LEN, BATCH * INNER], at=a)
        s_all = place("s_all", [LEN, BATCH * LEN], at=a)
        w_out = place("w_out", [P, KI, DIM], at=a)
        work = a[0]
        a = [work]
        w_in = place("w_in", [P, KD, PROJ], at=a)
        nslot = [place(f"nslot{i}", [LEN, DIM], at=a) for i in range(RING)]
        nt = [place(f"nt{i}", [P, KD, LEN], at=a) for i in range(RING)]
        bct = [place(f"bct{i}", [P, LEN], at=a) for i in range(RING)]
        ct = [place(f"ct{i}", [STATE, LEN], at=a) for i in range(RING)]
        nst, nmv, nve, nrs = ([[place(f"{name}{j}_{i}", [LEN, n], at=a) for i in range(RING)] for j in range(2)]
                              for name, n in (("nst", 6), ("nmv", 2), ("nve", 1), ("nrs", 1)))
        work_top = a[0]
        b = [phase]
        bsrc = place("bsrc", [BIAS_ROWS, P], at=b)
        bres = [place(f"bres{i}", [BIAS_ROWS, P], at=b) for i in range(2)]
        bpart = [place(f"bpart{i}", [BIAS_ROWS, P], BF16, at=b) for i in range(3)]
        patch = place("patch", [P, KP, BATCH * IMG], at=b)
        w_tok = place("w_tok", [P, KP, DIM], at=b)
        emb_t = place("emb_t", [P, KD, BATCH * IMG], at=b)
        a = [work]
        decs = [place(f"decs{i}", [LEN, HEADS], at=a) for i in range(RING)]
        dtx = [place(f"dtx{i}", [LEN, INNER], at=a) for i in range(RING)]
        xsd = [place(f"xsd{i}", [LEN, INNER], at=a) for i in range(RING)]
        gm = [place(f"gm{i}", [LEN, HEADS * LEN], at=a) for i in range(RING)]
        yb = [place(f"yb{i}", [LEN, INNER], at=a) for i in range(RING)]
        yt = [place(f"yt{i}", [P, KI, LEN], at=a) for i in range(RING)]
        tslot = [place(f"tslot{i}", [LEN, DIM], at=a) for i in range(RING)]
        tt = [place(f"tt{i}", [P, KD, LEN], at=a) for i in range(RING)]
        est = [place(f"est{i}", [LEN, 6], at=a) for i in range(RING)]
        emv = [place(f"emv{i}", [LEN, 2], at=a) for i in range(RING)]
        eve = [place(f"eve{i}", [LEN, 1], at=a) for i in range(RING)]
        ers = [place(f"ers{i}", [LEN, 1], at=a) for i in range(RING)]
        assert max(a[0], b[0], work_top) <= nc.sbuf_top

        a = [dead]
        xrow = [place(f"xrow{i}", [P, DIM], at=a) for i in range(RING)]
        xcol = [place(f"xcol{i}", [P, KD, P], at=a) for i in range(RING)]
        hrow = [place(f"hrow{i}", [P, HIDDEN], at=a) for i in range(RING)]
        hcol = [place(f"hcol{i}", [P, KF, P], at=a) for i in range(RING)]
        yrow = [place(f"yrow{i}", [P, DIM], at=a) for i in range(RING)]
        w_at = nc.sbuf_top - EXPERTS * WSIZE * 4
        assert a[0] <= w_at, (a[0], w_at)
        w_all = place("w_all", [P, EXPERTS, WSIZE], at=[w_at])
        h_end = place("h_end", [LEN, BATCH * DIM], at=[w_at + (EXPERTS - 1) * WSIZE * 4])
        u_end = place("u_end", [LEN, BATCH * DIM], at=[w_at + (EXPERTS - 2) * WSIZE * 4])
        a = [w_at]
        back = [place(f"back{i}", [LEN, BATCH * DIM], at=a) for i in range(TOP)]

        bank = [ctx.enter_context(nc.psum_tensor(f"bank{i}", [P, 512], F32)) for i in range(6)]
        pair = ctx.enter_context(nc.psum_tensor("pair", [P, 2, 512], F32))
        bank += [pair[:, 0, :], pair[:, 1, :]]
        xg = nc.dram_tensor("xg", [TILES * P, DIM], F32).ap()
        yg = nc.dram_tensor("yg", [TILES * P, DIM], F32).ap()
        h_dram = nc.dram_tensor("h_dram", [LEN, BATCH * DIM], F32).ap()
        u_dram = nc.dram_tensor("u_dram", [LEN, BATCH * DIM], F32).ap()
        bparts = nc.dram_tensor("bparts", [3, EXPERTS * (HIDDEN + DIM)], BF16).ap()

        settled = sem("settled")
        ld_tok = [sem(f"ld_tok{k}") for k in range(KP)]
        ld_ident, ld_h, ld_proj, ld_ssm, ld_row = (
            sem(n) for n in ("ld_ident", "ld_h", "ld_proj", "ld_ssm", "ld_row"))
        emb_mm, emb_sb, img_t, img_rows = (sem(n) for n in ("emb_mm", "emb_sb", "img_t", "img_rows"))
        ln, n1_done, res_sum, res_done, bdt_done, expa_done = (
            sem(n) for n in ("ln", "n1_done", "res_sum", "res_done", "bdt_done", "expa_done"))
        nst_done, nag_done, nve_done, npow_done = ([sem(f"{name}{j}") for j in range(2)] for name in
                                                   ("nst_done", "nag_done", "nve_done", "npow_done"))
        ns_done, t_done, nt_done, bc_mm, dt_mm, xs_mm, z_mm, s_mm = (
            sem(n) for n in ("ns_done", "t_done", "nt_done", "bc_mm", "dt_mm", "xs_mm", "z_mm", "s_mm"))
        bc_ev, c_ev, dt_ev, xs_ev, z_ev, sz_done, s_ev = (
            sem(n) for n in ("bc_ev", "c_ev", "dt_ev", "xs_ev", "z_ev", "sz_done", "s_ev"))
        dm, em, dec_done, mixed = (sem(n) for n in ("dm", "em", "dec_done", "mixed"))
        decs_done, prep_done, b_mm, scan_done, g_done, y_mm, ya_done, y2_done, t4_mm, yt_done, o_mm, h1_done = (
            sem(n) for n in ("decs_done", "prep_done", "b_mm", "scan_done", "g_done", "y_mm", "ya_done", "y2_done", "t4_mm",
                             "yt_done", "o_mm", "h1_done"))
        st_done, ag_done, ve_done, pow_done, tg_done, t2_mm, tc_done, tt_done, l_mm, lg_done, mxd, mi_done = (
            sem(n) for n in ("st_done", "ag_done", "ve_done", "pow_done", "tg_done", "t2_mm", "tc_done", "tt_done",
                             "l_mm", "lg_done", "mxd", "mi_done"))
        rt, rt_exp, rt_cnt, table_done, places_done, zero_set, zero_out, placed = (
            sem(n) for n in ("rt", "rt_exp", "rt_cnt", "table_done", "places_done", "zero_set", "zero_out", "placed"))
        ld_bias, bias_step, bias_out, bias_in = (sem(n) for n in ("ld_bias", "bias_step", "bias_out", "bias_in"))
        w_ld = [sem(f"w_ld{e}") for e in range(EXPERTS)]
        x_in, xc_mm, xc_ev, h_mm, h_ev, hc_mm, hc_ev, yr_mm, yr_ev, y_out = (
            sem(n) for n in ("x_in", "xc_mm", "xc_ev", "h_mm", "h_ev", "hc_mm", "hc_ev", "yr_mm", "yr_ev", "y_out"))
        back_in = [sem(f"back_in{c}") for c in range(CHUNKS)]
        kept, ends_in, hb_done, tail, tail_ve, tail_pow, tail_shift, tail_norm, fin, out_done = (
            sem(n) for n in ("kept", "ends_in", "hb_done", "tail", "tail_ve", "tail_pow", "tail_shift", "tail_norm", "fin", "out_done"))

        block = ctx.enter_context(nc.Block())

        def settle(eng):
            eng.sem_inc(settled, 1)

        def cols(b, n=DIM):
            return bass.ds(b * n, n)

        def pairs(eng, first, last, body):
            n = (last - first) // 2
            with eng.Fori(0, n) as p:
                for s in range(2):
                    body(p * 2 + (first + s), (first + s) % 2)
            for b in range(first + 2 * n, last):
                body(b, b % 2)

        def skewed(eng, stages, count=BATCH, peel=0):
            lo, hi = min(lag for lag, _ in stages), max(lag for lag, _ in stages)
            first, last = max(hi, peel), count + lo
            if (last - first) % 2:
                last -= 1

            def turn(n, parity):
                for lag, f in stages:
                    if not isinstance(n, int) or 0 <= n - lag < count:
                        f(n - lag, (parity - lag) % 2)

            for n in range(lo, first):
                turn(n, n % 2)
            with eng.Fori(0, (last - first) // 2) as p:
                for s in range(2):
                    turn(p * 2 + (first + s), (first + s) % 2)
            for n in range(last, count + hi):
                turn(n, n % 2)

        @block.sync
        def _(sp):
            for k in range(KP):
                sp.dma_start(w_tok[:, k, :], d["w_tok"][:, k, :]).then_inc(ld_tok[k], 16)
                sp.dma_start(patch[:, k, :], d["patch"][:, k, :]).then_inc(ld_tok[k], 16)
            sp.dma_start(ident[:, :], d["ident"]).then_inc(ld_ident, 16)
            sp.dma_start(h_all[IMG:LEN, :].rearrange("p (b c) -> p b c", b=BATCH),
                         d["txt"].rearrange("b t c -> t b c")).then_inc(ld_h, 16)
            sp.dma_start(w_in[:, :, :], d["w_in"]).then_inc(ld_proj, 16)
            sp.dma_start(b_bc[:, :], d["b_bc"]).then_inc(ld_proj, 16)
            sp.dma_start(gam_t[:, :], d["gam_t"]).then_inc(ld_proj, 16)
            sp.dma_start(bet_t[:, :], d["bet_t"]).then_inc(ld_proj, 16)
            sp.dma_start(delta[:, :], d["delta"]).then_inc(ld_ssm, 16)
            sp.dma_start(w_out[:, :, :], d["w_out"]).then_inc(ld_ssm, 16)
            sp.dma_start(wr[:, :, :], d["wr"]).then_inc(ld_ssm, 16)
            sp.dma_start(iota8[:, :], d["iota8"]).then_inc(ld_ssm, 16)
            sp.dma_start(small[:, :], d["small"].partition_broadcast(LEN)).then_inc(ld_ssm, 16)
            sp.dma_start(before[:, :], d["before"]).then_inc(ld_ssm, 16)
            for i in range(3):
                sp.wait_ge(bias_step, 2 * i + 1)
                sp.dma_start(bparts[i:i + 1, :].rearrange("o (r c) -> (o r) c", c=P), bpart[i][:, :]
                             ).then_inc(bias_out, 16)
            sp.wait_ge(bias_out, 48)
            sp.dma_start(bias3[:, :, :], bparts.rearrange("i (e n) -> i e n", e=EXPERTS)).then_inc(bias_in, 16)
            sp.wait_ge(zero_set, 1)
            sp.dma_start(xg.rearrange("(a p) n -> p a n", p=P),
                         zeros[:, :].unsqueeze(1).to_broadcast([P, TILES, DIM])).then_inc(zero_out, 16)

            def keep(b, s):
                sp.wait_ge(tc_done, b + (1 + RING))
                settle(sp)
                sp.dma_start(u_dram[:, cols(b)], hn_all[:, cols(b)]).then_inc(kept, 16)
                sp.dma_start(h_dram[:, cols(b)], h_all[:, cols(b)]).then_inc(kept, 16)

            pairs(sp, 0, BATCH, keep)

            sp.sem_inc(x_in, 16)
            sp.sem_inc(y_out, 16 * RING)
            sp.wait_ge(placed, 16 * TOP * BATCH)
            sp.wait_ge(kept, 32 * BATCH)

            def load_rows(i, s):
                sp.wait_ge(xc_mm, i + 1)
                sp.wait_ge(x_in, i * 16 + 16)
                settle(sp)
                sp.dma_start(xrow[s][:, :], xg[bass.ds(i * P, P), :]).then_inc(x_in, 16)

            def store_rows(i, s):
                sp.wait_ge(yr_ev, i + 2)
                sp.wait_ge(y_out, i * 16 + 16 * RING)
                settle(sp)
                sp.dma_start(yg[bass.ds(i * P, P), :], yrow[s][:, :]).then_inc(y_out, 16)

            skewed(sp, [(-2, load_rows), (1, store_rows)], TILES)

            dst = out.rearrange("b t c -> t b c")
            for c in range(CHUNKS):
                sp.wait_ge(fin, (c + 1))
                sp.dma_start(dst[:, PER * c:PER * (c + 1), :],
                             h_end[:, c * PER * DIM:(c + 1) * PER * DIM].rearrange("p (b c) -> p b c", b=PER)
                             ).then_inc(out_done, 16)
            sp.wait_ge(out_done, 16 * CHUNKS)

        @block.tensor
        def _(pe):
            for k in range(KP):
                pe.wait_ge(ld_tok[k], 32)
                for q in range(2 * KD):
                    e, half = q // 2, q % 2
                    mm = pe.matmul(bank[q][:, 0:HALF], w_tok[:, k, e * P:(e + 1) * P],
                                   patch[:, k, half * HALF:(half + 1) * HALF], start=(k == 0), stop=(k == KP - 1))
                    if k == KP - 1:
                        mm.then_inc(emb_mm, 1)
            pe.wait_ge(ld_ident, 16)
            pe.wait_ge(emb_sb, 2 * KD)
            for g in range(BATCH // 2):
                if g >= 4:
                    pe.wait_ge(img_rows, g - 3)
                for j in range(2 * KD):
                    bb, e = j // KD, j % KD
                    mm = pe.transpose(bank[4 + g % 4][0:IMG, j * P:(j + 1) * P],
                                      emb_t[:, e, (2 * g + bb) * IMG:(2 * g + bb + 1) * IMG], ident[:, :])
                mm.then_inc(img_t, 1)

            for s in (t_done, s_mm):
                pe.sem_inc(s, RING)
            pe.wait_ge(img_rows, BATCH // 2)
            pe.wait_ge(ld_proj, 64)

            def turn_rows(b, s):
                pe.wait_ge(ns_done, b + 1)
                pe.wait_ge(nt_done, b + 1)
                for k in range(KD):
                    mm = pe.transpose(bank[s][:, k * P:k * P + LEN], nslot[s][:, k * P:(k + 1) * P],
                                      ident[0:LEN, 0:LEN])
                mm.then_inc(t_done, 1)

            def project_narrow(b, s):
                pe.wait_ge(nt_done, b + 1 + RING)
                pe.wait_ge(bc_ev, b + 1)
                for k in range(KD):
                    mm = pe.matmul(bank[2][:, 0:LEN], w_in[:, k, C_BC:C_DT], nt[s][:, k, :],
                                   start=(k == 0), stop=(k == KD - 1))
                mm.then_inc(bc_mm, 1)
                pe.wait_ge(s_ev, b + 1)
                for k in range(KD):
                    mm = pe.matmul(bank[3][0:LEN, 256:256 + HEADS], nt[s][:, k, :], w_in[:, k, C_DT:PROJ],
                                   start=(k == 0), stop=(k == KD - 1))
                mm.then_inc(dt_mm, 1)
                pe.wait_ge(xs_ev, b + 1)
                for k in range(KD):
                    mm = pe.matmul(bank[4][0:LEN, :], nt[s][:, k, :], w_in[:, k, C_X:C_BC],
                                   start=(k == 0), stop=(k == KD - 1))
                mm.then_inc(xs_mm, 1)

            def project_z(b, s):
                pe.wait_ge(z_ev, b + 1)
                for k in range(KD):
                    mm = pe.matmul(bank[5][0:LEN, :], nt[s][:, k, :], w_in[:, k, C_Z:C_X],
                                   start=(k == 0), stop=(k == KD - 1))
                mm.then_inc(z_mm, 1)
                pe.wait_ge(c_ev, b + 1)
                pe.wait_ge(dt_ev, b + 1)
                pe.matmul(bank[3][0:LEN, 0:LEN], bct[s][0:STATE, :], ct[s][:, :],
                          start=True, stop=True).then_inc(s_mm, 1)

            skewed(pe, [(0, project_narrow), (-1, turn_rows), (0, project_z)])

            pe.wait_ge(ld_ssm, 96)
            for s in (b_mm, y_mm, t4_mm, t2_mm, o_mm, l_mm):
                pe.sem_inc(s, RING)
            pe.wait_ge(s_ev, BATCH + 1)
            pe.wait_ge(dt_ev, BATCH)
            pe.wait_ge(xs_ev, BATCH + 1)
            pe.wait_ge(z_ev, BATCH + 1)
            pe.wait_ge(bc_ev, BATCH + 1)

            def spread_decays(b, s):
                pe.wait_ge(decs_done, b + 1)
                pe.wait_ge(scan_done, b + 1)
                for h in range(HEADS):
                    mm = pe.transpose(pair[0:LEN, h // HPB, h % HPB * LEN:(h % HPB + 1) * LEN],
                                      decs[s][:, h:h + 1].to_broadcast([LEN, LEN]), ident[0:LEN, 0:LEN])
                mm.then_inc(b_mm, 1)

            def turn_target(b, s):
                pe.wait_ge(tg_done, b + 1)
                pe.wait_ge(tt_done, b + 1)
                for k in range(KD):
                    mm = pe.transpose(bank[3][:, k * P:k * P + LEN], tslot[s][:, k * P:(k + 1) * P],
                                      ident[0:LEN, 0:LEN])
                mm.then_inc(t2_mm, 1)

            def mix(b, s):
                pe.wait_ge(g_done, b + 1)
                pe.wait_ge(prep_done, b + 1)
                pe.wait_ge(ya_done, b + 2)
                for h in range(HEADS):
                    mm = pe.matmul(bank[0][0:LEN, h * HEAD:(h + 1) * HEAD], gm[s][:, h * LEN:(h + 1) * LEN],
                                   dtx[s][:, h * HEAD:(h + 1) * HEAD], start=True, stop=True)
                mm.then_inc(y_mm, 1)

            def project_out(b, s):
                pe.wait_ge(yt_done, b + 1 + 1)
                pe.wait_ge(h1_done, b + 1)
                for k in range(KI):
                    mm = pe.matmul(bank[2][0:LEN, 0:DIM], yt[s][:, k, :], w_out[:, k, :],
                                   start=(k == 0), stop=(k == KI - 1))
                mm.then_inc(o_mm, 1)

            def logits(b, s):
                pe.wait_ge(tt_done, b + 1 + 1)
                pe.wait_ge(lg_done, b + 1)
                for k in range(KD):
                    mm = pe.matmul(bank[4][0:LEN, 0:EXPERTS], tt[s][:, k, :], wr[:, k, :],
                                   start=(k == 0), stop=(k == KD - 1))
                mm.then_inc(l_mm, 1)

            def turn_gated(b, s):
                pe.wait_ge(y2_done, b + 1)
                pe.wait_ge(yt_done, b + 1)
                for k in range(KI):
                    mm = pe.transpose(bank[1][:, k * P:k * P + LEN], yb[s][:, k * P:(k + 1) * P],
                                      ident[0:LEN, 0:LEN])
                mm.then_inc(t4_mm, 1)

            skewed(pe, [(0, spread_decays), (2, turn_gated), (1, mix), (4, turn_target), (2, project_out),
                        (4, logits)])

            pe.wait_ge(rt, RT_PICKED)
            for i in range(2):
                mm = pe.matmul(bank[5][0:LEN, i * P:(i + 1) * P], before[:, i * LEN:(i + 1) * LEN], t128[2][:, :],
                               start=True, stop=True)
            mm.then_inc(rt_cnt, 1)

            for s, n in ((xc_mm, RING), (h_mm, HALVES * RING), (hc_mm, HALVES * RING), (yr_mm, RING)):
                pe.sem_inc(s, n)
            pe.wait_ge(table_done, 1)
            pe.wait_ge(bias_in, 16)
            pe.wait_ge(mixed, 1)
            pe.wait_ge(places_done, 1)

            def turn_x(i, s):
                pe.wait_ge(x_in, i * 16 + 32)
                pe.wait_ge(xc_ev, i + 1)
                for k in range(KD):
                    mm = pe.transpose(bank[0][:, k * P:(k + 1) * P], xrow[s][:, k * P:(k + 1) * P], ident[:, :])
                mm.then_inc(xc_mm, 1)

            expert_of = [None, None]

            def look_up(product):
                def stage(i, s):
                    expert_of[product] = pe.value_load(tile_slot[0:1, bass.ds(i, 1)], min_val=0, max_val=EXPERTS - 1)
                return stage

            def first_product(half):
                def stage(i, s):
                    if half == 0:
                        pe.wait_ge(xc_ev, i + 2)
                        if isinstance(i, int) and i < EXPERTS:
                            pe.wait_ge(w_ld[i], 16)
                    pe.wait_ge(h_ev, i * HALVES + (half + 1))
                    e = expert_of[0]
                    dst = bank[1 + half][:, :]
                    pe.matmul(dst, ones3[:, :], bias3[:, bass.ds(e, 1), half * HH:(half + 1) * HH],
                              start=True, stop=False)
                    for k in range(KD):
                        at = k * HIDDEN + half * HH
                        mm = pe.matmul(dst, xcol[s][:, k, :], w_all[:, bass.ds(e, 1), at:at + HH],
                                       start=False, stop=(k == KD - 1))
                    mm.then_inc(h_mm, 1)
                return stage

            def turn_hidden(half):
                def stage(i, s):
                    pe.wait_ge(h_ev, i * HALVES + (half + 1 + HALVES))
                    pe.wait_ge(hc_ev, i * HALVES + (half + 1))
                    for k in range(KH):
                        at = (half * KH + k) * P
                        mm = pe.transpose(bank[3 + half][:, k * P:(k + 1) * P], hrow[s][:, at:at + P], ident[:, :])
                    mm.then_inc(hc_mm, 1)
                return stage

            def second_product(i, s):
                pe.wait_ge(hc_ev, i * HALVES + 2 * HALVES)
                pe.wait_ge(yr_ev, i + 1)
                e = expert_of[1]
                dst = bank[5][:, 0:DIM]
                pe.matmul(dst, ones3[:, :], bias3[:, bass.ds(e, 1), HIDDEN:HIDDEN + DIM], start=True, stop=False)
                for k in range(KF):
                    at = KD * HIDDEN + k * DIM
                    mm = pe.matmul(dst, hcol[s][:, k, :], w_all[:, bass.ds(e, 1), at:at + DIM],
                                   start=False, stop=(k == KF - 1))
                mm.then_inc(yr_mm, 1)

            skewed(pe, [(0, look_up(0)), (1, look_up(1)), (1, turn_hidden(0)), (0, first_product(0)),
                        (1, turn_hidden(1)), (-1, turn_x), (0, first_product(1)), (1, second_product)],
                   TILES, peel=EXPERTS)

        @block.scalar
        def _(act):
            act.dma_start(posb[:, :], d["pos"]).then_inc(ld_h, 16)
            act.dma_start(tokb[:, :], d["tok_b"].partition_broadcast(IMG)).then_inc(ld_h, 16)
            act.dma_start(bout[:, :], d["b_out"].partition_broadcast(LEN)).then_inc(ld_row, 16)
            act.dma_start(rows8[:, :], d["rows8"].partition_broadcast(LEN)).then_inc(ld_row, 16)
            act.dma_start(bx[:, :], d["b_x"].partition_broadcast(LEN)).then_inc(ld_row, 16)
            act.dma_start(bz[:, :], d["b_z"].partition_broadcast(LEN)).then_inc(ld_row, 16)
            act.dma_start(rowmask[:, :], d["rowmask"]).then_inc(ld_row, 16)
            act.dma_start(fgam[:, :], d["f_gam"].partition_broadcast(LEN)).then_inc(ld_row, 16)
            act.dma_start(fbet[:, :], d["f_bet"].partition_broadcast(LEN)).then_inc(ld_row, 16)
            act.dma_start(bsrc[:, :], d["biases"]).then_inc(ld_bias, 16)
            for q in range(2 * KD):
                e, half = q // 2, q % 2
                act.wait_ge(emb_mm, q + 1)
                act.activation(emb_t[:, e, half * HALF:(half + 1) * HALF], bank[q][:, 0:HALF],
                               ACT.Copy).then_inc(emb_sb, 1)
            act.wait_ge(ld_row, 112)
            act.activation(exp_a[:, :], rows8[:, 2 * HEADS:3 * HEADS], ACT.Exp).then_inc(expa_done, 1)

            act.sem_inc(nt_done, RING)
            for s in (bc_ev, s_ev):
                act.sem_inc(s, 1)
            act.wait_ge(ld_proj, 64)

            def norm_t(b, s):
                act.wait_ge(t_done, b + 1 + RING)
                act.wait_ge(s_mm, b + 1)
                for k in range(KD):
                    i = act.activation(nt[s][:, k, :], bank[s][:, k * P:k * P + LEN], ACT.Identity,
                                       bias=bet_t[:, k:k + 1], scale=gam_t[:, k:k + 1])
                i.then_inc(nt_done, 1)

            def keep_bc(b, s):
                act.wait_ge(bc_mm, b + 1)
                act.wait_ge(s_mm, b + 1)
                act.activation(bct[s][:, :], bank[2][:, 0:LEN], ACT.Identity, bias=b_bc[:, 0:1]).then_inc(bc_ev, 1)
                act.wait_ge(bc_ev, b + 1 + 1)
                act.activation(ct[s][:, :], bct[s][STATE:P, :], ACT.Copy).then_inc(c_ev, 1)

            def keep_scores(b, s):
                act.wait_ge(s_mm, b + 1 + RING)
                settle(act)
                act.activation(s_all[:, bass.ds(b * LEN, LEN)], bank[3][0:LEN, 0:LEN], ACT.Copy).then_inc(s_ev, 1)

            def gate_values(b, s):
                if s == 0:
                    act.wait_ge(z_ev, b + 1 + 2)
                    settle(act)
                    z = sz_all[:, bass.ds(b * INNER, 2 * INNER)]
                    act.activation(z, z, ACT.Silu).then_inc(sz_done, 1)

            skewed(act, [(0, keep_bc), (-1, norm_t), (2, gate_values), (0, keep_scores)])

            act.wait_ge(dm, 1)
            act.activation(t128[2][:, :], t128[0][:, :], ACT.Exp).then_inc(em, 1)
            act.wait_ge(dm, DM)
            act.activation(dec_all[:, :], t128[3][:, :], ACT.Exp, bias=rowmask[:, 0:1], scale=-1.0).then_inc(dec_done, 1)

            for s in (tt_done, yt_done):
                act.sem_inc(s, 1)
            act.sem_inc(tc_done, RING)

            def keep_target(b, s):
                act.wait_ge(tg_done, b + 1)
                settle(act)
                act.activation(hn_all[:, cols(b)], tslot[s][:, :], ACT.Copy).then_inc(tc_done, 1)
                act.wait_ge(t2_mm, b + 1 + RING)
                act.wait_ge(l_mm, b + 1)
                act.activation(tt[s][:, :, :], bank[3][:, 0:KD * P].rearrange("p (k c) -> p k c", k=KD)[:, :, 0:LEN],
                               ACT.Copy).then_inc(tt_done, 1)

            def gated_t(b, s):
                act.wait_ge(t4_mm, b + 1 + RING)
                act.wait_ge(o_mm, b + 1)
                act.activation(yt[s][:, :, :], bank[1][:, :].rearrange("p (k c) -> p k c", k=KI)[:, :, 0:LEN],
                               ACT.Copy).then_inc(yt_done, 1)

            def slot_decays(b, s):
                act.wait_ge(b_mm, b + 1)
                settle(act)
                act.activation(decs[s][:, :], dec_all[:, cols(b, HEADS)], ACT.Copy).then_inc(decs_done, 1)

            act.wait_ge(dec_done, 1)
            act.wait_ge(s_mm, BATCH + RING)
            skewed(act, [(2, gated_t), (-1, slot_decays), (4, keep_target)])

            act.wait_ge(rt, 1)
            act.activation(t16[1][:, :], t16[0][:, :], ACT.Exp).then_inc(rt_exp, 1)

            def load_expert(e):
                act.dma_start(w_all[:, EXPERTS - 1 - e, :], d["experts"][e]).then_inc(w_ld[e], 16)

            act.wait_ge(mixed, 1)
            for e in range(W_FIRST):
                load_expert(e)

            def load_next(i, s):
                if isinstance(i, int) and i + W_FIRST < EXPERTS:
                    load_expert(i + W_FIRST)

            act.sem_inc(h_ev, HALVES)

            def relu(half):
                def stage(i, s):
                    act.wait_ge(h_mm, i * HALVES + (half + 1 + HALVES * RING))
                    act.wait_ge(hc_mm, i * HALVES + HALVES)
                    act.activation(hrow[s][:, half * HH:(half + 1) * HH], bank[1 + half][:, :],
                                   ACT.Relu).then_inc(h_ev, 1)
                return stage

            skewed(act, [(0, relu(0)), (0, relu(1)), (0, load_next)], TILES, peel=EXPERTS - W_FIRST)

            shift = t16[0]
            for b in range(BATCH):
                if b % PER == 0:
                    act.wait_ge(tail_shift, b // PER + 1)
                at = slice(b * DIM, (b + 1) * DIM)
                act.activation(u_end[:, at], u_end[:, at], ACT.Identity, bias=shift[:, b:b + 1],
                               scale=rstd[:, b:b + 1]).then_inc(tail_norm, 1)

        @block.vector
        def _(dve):
            dve.wait_ge(ld_bias, 16)
            for i, rest in enumerate((bsrc, *bres)):
                dve.tensor_copy(bpart[i][:, :], rest[:, :]).then_inc(bias_step, 1)
                if i < 2:
                    dve.wait_ge(bias_step, 2 * i + 1)
                    dve.tensor_tensor(bres[i][:, :], rest[:, :], bpart[i][:, :], ALU.subtract).then_inc(bias_step, 1)
                    dve.wait_ge(bias_step, 2 * i + 2)

            dve.memset(mhalf[:, :], -0.5).then_inc(ln, 1)
            dve.memset(zeros[:, :], 0.0).then_inc(zero_set, 1)
            dve.memset(ones3[:, :], 1.0)
            dve.wait_ge(ld_h, 48)
            dve.tensor_tensor(posb[:, :], posb[:, :], tokb[:, :], ALU.add).then_inc(ln, 1)
            dve.wait_ge(ln, 2)
            for g in range(BATCH // 2):
                dve.wait_ge(img_t, g + 1)
                dve.tensor_tensor(h_all[0:IMG, 2 * g * DIM:(2 * g + 2) * DIM].rearrange("p (b c) -> p b c", b=2),
                                  bank[4 + g % 4][0:IMG, :].rearrange("p (b c) -> p b c", b=2),
                                  posb[:, :].unsqueeze(1).to_broadcast([IMG, 2, DIM]),
                                  ALU.add).then_inc(img_rows, 1)
            dve.wait_ge(img_rows, BATCH // 2)

            dve.wait_ge(ld_row, 112)
            dve.tensor_tensor(bdt[:, :], rows8[:, 0:HEADS], rows8[:, HEADS:2 * HEADS], ALU.add).then_inc(bdt_done, 1)
            dve.wait_ge(bdt_done, 1)
            for s in (xs_ev, z_ev):
                dve.sem_inc(s, 1)

            def moments(j, rows, b, s):
                settle(dve)
                dve.bn_stats(nst[j][s][:, :], rows[:, cols(b)]).then_inc(nst_done[j], 1)
                dve.wait_ge(nst_done[j], b + 1)
                settle(dve)
                dve.bn_aggr(nmv[j][s][:, :], nst[j][s][:, :]).then_inc(nag_done[j], 1)
                dve.wait_ge(nag_done[j], b + 1)
                dve.tensor_scalar(nve[j][s][:, :], nmv[j][s][:, 1:2], EPS, None, ALU.add).then_inc(nve_done[j], 1)

            def first_moments(b, s):
                moments(0, h_all, b, s)

            def first_norm(b, s):
                dve.wait_ge(npow_done[0], b + 1)
                dve.tensor_scalar(hn_all[:, cols(b)], h_all[:, cols(b)], nmv[0][s][:, 0:1], nrs[0][s][:, :],
                                  ALU.subtract, ALU.mult).then_inc(n1_done, 1)
                dve.wait_ge(n1_done, b + 1)
                moments(1, hn_all, b, s)

            def second_norm(b, s):
                dve.wait_ge(npow_done[1], b + 1)
                dve.wait_ge(t_done, b + 1)
                dve.tensor_scalar(nslot[s][:, :], hn_all[:, cols(b)], nmv[1][s][:, 0:1], nrs[1][s][:, :],
                                  ALU.subtract, ALU.mult).then_inc(ns_done, 1)

            def add_dt_bias(b, s):
                dve.wait_ge(dt_mm, b + 1)
                dve.tensor_tensor(dt_all[:, cols(b, HEADS)], bank[3][0:LEN, 256:256 + HEADS], bdt[:, :],
                                  ALU.add).then_inc(dt_ev, 1)

            def add_x_bias(b, s):
                if isinstance(b, int) and b == 0:
                    dve.wait_ge(bias_out, 48)
                dve.wait_ge(xs_mm, b + 1)
                dve.tensor_tensor(xs_all[:, cols(b, INNER)], bank[4][0:LEN, :], bx[:, :], ALU.add).then_inc(xs_ev, 1)

            def add_z_bias(b, s):
                dve.wait_ge(z_mm, b + 1)
                dve.tensor_tensor(sz_all[:, cols(b, INNER)], bank[5][0:LEN, :], bz[:, :], ALU.add).then_inc(z_ev, 1)

            skewed(dve, [(-2, second_norm), (0, add_dt_bias), (-4, first_moments), (0, add_x_bias),
                         (-3, first_norm), (0, add_z_bias)], peel=1)

            count = [0]

            def step(i):
                count[0] += 1
                i.then_inc(dm, 1)
                dve.wait_ge(dm, count[0])

            x, neg, e_, q, q2 = dt_all, t128[0], t128[2], t128[4], t128[5]
            dve.wait_ge(dt_ev, BATCH)
            step(dve.scalar_tensor_tensor(neg[:, :], x[:, :], -1.0, x[:, :], ALU.mult, ALU.min))
            step(dve.tensor_scalar(t128[1][:, :], x[:, :], 0.0, None, ALU.max))
            dve.wait_ge(em, 1)
            step(dve.tensor_scalar(t128[3][:, :], e_[:, :], 2.0, None, ALU.add))
            step(dve.reciprocal(neg[:, :], t128[3][:, :]))
            step(dve.tensor_tensor(q[:, :], e_[:, :], neg[:, :], ALU.mult))
            step(dve.tensor_tensor(q2[:, :], q[:, :], q[:, :], ALU.mult))
            step(dve.tensor_scalar(t128[3][:, :], q2[:, :], 1.0 / 17, None, ALU.mult))
            for odd in range(15, 1, -2):
                step(dve.scalar_tensor_tensor(t128[3][:, :], t128[3][:, :], 1.0 / odd, q2[:, :], ALU.add, ALU.mult))
            step(dve.scalar_tensor_tensor(t128[3][:, :], t128[3][:, :], 1.0, q[:, :], ALU.add, ALU.mult))
            step(dve.scalar_tensor_tensor(dt_all[:, :], t128[3][:, :], 2.0, t128[1][:, :], ALU.mult, ALU.add))
            dve.wait_ge(expa_done, 1)
            step(dve.tensor_tensor(t128[3][:, :].rearrange("p (b h) -> p b h", h=HEADS),
                                   dt_all[:, :].rearrange("p (b h) -> p b h", h=HEADS),
                                   exp_a[:, :].unsqueeze(1).to_broadcast([LEN, BATCH, HEADS]), ALU.mult))
            assert count[0] == DM

            dve.wait_ge(ld_ssm, 96)
            for s in (scan_done, h1_done, lg_done):
                dve.sem_inc(s, 1)
            dve.sem_inc(ya_done, RING)
            dve.wait_ge(s_ev, BATCH + 1)

            def scan(b, s):
                dve.wait_ge(b_mm, b + 1 + RING)
                dve.wait_ge(y_mm, b + 1)
                for h in range(HEADS // HPB):
                    at = slice(h * HPB * LEN, (h + 1) * HPB * LEN)
                    i = dve.tensor_tensor_scan(gm[s][:, at], pair[0:LEN, h, 0:HPB * LEN], delta[:, :], 0.0,
                                               ALU.mult, ALU.add)
                i.then_inc(scan_done, 1)

            def add_skip(b, s):
                dve.wait_ge(y_mm, b + 1 + RING)
                dve.wait_ge(prep_done, b + 1)
                dve.wait_ge(t4_mm, b + 1)
                dve.tensor_tensor(yb[s][:, :], bank[0][0:LEN, :], xsd[s][:, :], ALU.add).then_inc(ya_done, 1)

            def weigh(b, s):
                dve.wait_ge(scan_done, b + 1 + 1)
                g3 = gm[s][:, :].rearrange("p (h t) -> p h t", h=HEADS)
                dve.tensor_tensor(g3, g3, s_all[:, bass.ds(b * LEN, LEN)].unsqueeze(1).to_broadcast([LEN, HEADS, LEN]),
                                  ALU.mult).then_inc(g_done, 1)

            def add_residual(b, s):
                dve.wait_ge(o_mm, b + 1 + RING)
                dve.tensor_tensor(h_all[:, cols(b)], bank[2][0:LEN, 0:DIM], h_all[:, cols(b)],
                                  ALU.add).then_inc(h1_done, 1)
                dve.wait_ge(h1_done, b + 1 + 1)
                settle(dve)
                dve.bn_stats(est[s][:, :], h_all[:, cols(b)]).then_inc(st_done, 1)
                dve.wait_ge(st_done, b + 1)
                settle(dve)
                dve.bn_aggr(emv[s][:, :], est[s][:, :]).then_inc(ag_done, 1)
                dve.wait_ge(ag_done, b + 1)
                dve.tensor_scalar(eve[s][:, :], emv[s][:, 1:2], EPS, None, ALU.add).then_inc(ve_done, 1)

            def add_router_bias(b, s):
                dve.wait_ge(l_mm, b + 1 + RING)
                at = cols(b, EXPERTS)
                dve.tensor_tensor(logit[:, at], bank[4][0:LEN, 0:EXPERTS], rows8[:, 4 * HEADS:5 * HEADS],
                                  ALU.add).then_inc(lg_done, 1)

            def norm_target(b, s):
                dve.wait_ge(pow_done, b + 1)
                dve.wait_ge(t2_mm, b + 1)
                dve.wait_ge(tc_done, b + 1)
                dve.tensor_scalar(tslot[s][:, :], h_all[:, cols(b)], emv[s][:, 0:1], ers[s][:, :],
                                  ALU.subtract, ALU.mult).then_inc(tg_done, 1)

            skewed(dve, [(5, add_router_bias), (3, add_residual), (0, scan), (1, add_skip), (3, norm_target),
                         (0, weigh)])

            dve.wait_ge(lg_done, BATCH + 1)
            for b in range(BATCH):
                at = slice(b * EXPERTS, (b + 1) * EXPERTS)
                dve.max(mx8[:, at], logit[:, at]).then_inc(mxd, 1)
            dve.wait_ge(mxd, BATCH)
            for b in range(BATCH):
                at = slice(b * EXPERTS, (b + 1) * EXPERTS)
                dve.max_index(ix8[:, at], mx8[:, at], logit[:, at]).then_inc(mi_done, 1)
            dve.wait_ge(mi_done, BATCH)
            picked = [0]

            def step(i, *also):
                picked[0] += 1
                i.then_inc(rt, 1)
                dve.wait_ge(rt, picked[0])

            def by_batch(t):
                return t[:, :].rearrange("p (b e) -> p b e", e=EXPERTS)

            def per_expert(t):
                return t[:, :].unsqueeze(2).to_broadcast([LEN, BATCH, EXPERTS])

            first, second = mx8[:, 0:8 * BATCH:8], mx8[:, 1:8 * BATCH:8]
            is1, is2, pick, tot, cum, rank = t128
            step(dve.tensor_tensor(t16[0][:, :], second, first, ALU.subtract))
            step(dve.tensor_copy(t16[4][:, :], ix8[:, 0:8 * BATCH:8]))
            step(dve.tensor_copy(t16[5][:, :], ix8[:, 1:8 * BATCH:8]))
            step(dve.tensor_tensor(by_batch(is1), by_batch(iota8), per_expert(t16[4]), ALU.is_equal))
            step(dve.tensor_tensor(by_batch(is2), by_batch(iota8), per_expert(t16[5]), ALU.is_equal))
            step(dve.tensor_tensor(pick[:, :], is1[:, :], is2[:, :], ALU.add))
            assert picked[0] == RT_PICKED
            dve.wait_ge(rt_exp, 1)
            w1, w2 = t16[3], t16[2]
            step(dve.tensor_scalar(w2[:, :], t16[1][:, :], 1.0, None, ALU.add))
            step(dve.reciprocal(w1[:, :], w2[:, :]))
            step(dve.tensor_tensor(w2[:, :], t16[1][:, :], w1[:, :], ALU.mult))

            count8, end8, tiles8, tend8, tstart8, shift8, start8 = r8

            def by_expert(t):
                return t[:, :].rearrange("p (e b) -> p e b", e=EXPERTS)

            dve.wait_ge(rt_cnt, 1)
            step(dve.tensor_copy(by_expert(tot), bank[5][0:LEN, P:2 * P].rearrange("p (b e) -> p e b", e=EXPERTS)))
            step(dve.tensor_tensor_scan(cum[:, :], tot[:, :], zeros[0:LEN, 0:P], 0.0, ALU.add, ALU.add))
            step(dve.tensor_reduce(count8[:, :], by_expert(tot), AXIS_X, ALU.add))
            g = grid[:, 0:EXPERTS * MOST].rearrange("p (e k) -> p e k", k=MOST)
            step(dve.tensor_tensor(g, count8[:, :].unsqueeze(2).to_broadcast([LEN, EXPERTS, MOST]),
                                   small[:, 0:MOST].unsqueeze(1).to_broadcast([LEN, EXPERTS, MOST]), ALU.is_gt))
            step(dve.tensor_reduce(end8[:, :], g, AXIS_X, ALU.add))
            step(dve.tensor_scalar(tiles8[:, :], end8[:, :], 1.0, None, ALU.add))
            step(dve.tensor_tensor_scan(tend8[:, :], tiles8[:, :], zeros[0:LEN, 0:EXPERTS], 0.0, ALU.add, ALU.add))
            g = grid[:, :].rearrange("p (t e) -> p t e", e=EXPERTS)
            step(dve.tensor_tensor(g, tend8[:, :].unsqueeze(1).to_broadcast([LEN, TILES, EXPERTS]),
                                   small[:, MOST:MOST + TILES].unsqueeze(2).to_broadcast([LEN, TILES, EXPERTS]),
                                   ALU.is_gt))
            step(dve.tensor_reduce(tile_row[:, :], g, AXIS_X, ALU.add))
            step(dve.tensor_scalar(tile_row[:, :], tile_row[:, :], 1.0, 0.0, ALU.subtract, ALU.max))
            dve.tensor_copy(tile_slot[:, :], tile_row[:, :]).then_inc(table_done, 1)
            step(dve.tensor_tensor(tstart8[:, :], tend8[:, :], tiles8[:, :], ALU.subtract))
            step(dve.tensor_tensor(start8[:, :], cum[:, BATCH - 1:BATCH * EXPERTS:BATCH], count8[:, :], ALU.subtract))
            step(dve.scalar_tensor_tensor(shift8[:, :], tstart8[:, :], float(P), start8[:, :], ALU.mult, ALU.subtract))
            step(dve.tensor_tensor(cum[:, :], cum[:, :], tot[:, :], ALU.subtract))
            step(dve.tensor_tensor(by_expert(cum), by_expert(cum),
                                   shift8[:, :].unsqueeze(2).to_broadcast([LEN, EXPERTS, BATCH]), ALU.add))
            step(dve.tensor_tensor(by_batch(rank), bank[5][0:LEN, 0:P].rearrange("p (b e) -> p b e", e=EXPERTS),
                                   cum[:, :].rearrange("p (e b) -> p b e", e=EXPERTS), ALU.add))
            for mask, row, dst in zip((is1, is2), placef, place_of):
                step(dve.tensor_tensor(tot[:, :], mask[:, :], rank[:, :], ALU.mult))
                step(dve.tensor_reduce(row[:, :], by_batch(tot), AXIS_X, ALU.add))
                i = dve.tensor_copy(dst[:, :], row[:, :])
            i.then_inc(places_done, 1)

            for s, n in ((xc_ev, 1), (hc_ev, HALVES), (yr_ev, 1)):
                dve.sem_inc(s, n)
            dve.wait_ge(mixed, 1)

            def columns_x(i, s):
                dve.wait_ge(xc_mm, i + (1 + RING))
                dve.wait_ge(h_mm, i * HALVES + HALVES)
                dve.tensor_copy(xcol[s][:, :, :], bank[0][:, 0:DIM].rearrange("p (k c) -> p k c", k=KD)
                                ).then_inc(xc_ev, 1)

            def columns_hidden(half):
                def stage(i, s):
                    dve.wait_ge(hc_mm, i * HALVES + (half + 1 + HALVES * RING))
                    dve.wait_ge(yr_mm, i + 1)
                    dve.tensor_copy(hcol[s][:, half * KH:(half + 1) * KH, :],
                                    bank[3 + half][:, :].rearrange("p (k c) -> p k c", k=KH)).then_inc(hc_ev, 1)
                return stage

            def results(i, s):
                dve.wait_ge(yr_mm, i + (1 + RING))
                dve.wait_ge(y_out, i * 16 + 16)
                dve.tensor_copy(yrow[s][:, :], bank[5][:, 0:DIM]).then_inc(yr_ev, 1)

            skewed(dve, [(1, columns_hidden(0)), (1, columns_hidden(1)), (-1, columns_x), (1, results)], TILES)

            shift = t16[0]
            at_tail = [0]
            dve.wait_ge(hb_done, 1)

            def tail_step(i):
                at_tail[0] += 1
                i.then_inc(tail, 1)

            for c in range(CHUNKS):
                batches = range(c * PER, (c + 1) * PER)
                dve.wait_ge(back_in[c], 16 * TOP * PER)
                for w, y in zip((w1, w2), back):
                    for b in batches:
                        at = slice(b * DIM, (b + 1) * DIM)
                        tail_step(dve.scalar_tensor_tensor(u_end[:, at], y[:, at], w[:, b:b + 1], u_end[:, at],
                                                           ALU.mult, ALU.add))
                    dve.wait_ge(tail, at_tail[0])
                for b in batches:
                    tail_step(dve.bn_stats(stats[:, 6 * b:6 * b + 6], u_end[:, b * DIM:(b + 1) * DIM]))
                dve.wait_ge(tail, at_tail[0])
                for b in batches:
                    tail_step(dve.bn_aggr(mv[:, 2 * b:2 * b + 2], stats[:, 6 * b:6 * b + 6]))
                dve.wait_ge(tail, at_tail[0])
                dve.tensor_scalar(ve[:, c * PER:(c + 1) * PER], mv[:, 2 * c * PER + 1:2 * (c + 1) * PER:2], EPS, None,
                                  ALU.add).then_inc(tail_ve, 1)
                dve.wait_ge(tail_pow, c + 1)
                at = slice(c * PER, (c + 1) * PER)
                dve.scalar_tensor_tensor(shift[:, at], mv[:, 2 * c * PER:2 * (c + 1) * PER:2], -1.0, rstd[:, at],
                                         ALU.mult, ALU.mult).then_inc(tail_shift, 1)
                dve.wait_ge(tail_norm, (c + 1) * PER)
                at = slice(c * PER * DIM, (c + 1) * PER * DIM)
                x4 = u_end[:, at].rearrange("p (b c) -> p b c", b=PER)
                tail_step(dve.tensor_tensor(x4, x4, fgam[:, :].unsqueeze(1).to_broadcast([LEN, PER, DIM]), ALU.mult))
                dve.wait_ge(tail, at_tail[0])
                dve.tensor_tensor(h_end[:, at], h_end[:, at], u_end[:, at], ALU.add).then_inc(fin, 1)

        @block.gpsimd
        def _(pool):
            pool.wait_ge(ln, 1)
            pool.wait_ge(ld_row, 112)

            def first_root(b, s):
                pool.wait_ge(nve_done[0], b + 1)
                pool.tensor_tensor(nrs[0][s][:, :], nve[0][s][:, :], mhalf[:, 0:1], ALU.pow).then_inc(npow_done[0], 1)

            def second_root(b, s):
                pool.wait_ge(nve_done[1], b + 1)
                pool.tensor_tensor(nrs[1][s][:, :], nve[1][s][:, :], mhalf[:, 0:1], ALU.pow).then_inc(npow_done[1], 1)

            def residual(b, s):
                h = h_all[:, cols(b)]
                pool.wait_ge(n1_done, b + 1)
                settle(pool)
                pool.tensor_tensor(h, h, hn_all[:, cols(b)], ALU.add).then_inc(res_sum, 1)
                pool.wait_ge(res_sum, b + 1)
                settle(pool)
                pool.tensor_tensor(h, h, bout[:, :], ALU.add).then_inc(res_done, 1)

            skewed(pool, [(-4, first_root), (-3, second_root), (-3, residual)])

            pool.wait_ge(dec_done, 1)
            pool.wait_ge(s_mm, BATCH + RING)
            pool.wait_ge(sz_done, BATCH // 2)
            pool.wait_ge(xs_ev, BATCH + 1)

            def by_head(t):
                return t.rearrange("p (h c) -> p h c", h=HEADS)

            def prepare(b, s):
                pool.wait_ge(y_mm, b + 1)
                pool.wait_ge(ya_done, b + 1)
                x = by_head(xs_all[:, cols(b, INNER)])
                pool.tensor_tensor(by_head(dtx[s][:, :]), x,
                                   dt_all[:, cols(b, HEADS)].unsqueeze(2).to_broadcast([LEN, HEADS, HEAD]), ALU.mult)
                pool.tensor_tensor(by_head(xsd[s][:, :]), x,
                                   rows8[:, 3 * HEADS:4 * HEADS].unsqueeze(2).to_broadcast([LEN, HEADS, HEAD]),
                                   ALU.mult).then_inc(prep_done, 1)

            def gate(b, s):
                pool.wait_ge(ya_done, b + 1 + RING)
                settle(pool)
                pool.tensor_tensor(yb[s][:, :], yb[s][:, :], sz_all[:, cols(b, INNER)], ALU.mult).then_inc(y2_done, 1)

            def inverse_root(b, s):
                pool.wait_ge(ve_done, b + 1)
                pool.tensor_tensor(ers[s][:, :], eve[s][:, :], mhalf[:, 0:1], ALU.pow).then_inc(pow_done, 1)

            skewed(pool, [(0, prepare), (3, inverse_root), (1, gate)])

            pool.wait_ge(l_mm, BATCH + RING)
            pool.wait_ge(mi_done, BATCH)
            pool.wait_ge(tt_done, BATCH + 1)
            pool.wait_ge(tc_done, BATCH + RING)
            pool.wait_ge(y2_done, BATCH)
            pool.wait_ge(pow_done, BATCH)
            pool.drain().then_inc(mixed, 1)


            pool.wait_ge(zero_out, 16)
            pool.wait_ge(places_done, 1)
            for b in range(BATCH):
                for dst in place_of:
                    pool.indirect_dma_start(xg[:, :], bass.IndirectOffsetOnAxis(dst[:, b:b + 1], 0),
                                            hn_all[:, b * DIM:(b + 1) * DIM], None).then_inc(placed, 16)

            pool.wait_ge(yr_mm, 2 * (MOST + 1) + RING)
            pool.wait_ge(kept, 32 * BATCH)
            pool.dma_start(u_end[:, :], u_dram).then_inc(ends_in, 16)
            pool.dma_start(h_end[:, :], h_dram).then_inc(ends_in, 16)
            pool.wait_ge(ends_in, 32)
            h3 = h_end[:, :].rearrange("p (b c) -> p b c", b=BATCH)
            pool.tensor_tensor(h3, h3, fbet[:, :].unsqueeze(1).to_broadcast([LEN, BATCH, DIM]),
                               ALU.add).then_inc(hb_done, 1)

            pool.wait_ge(y_out, 16 * (TILES + RING))
            for c in range(CHUNKS + 1):
                if c < CHUNKS:
                    for b in range(c * PER, (c + 1) * PER):
                        for i in range(TOP):
                            pool.indirect_dma_start(back[i][:, b * DIM:(b + 1) * DIM], None, yg[:, :],
                                                    bass.IndirectOffsetOnAxis(place_of[i][:, b:b + 1], 0)
                                                    ).then_inc(back_in[c], 16)
                if c > 0:
                    at = slice((c - 1) * PER, c * PER)
                    pool.wait_ge(tail_ve, c)
                    pool.tensor_tensor(rstd[:, at], ve[:, at], mhalf[:, at], ALU.pow).then_inc(tail_pow, 1)


def kernel(x, txt, L0_tok_W, L0_tok_b, L0_tok_pos_embd, L0_attn_ln_gamma, L0_attn_ln_beta, L0_attn_W_in,
           L0_attn_b_in, L0_attn_A_log, L0_attn_D_skip, L0_attn_dt_bias, L0_attn_W_out, L0_attn_b_out, L0_ffn_Wr,
           L0_ffn_br, L0_ffn_W1, L0_ffn_b1, L0_ffn_W2, L0_ffn_b2, L0_ffn_gamma, L0_ffn_beta):
    import concourse.bacc as bacc
    from concourse.bass_utils import run_bass_kernel_spmd

    def tiles(w, k):
        return np.asarray(w).reshape(k, P, -1).transpose(1, 0, 2)

    side = 16
    per = 96 // side
    patches = np.asarray(x).reshape(BATCH, 3, per, side, per, side).transpose(1, 3, 5, 0, 2, 4)
    w1 = np.asarray(L0_ffn_W1).transpose(0, 2, 1).reshape(EXPERTS, KD, P, HIDDEN).transpose(0, 2, 1, 3)
    w2 = np.asarray(L0_ffn_W2).transpose(0, 2, 1).reshape(EXPERTS, KF, P, DIM).transpose(0, 2, 1, 3)
    b_in = np.asarray(L0_attn_b_in)
    eye = np.eye(P, dtype=np.float32)
    arrays = {
        "patch": tiles(patches.reshape(PATCH, BATCH * IMG), KP),
        "w_tok": tiles(np.asarray(L0_tok_W).T, KP),
        "txt": txt,
        "pos": np.asarray(L0_tok_pos_embd)[0],
        "tok_b": L0_tok_b,
        "w_in": tiles(L0_attn_W_in, KD),
        "w_out": tiles(L0_attn_W_out, KI),
        "wr": tiles(np.asarray(L0_ffn_Wr).T, KD),
        "b_bc": b_in[C_BC:C_DT].reshape(P, 1),
        "b_x": b_in[C_X:C_BC],
        "b_z": b_in[C_Z:C_X],
        "b_out": L0_attn_b_out,
        "gam_t": np.asarray(L0_attn_ln_gamma).reshape(KD, P).T,
        "bet_t": np.asarray(L0_attn_ln_beta).reshape(KD, P).T,
        "rows8": np.concatenate([b_in[C_DT:], np.asarray(L0_attn_dt_bias), np.asarray(L0_attn_A_log),
                                 np.asarray(L0_attn_D_skip), np.asarray(L0_ffn_br)]),
        "experts": np.concatenate([w1.reshape(EXPERTS, P, -1), w2.reshape(EXPERTS, P, -1)], axis=2),
        "biases": np.concatenate([np.asarray(L0_ffn_b1), np.asarray(L0_ffn_b2)], axis=1)[::-1].reshape(BIAS_ROWS, P),
        "f_gam": L0_ffn_gamma,
        "f_bet": L0_ffn_beta,
        "ident": eye,
        "delta": np.tile(eye[:LEN, :LEN], (1, HPB)),
        "iota8": np.tile(np.arange(EXPERTS, dtype=np.float32), (LEN, BATCH)),
        "small": np.concatenate([P * np.arange(1, MOST + 1), np.arange(TILES)]).astype(np.float32),
        "before": np.concatenate([np.triu(np.ones((LEN, LEN)), 1), np.ones((LEN, LEN))], axis=1).astype(np.float32),
        "rowmask": np.where(np.arange(LEN) == 0, -1e30, 0.0).astype(np.float32).reshape(LEN, 1),
    }
    arrays = {f"in_{k}": np.ascontiguousarray(v) for k, v in arrays.items()}
    nc = bacc.Bacc("TRN2", target_bir_lowering=False, num_devices=1)
    d = {k[3:]: nc.dram_tensor(k, v.shape, F32, kind="ExternalInput").ap() for k, v in arrays.items()}
    out = nc.dram_tensor("out", (BATCH, LEN, DIM), F32, kind="ExternalOutput").ap()
    build(nc, d, out)
    r = run_bass_kernel_spmd(nc, [arrays], core_ids=[0])
    return r.results[0]["out"]
```

```python
from contextlib import ExitStack

import numpy as np
import concourse.bass as bass
from concourse import mybir

F32 = mybir.dt.float32
BF16 = mybir.dt.bfloat16
U32 = mybir.dt.uint32
ALU = mybir.AluOpType
ACT = mybir.ActivationFunctionType
AXIS_X = mybir.AxisListType.X

BATCH, IMG, TXT, DIM = 16, 36, 77, 256
LEN = IMG + TXT
TOK = BATCH * LEN
PATCH = 768
INNER, STATE, HEADS, HEAD = 512, 64, 8, 64
PROJ = 2 * INNER + 2 * STATE + HEADS
EXPERTS, HIDDEN = 8, 1024
EPS = 1e-5
P = 128
KP = PATCH // P
KD = DIM // P
KI = INNER // P
KF = HIDDEN // P
TOP = 2
TILES = (TOP * TOK + EXPERTS * (P - 1)) // P
REGION = -(-TOK // P)
WSIZE = KD * HIDDEN + KF * DIM
BIAS_ROWS = EXPERTS * DIM // P
W_FIRST = 2
Y_RING = 6
HALVES = 2
HH = HIDDEN // HALVES
KH = HH // P
CHUNKS = 8
PER = BATCH // CHUNKS
HALF = BATCH * IMG // 2
HPB = 4
RING = 2
LATE = 2
R_STEPS = 10
R_PICKED = 7
DM = 17
C_Z, C_X, C_BC, C_DT = 0, INNER, 2 * INNER, 2 * INNER + 2 * STATE


def build(nc, d, out):
    with ExitStack() as ctx:
        def sem(name):
            return ctx.enter_context(nc.semaphore(name))

        top = [16512]

        def place(name, shape, dt=F32, at=None):
            size = 4
            for n in shape[1:]:
                size *= n
            size = -(-size // 32) * 32
            where = top[0] if at is None else at[0]
            t = nc.alloc_sbuf_tensor_at(name, list(shape), dt, offset=where)
            if at is None:
                top[0] += size
            else:
                at[0] += size
            return t

        ident = place("ident", [P, P])
        iota8 = place("iota8", [LEN, 2 * TOP * EXPERTS])
        zeros = place("zeros", [P, DIM])
        rowmask = place("rowmask", [LEN, 1])
        fgam = place("fgam", [LEN, DIM])
        fbet = place("fbet", [LEN, DIM])
        b_bc = place("b_bc", [P, 1])
        gam_t = place("gam_t", [P, KD])
        bet_t = place("bet_t", [P, KD])
        rows8 = place("rows8", [LEN, 5 * HEADS])
        bdt = place("bdt", [LEN, HEADS])
        exp_a = place("exp_a", [LEN, HEADS])
        wr = place("wr", [P, KD, EXPERTS])
        mhalf = place("mhalf", [LEN, BATCH])
        stats = place("stats", [LEN, BATCH * 6])
        mv = place("mv", [LEN, BATCH * 2])
        ve = place("ve", [LEN, BATCH])
        rstd = place("rstd", [LEN, BATCH])
        dt_all = place("dt_all", [LEN, BATCH * HEADS])
        dec_all = place("dec_all", [LEN, BATCH * HEADS])
        pair_logits = place("pair_logits", [LEN, 2 * EXPERTS])
        mx8 = place("mx8", [LEN, 2 * 8])
        ix8 = place("ix8", [LEN, 2 * 8], U32)
        ixf = place("ixf", [LEN, 2 * TOP])
        mask = place("mask", [LEN, 2 * TOP * EXPERTS])
        picks = place("picks", [LEN, 2 * EXPERTS])
        seen = place("seen", [LEN, 2 * EXPERTS])
        rank = place("rank", [LEN, 2 * EXPERTS])
        ranked = place("ranked", [LEN, 2 * TOP * EXPERTS])
        placef = place("placef", [LEN, 2 * TOP])
        t128 = [place(f"t128_{i}", [LEN, BATCH * HEADS]) for i in range(6)]
        t16 = [place(f"t16_{i}", [LEN, BATCH]) for i in range(6)]
        small = place("small", [LEN, REGION - 1 + TILES + EXPERTS])
        before = place("before", [LEN, 2 * LEN])
        grid = place("grid", [LEN, TILES * EXPERTS])
        r8 = [place(f"r8_{i}", [LEN, EXPERTS]) for i in range(5)]
        row_f = [place(f"row_f{i}", [LEN, TILES]) for i in range(3)]
        tile_slot = place("tile_slot", [LEN, TILES], U32)
        tile_at = place("tile_at", [LEN, TILES], U32)
        place_of = place("place_of", [LEN, BATCH * TOP], U32)
        listed_at = place("listed_at", [LEN, BATCH * TOP], U32)
        in_tile = place("in_tile", [LEN, BATCH * TOP], U32)
        tile_no = place("tile_no", [LEN, BATCH * TOP], U32)
        goals = place("goals", [LEN, BATCH * TOP], U32)
        goal_of = place("goal_of", [P, TILES], U32)
        bias3 = place("bias3", [3, EXPERTS, DIM], BF16)
        ones3 = place("ones3", [3, P], BF16)
        dead = top[0]
        hn_all = place("hn_all", [LEN, BATCH * DIM])
        h_all = place("h_all", [LEN, BATCH * DIM])
        delta = place("delta", [LEN, HPB * LEN])
        biases = [top[0]]
        bx = place("bx", [LEN, INNER])
        bz = place("bz", [LEN, INNER])
        posb = place("posb", [IMG, DIM])
        tokb = place("tokb", [IMG, DIM])
        biases_end = top[0]
        bout = place("bout", [LEN, DIM])
        phase = top[0]

        a = [phase]
        xs_all = place("xs_all", [LEN, BATCH * INNER], at=a)
        sz_all = place("sz_all", [LEN, BATCH * INNER], at=a)
        s_all = place("s_all", [LEN, BATCH * LEN], at=a)
        w_out = place("w_out", [P, KI, DIM], at=a)
        work = a[0]
        a = [work]
        w_in = place("w_in", [P, KD, PROJ], at=a)
        nslot = [place(f"nslot{i}", [LEN, DIM], at=a) for i in range(RING)]
        nt = [place(f"nt{i}", [P, KD, LEN], at=a) for i in range(RING)]
        bct = [place(f"bct{i}", [P, LEN], at=a) for i in range(RING)]
        ct = [place(f"ct{i}", [STATE, LEN], at=a) for i in range(RING)]
        nst, nmv, nve, nrs = ([[place(f"{name}{j}_{i}", [LEN, n], at=a) for i in range(RING)] for j in range(2)]
                              for name, n in (("nst", 6), ("nmv", 2), ("nve", 1), ("nrs", 1)))
        work_top = a[0]
        b = [phase]
        bsrc = place("bsrc", [BIAS_ROWS, P], at=b)
        bres = [place(f"bres{i}", [BIAS_ROWS, P], at=b) for i in range(2)]
        bpart = [place(f"bpart{i}", [BIAS_ROWS, P], BF16, at=b) for i in range(3)]
        patch = place("patch", [P, KP, BATCH * IMG], at=b)
        w_tok = place("w_tok", [P, KP, DIM], at=b)
        emb_t = place("emb_t", [P, KD, BATCH * IMG], at=b)
        a = [work]
        decs = [place(f"decs{i}", [LEN, HEADS], at=a) for i in range(RING)]
        dtx = [place(f"dtx{i}", [LEN, INNER], at=a) for i in range(RING)]
        xsd = [place(f"xsd{i}", [LEN, INNER], at=a) for i in range(RING)]
        gm = [place(f"gm{i}", [LEN, HEADS * LEN], at=a) for i in range(RING)]
        yb = [place(f"yb{i}", [LEN, INNER], at=biases) for i in range(RING)]
        yt = [place(f"yt{i}", [P, KI, LEN], at=a) for i in range(RING)]
        tslot = [place(f"tslot{i}", [LEN, DIM], at=biases) for i in range(RING)]
        assert biases[0] <= biases_end
        tt = [place(f"tt{i}", [P, KD, LEN], at=a) for i in range(RING)]
        est = [place(f"est{i}", [LEN, 6], at=a) for i in range(RING)]
        emv = [place(f"emv{i}", [LEN, 2], at=a) for i in range(RING)]
        eve = [place(f"eve{i}", [LEN, 1], at=a) for i in range(RING)]
        ers = [place(f"ers{i}", [LEN, 1], at=a) for i in range(RING)]
        assert max(a[0], b[0], work_top) <= nc.sbuf_top - WSIZE * 4, (max(a[0], b[0], work_top), nc.sbuf_top - WSIZE * 4)

        a = [dead]
        xrow = [place(f"xrow{i}", [P, DIM], at=a) for i in range(RING)]
        xcol = [place(f"xcol{i}", [P, KD, P], at=a) for i in range(RING)]
        hrow = [place(f"hrow{i}", [P, HIDDEN], at=a) for i in range(RING)]
        b1col = [place(f"b1col{i}", [P, KF], at=a) for i in range(Y_RING)]
        hcol = [place(f"hcol{i}", [P, KF, P], at=a) for i in range(RING)]
        yrow = [place(f"yrow{i}", [P, DIM], at=a) for i in range(Y_RING)]
        w_at = nc.sbuf_top - EXPERTS * WSIZE * 4
        assert a[0] <= w_at, (a[0], w_at)
        w_all = place("w_all", [P, EXPERTS, WSIZE], at=[w_at])
        h_end = place("h_end", [LEN, BATCH * DIM], at=[w_at + (EXPERTS - 1) * WSIZE * 4])
        u_end = place("u_end", [LEN, BATCH * DIM], at=[w_at + (EXPERTS - 2) * WSIZE * 4])
        a = [w_at]
        back = [place(f"back{i}", [LEN, BATCH * DIM], at=a) for i in range(TOP)]

        bank = [ctx.enter_context(nc.psum_tensor(f"bank{i}", [P, 512], F32)) for i in range(6)]
        pair = ctx.enter_context(nc.psum_tensor("pair", [P, 2, 512], F32))
        bank += [pair[:, 0, :], pair[:, 1, :]]
        xg = nc.dram_tensor("xg", [(EXPERTS * REGION + 1) * P, DIM], F32).ap()
        yg = nc.dram_tensor("yg", [TOP * TOK + TILES * P, DIM], F32).ap()
        goal_list = nc.dram_tensor("goal_list", [TILES * P, 1], U32).ap()
        h_dram = nc.dram_tensor("h_dram", [LEN, BATCH * DIM], F32).ap()
        u_dram = nc.dram_tensor("u_dram", [LEN, BATCH * DIM], F32).ap()
        bparts = nc.dram_tensor("bparts", [3, EXPERTS * DIM], BF16).ap()

        settled = sem("settled")
        ld_tok = [sem(f"ld_tok{k}") for k in range(KP)]
        ld_ident, ld_h, ld_proj, ld_ssm, ld_row = (
            sem(n) for n in ("ld_ident", "ld_h", "ld_proj", "ld_ssm", "ld_row"))
        emb_mm, emb_sb, img_t, img_rows = (sem(n) for n in ("emb_mm", "emb_sb", "img_t", "img_rows"))
        ln, n1_done, res_sum, res_done, bdt_done, expa_done = (
            sem(n) for n in ("ln", "n1_done", "res_sum", "res_done", "bdt_done", "expa_done"))
        nst_done, nag_done, nve_done, npow_done = ([sem(f"{name}{j}") for j in range(2)] for name in
                                                   ("nst_done", "nag_done", "nve_done", "npow_done"))
        ns_done, t_done, nt_done, bc_mm, dt_mm, xs_mm, z_mm, s_mm = (
            sem(n) for n in ("ns_done", "t_done", "nt_done", "bc_mm", "dt_mm", "xs_mm", "z_mm", "s_mm"))
        bc_ev, c_ev, dt_ev, xs_ev, z_ev, sz_done, s_ev = (
            sem(n) for n in ("bc_ev", "c_ev", "dt_ev", "xs_ev", "z_ev", "sz_done", "s_ev"))
        dm, em, dec_done, mixed = (sem(n) for n in ("dm", "em", "dec_done", "mixed"))
        decs_done, prep_done, b_mm, scan_done, g_done, y_mm, ya_done, y2_done, t4_mm, yt_done, o_mm, h1_done, xsd_done = (
            sem(n) for n in ("decs_done", "prep_done", "b_mm", "scan_done", "g_done", "y_mm", "ya_done", "y2_done",
                             "t4_mm", "yt_done", "o_mm", "h1_done", "xsd_done"))
        st_done, ag_done, ve_done, pow_done, tg_done, t2_mm, tc_done, tt_done, l_mm, lg_done = (
            sem(n) for n in ("st_done", "ag_done", "ve_done", "pow_done", "tg_done", "t2_mm", "tc_done", "tt_done",
                             "l_mm", "lg_done"))
        route, rank_mm, seen_done, place_done, apart, table_step, ratio_done, count_mm, table_done = (
            sem(n) for n in ("route", "rank_mm", "seen_done", "place_done", "apart", "table_step",
                             "ratio_done", "count_mm", "table_done"))
        listed, ld_goals, unlisted, goals_out, goals_in, zero_set, zero_out, placed = (
            sem(n) for n in ("listed", "ld_goals", "unlisted", "goals_out", "goals_in", "zero_set", "zero_out", "placed"))
        ld_bias, bias_step, bias_out, bias_in = (sem(n) for n in ("ld_bias", "bias_step", "bias_out", "bias_in"))
        w_ld = [sem(f"w_ld{e}") for e in range(EXPERTS)]
        x_in, xc_mm, xc_ev, h_mm, h_ev, hc_mm, hc_ev, yr_mm, yr_ev, y_out, y_free, b1_in = (
            sem(n) for n in ("x_in", "xc_mm", "xc_ev", "h_mm", "h_ev", "hc_mm", "hc_ev", "yr_mm", "yr_ev", "y_out",
                             "y_free", "b1_in"))
        scaled = [sem(f"scaled{c}") for c in range(CHUNKS)]
        fin = [sem(f"fin{c}") for c in range(CHUNKS)]
        back_in = [sem(f"back_in{c}") for c in range(CHUNKS)]
        kept, ends_in, hb_done, tail, tail_ve, tail_pow, tail_shift, tail_norm, out_done = (
            sem(n) for n in ("kept", "ends_in", "hb_done", "tail", "tail_ve", "tail_pow", "tail_shift", "tail_norm",
                             "out_done"))

        block = ctx.enter_context(nc.Block())

        def settle(eng):
            eng.sem_inc(settled, 1)

        def finish(eng, c):
            eng.wait_ge(tail_norm, (c + 1) * PER)
            at = slice(c * PER * DIM, (c + 1) * PER * DIM)
            rows = u_end[:, at].rearrange("p (b c) -> p b c", b=PER)
            eng.tensor_tensor(rows, rows, fgam[:, :].unsqueeze(1).to_broadcast([LEN, PER, DIM]), ALU.mult
                              ).then_inc(scaled[c], 1)
            eng.wait_ge(scaled[c], 1)
            eng.tensor_tensor(h_end[:, at], h_end[:, at], u_end[:, at], ALU.add).then_inc(fin[c], 1)

        def cols(b, n=DIM):
            return bass.ds(b * n, n)

        def pairs(eng, first, last, body):
            n = (last - first) // 2
            with eng.Fori(0, n) as p:
                for s in range(2):
                    body(p * 2 + (first + s), (first + s) % 2)
            for b in range(first + 2 * n, last):
                body(b, b % 2)

        def late(b):
            return isinstance(b, int) and b >= BATCH - LATE

        def skewed(eng, stages, count=BATCH, peel=0, ring=RING):
            lo, hi = min(lag for lag, _ in stages), max(lag for lag, _ in stages)
            first, last = max(hi, peel), count + lo
            last -= (last - first) % ring

            def turn(n, place):
                for lag, f in stages:
                    if not isinstance(n, int) or 0 <= n - lag < count:
                        f(n - lag, (place - lag) % ring)

            for n in range(lo, first):
                turn(n, n % ring)
            if last > first:
                with eng.Fori(0, (last - first) // ring) as p:
                    for s in range(ring):
                        turn(p * ring + (first + s), (first + s) % ring)
            for n in range(max(first, last), count + hi):
                turn(n, n % ring)

        @block.sync
        def _(sp):
            for k in range(KP):
                sp.dma_start(w_tok[:, k, :], d["w_tok"][:, k, :]).then_inc(ld_tok[k], 16)
                sp.dma_start(patch[:, k, :], d["patch"][:, k, :]).then_inc(ld_tok[k], 16)
            sp.dma_start(ident[:, :], d["ident"]).then_inc(ld_ident, 16)
            sp.dma_start(h_all[IMG:LEN, :].rearrange("p (b c) -> p b c", b=BATCH),
                         d["txt"].rearrange("b t c -> t b c")).then_inc(ld_h, 16)
            sp.dma_start(w_in[:, :, :], d["w_in"]).then_inc(ld_proj, 16)
            sp.dma_start(b_bc[:, :], d["b_bc"]).then_inc(ld_proj, 16)
            sp.dma_start(gam_t[:, :], d["gam_t"]).then_inc(ld_proj, 16)
            sp.dma_start(bet_t[:, :], d["bet_t"]).then_inc(ld_proj, 16)
            sp.dma_start(delta[:, :], d["delta"]).then_inc(ld_ssm, 16)
            sp.dma_start(w_out[:, :, :], d["w_out"]).then_inc(ld_ssm, 16)
            sp.dma_start(wr[:, :, :], d["wr"]).then_inc(ld_ssm, 16)
            sp.dma_start(iota8[:, :], d["iota8"]).then_inc(ld_ssm, 16)
            sp.dma_start(small[:, :], d["small"].partition_broadcast(LEN)).then_inc(ld_ssm, 16)
            sp.dma_start(before[:, :], d["before"]).then_inc(ld_ssm, 16)
            sp.dma_start(goals[:, :], d["goals"]).then_inc(ld_goals, 16)
            sp.dma_start(goal_list, d["unlisted"]).then_inc(unlisted, 16)
            for i in range(3):
                sp.wait_ge(bias_step, 2 * i + 1)
                sp.dma_start(bparts[i:i + 1, :].rearrange("o (r c) -> (o r) c", c=P), bpart[i][:, :]
                             ).then_inc(bias_out, 16)
            sp.wait_ge(bias_out, 48)
            sp.dma_start(bias3[:, :, :], bparts.rearrange("i (e n) -> i e n", e=EXPERTS)).then_inc(bias_in, 16)
            sp.wait_ge(zero_set, 1)
            sp.dma_start(xg.rearrange("(a p) n -> p a n", p=P),
                         zeros[:, :].unsqueeze(1).to_broadcast([P, EXPERTS * REGION + 1, DIM])).then_inc(zero_out, 16)

            def keep(b, s):
                sp.wait_ge(tc_done, b + (1 + RING))
                settle(sp)
                sp.dma_start(u_dram[:, cols(b)], hn_all[:, cols(b)]).then_inc(kept, 16)
                sp.dma_start(h_dram[:, cols(b)], h_all[:, cols(b)]).then_inc(kept, 16)

            pairs(sp, 0, BATCH, keep)

            sp.sem_inc(x_in, 16)
            sp.wait_ge(table_done, 1)
            sp.wait_ge(placed, 16 * TOP * BATCH)
            sp.wait_ge(kept, 32 * BATCH)

            def first_place(i):
                return sp.value_load(tile_at[0:1, bass.ds(i, 1)], min_val=0, max_val=EXPERTS * REGION) * P

            def load_rows(i, s):
                sp.wait_ge(xc_mm, i + 1)
                sp.wait_ge(x_in, i * 16 + 16)
                settle(sp)
                sp.dma_start(xrow[s % RING][:, :], xg[bass.ds(first_place(i), P), :]).then_inc(x_in, 16)

            def load_bias(i, s):
                sp.wait_ge(yr_mm, i + 1)
                sp.wait_ge(b1_in, i * 16 + 16)
                settle(sp)
                e = sp.value_load(tile_slot[0:1, bass.ds(i, 1)], min_val=0, max_val=EXPERTS - 1)
                sp.dma_start(b1col[s][:, :], d["b1"][bass.ds(e, 1), :, :].rearrange("e p k -> (e p) k")
                             ).then_inc(b1_in, 16)

            sp.sem_inc(b1_in, 16)
            skewed(sp, [(0, load_rows), (1, load_bias)], TILES, ring=Y_RING)

            sp.wait_ge(y_out, 16 * TILES)
            for c in range(CHUNKS):
                for i in range(TOP):
                    first = (i * BATCH + c * PER) * LEN
                    sp.dma_start(back[i][:, c * PER * DIM:(c + 1) * PER * DIM].rearrange("p (b n) -> p b n", b=PER),
                                 yg[first:first + PER * LEN, :].rearrange("(b p) n -> p b n", b=PER)
                                 ).then_inc(back_in[c], 16)

            dst = out.rearrange("b t c -> t b c")
            for c in range(CHUNKS):
                sp.wait_ge(fin[c], 1)
                sp.dma_start(dst[:, PER * c:PER * (c + 1), :],
                             h_end[:, c * PER * DIM:(c + 1) * PER * DIM].rearrange("p (b c) -> p b c", b=PER)
                             ).then_inc(out_done, 16)
            sp.wait_ge(out_done, 16 * CHUNKS)

        @block.tensor
        def _(pe):
            for k in range(KP):
                pe.wait_ge(ld_tok[k], 32)
                for q in range(2 * KD):
                    e, half = q // 2, q % 2
                    mm = pe.matmul(bank[q][:, 0:HALF], w_tok[:, k, e * P:(e + 1) * P],
                                   patch[:, k, half * HALF:(half + 1) * HALF], start=(k == 0), stop=(k == KP - 1))
                    if k == KP - 1:
                        mm.then_inc(emb_mm, 1)
            pe.wait_ge(ld_ident, 16)
            pe.wait_ge(emb_sb, 2 * KD)
            for g in range(BATCH // 2):
                if g >= 4:
                    pe.wait_ge(img_rows, g - 3)
                for j in range(2 * KD):
                    bb, e = j // KD, j % KD
                    mm = pe.transpose(bank[4 + g % 4][0:IMG, j * P:(j + 1) * P],
                                      emb_t[:, e, (2 * g + bb) * IMG:(2 * g + bb + 1) * IMG], ident[:, :])
                mm.then_inc(img_t, 1)

            for s in (t_done, s_mm):
                pe.sem_inc(s, RING)
            pe.wait_ge(img_rows, BATCH // 2)
            pe.wait_ge(ld_proj, 64)

            def turn_rows(b, s):
                pe.wait_ge(ns_done, b + 1)
                pe.wait_ge(nt_done, b + 1)
                for k in range(KD):
                    mm = pe.transpose(bank[s][:, k * P:k * P + LEN], nslot[s][:, k * P:(k + 1) * P],
                                      ident[0:LEN, 0:LEN])
                mm.then_inc(t_done, 1)

            def project_narrow(b, s):
                pe.wait_ge(nt_done, b + 1 + RING)
                pe.wait_ge(bc_ev, b + 1)
                for k in range(KD):
                    mm = pe.matmul(bank[2][:, 0:LEN], w_in[:, k, C_BC:C_DT], nt[s][:, k, :],
                                   start=(k == 0), stop=(k == KD - 1))
                mm.then_inc(bc_mm, 1)
                pe.wait_ge(s_ev, b + 1)
                for k in range(KD):
                    mm = pe.matmul(bank[3][0:LEN, 256:256 + HEADS], nt[s][:, k, :], w_in[:, k, C_DT:PROJ],
                                   start=(k == 0), stop=(k == KD - 1))
                mm.then_inc(dt_mm, 1)
                if not late(b):
                    project_x(b, s)

            def project_x(b, s):
                pe.wait_ge(xs_ev, b + 1)
                for k in range(KD):
                    mm = pe.matmul(bank[4][0:LEN, :], nt[s][:, k, :], w_in[:, k, C_X:C_BC],
                                   start=(k == 0), stop=(k == KD - 1))
                mm.then_inc(xs_mm, 1)

            def project_z(b, s):
                pe.wait_ge(z_ev, b + 1)
                for k in range(KD):
                    mm = pe.matmul(bank[5][0:LEN, :], nt[s][:, k, :], w_in[:, k, C_Z:C_X],
                                   start=(k == 0), stop=(k == KD - 1))
                mm.then_inc(z_mm, 1)

            def project_rest(b, s):
                if not late(b):
                    project_z(b, s)
                pe.wait_ge(c_ev, b + 1)
                pe.wait_ge(dt_ev, b + 1)
                pe.matmul(bank[3][0:LEN, 0:LEN], bct[s][0:STATE, :], ct[s][:, :],
                          start=True, stop=True).then_inc(s_mm, 1)

            skewed(pe, [(0, project_narrow), (-1, turn_rows), (0, project_rest)])
            for b in range(BATCH - LATE, BATCH):
                project_x(b, b % RING)
                project_z(b, b % RING)

            pe.wait_ge(ld_ssm, 96)
            for s in (b_mm, y_mm, t4_mm, t2_mm, o_mm, l_mm):
                pe.sem_inc(s, RING)
            pe.wait_ge(s_ev, BATCH + 1)
            pe.wait_ge(dt_ev, BATCH)
            pe.wait_ge(xs_ev, BATCH + 1)
            pe.wait_ge(z_ev, BATCH + 1)
            pe.wait_ge(bc_ev, BATCH + 1)

            def spread_decays(b, s):
                pe.wait_ge(decs_done, b + 1)
                pe.wait_ge(scan_done, b + 1)
                for h in range(HEADS):
                    mm = pe.transpose(pair[0:LEN, h // HPB, h % HPB * LEN:(h % HPB + 1) * LEN],
                                      decs[s][:, h:h + 1].to_broadcast([LEN, LEN]), ident[0:LEN, 0:LEN])
                mm.then_inc(b_mm, 1)

            def turn_target(b, s):
                pe.wait_ge(tg_done, b + 1)
                pe.wait_ge(tt_done, b + 1)
                for k in range(KD):
                    mm = pe.transpose(bank[3][:, k * P:k * P + LEN], tslot[s][:, k * P:(k + 1) * P],
                                      ident[0:LEN, 0:LEN])
                mm.then_inc(t2_mm, 1)

            def mix(b, s):
                pe.wait_ge(g_done, b + 1)
                pe.wait_ge(prep_done, b + 1)
                pe.wait_ge(ya_done, b + 2)
                for h in range(HEADS):
                    mm = pe.matmul(bank[0][0:LEN, h * HEAD:(h + 1) * HEAD], gm[s][:, h * LEN:(h + 1) * LEN],
                                   dtx[s][:, h * HEAD:(h + 1) * HEAD], start=True, stop=True)
                mm.then_inc(y_mm, 1)

            def project_out(b, s):
                pe.wait_ge(yt_done, b + 1 + 1)
                pe.wait_ge(h1_done, b + 1)
                for k in range(KI):
                    mm = pe.matmul(bank[2][0:LEN, 0:DIM], yt[s][:, k, :], w_out[:, k, :],
                                   start=(k == 0), stop=(k == KI - 1))
                mm.then_inc(o_mm, 1)

            def logits(b, s):
                pe.wait_ge(tt_done, b + 1 + 1)
                pe.wait_ge(lg_done, b + 1)
                for k in range(KD):
                    mm = pe.matmul(bank[4][0:LEN, 0:EXPERTS], tt[s][:, k, :], wr[:, k, :],
                                   start=(k == 0), stop=(k == KD - 1))
                mm.then_inc(l_mm, 1)

            def turn_gated(b, s):
                pe.wait_ge(y2_done, b + 1)
                pe.wait_ge(yt_done, b + 1)
                for k in range(KI):
                    mm = pe.transpose(bank[1][:, k * P:k * P + LEN], yb[s][:, k * P:(k + 1) * P],
                                      ident[0:LEN, 0:LEN])
                mm.then_inc(t4_mm, 1)

            def ranks(b, s):
                if s == 0:
                    pe.wait_ge(route, b * (R_STEPS // 2) + R_PICKED)
                    pe.wait_ge(seen_done, b + 2)
                    order, ones = before[:, 0:LEN], before[:, LEN:2 * LEN]
                    dst = bank[5][0:LEN, 0:2 * EXPERTS]
                    both = dst.rearrange("p (b e) -> p b e", b=2)
                    pe.matmul(dst, order, picks[:, :], start=True, stop=False)
                    for half in range(2):
                        pe.matmul(both, ones, seen[:, half * EXPERTS:(half + 1) * EXPERTS].unsqueeze(1).to_broadcast(
                            [LEN, 2, EXPERTS]), start=False, stop=False)
                    pe.matmul(dst[:, EXPERTS:2 * EXPERTS], ones, picks[:, 0:EXPERTS], start=False, stop=True
                              ).then_inc(rank_mm, 2)

            skewed(pe, [(0, spread_decays), (2, turn_gated), (7, ranks), (1, mix), (4, turn_target),
                        (2, project_out), (4, logits)])

            pe.wait_ge(seen_done, BATCH + 2)
            for half in range(2):
                mm = pe.matmul(bank[5][0:LEN, P:P + EXPERTS], before[:, LEN:2 * LEN],
                               seen[:, half * EXPERTS:(half + 1) * EXPERTS], start=(half == 0), stop=(half == 1))
            mm.then_inc(count_mm, 1)

            for s, n in ((xc_mm, RING), (h_mm, HALVES * RING), (hc_mm, HALVES * RING), (yr_mm, Y_RING)):
                pe.sem_inc(s, n)
            pe.wait_ge(table_done, 1)
            pe.wait_ge(bias_in, 16)
            pe.wait_ge(mixed, 1)

            def turn_x(i, s):
                pe.wait_ge(x_in, i * 16 + 32)
                pe.wait_ge(xc_ev, i + 1)
                for k in range(KD):
                    mm = pe.transpose(bank[0][:, k * P:(k + 1) * P], xrow[s][:, k * P:(k + 1) * P], ident[:, :])
                mm.then_inc(xc_mm, 1)

            expert_of = [None, None]

            def look_up(product):
                def stage(i, s):
                    expert_of[product] = pe.value_load(tile_slot[0:1, bass.ds(i, 1)], min_val=0, max_val=EXPERTS - 1)
                return stage

            def first_product(half):
                def stage(i, s):
                    if half == 0:
                        pe.wait_ge(xc_ev, i + 2)
                        if isinstance(i, int) and i < EXPERTS:
                            pe.wait_ge(w_ld[i], 16)
                    pe.wait_ge(h_ev, i * HALVES + (half + 1))
                    e = expert_of[0]
                    dst = bank[1 + half][:, :]
                    for k in range(KD):
                        at = k * HIDDEN + half * HH
                        mm = pe.matmul(dst, xcol[s][:, k, :], w_all[:, bass.ds(e, 1), at:at + HH],
                                       start=(k == 0), stop=(k == KD - 1))
                    mm.then_inc(h_mm, 1)
                return stage

            def turn_hidden(half):
                def stage(i, s):
                    pe.wait_ge(h_ev, i * HALVES + (half + 1 + HALVES))
                    pe.wait_ge(hc_ev, i * HALVES + (half + 1))
                    for k in range(KH):
                        at = (half * KH + k) * P
                        mm = pe.transpose(bank[3 + half][:, k * P:(k + 1) * P], hrow[s][:, at:at + P], ident[:, :])
                    mm.then_inc(hc_mm, 1)
                return stage

            def second_product(i, s):
                pe.wait_ge(hc_ev, i * HALVES + 2 * HALVES)
                pe.wait_ge(yr_ev, i + 1)
                e = expert_of[1]
                dst = bank[5][:, 0:DIM]
                pe.matmul(dst, ones3[:, :], bias3[:, bass.ds(e, 1), :], start=True, stop=False)
                for k in range(KF):
                    at = KD * HIDDEN + k * DIM
                    mm = pe.matmul(dst, hcol[s][:, k, :], w_all[:, bass.ds(e, 1), at:at + DIM],
                                   start=False, stop=(k == KF - 1))
                mm.then_inc(yr_mm, 1)

            skewed(pe, [(0, look_up(0)), (1, look_up(1)), (1, turn_hidden(0)), (0, first_product(0)),
                        (1, turn_hidden(1)), (-1, turn_x), (0, first_product(1)), (1, second_product)],
                   TILES, peel=EXPERTS)

        @block.scalar
        def _(act):
            act.dma_start(posb[:, :], d["pos"]).then_inc(ld_h, 16)
            act.dma_start(tokb[:, :], d["tok_b"].partition_broadcast(IMG)).then_inc(ld_h, 16)
            act.dma_start(bout[:, :], d["b_out"].partition_broadcast(LEN)).then_inc(ld_row, 16)
            act.dma_start(rows8[:, :], d["rows8"].partition_broadcast(LEN)).then_inc(ld_row, 16)
            act.dma_start(bx[:, :], d["b_x"].partition_broadcast(LEN)).then_inc(ld_row, 16)
            act.dma_start(bz[:, :], d["b_z"].partition_broadcast(LEN)).then_inc(ld_row, 16)
            act.dma_start(rowmask[:, :], d["rowmask"]).then_inc(ld_row, 16)
            act.dma_start(fgam[:, :], d["f_gam"].partition_broadcast(LEN)).then_inc(ld_row, 16)
            act.dma_start(fbet[:, :], d["f_bet"].partition_broadcast(LEN)).then_inc(ld_row, 16)
            act.dma_start(bsrc[:, :], d["b2"]).then_inc(ld_bias, 16)

            def load_expert(e):
                act.dma_start(w_all[:, EXPERTS - 1 - e, :], d["experts"][e]).then_inc(w_ld[e], 16)

            for q in range(2 * KD):
                e, half = q // 2, q % 2
                act.wait_ge(emb_mm, q + 1)
                act.activation(emb_t[:, e, half * HALF:(half + 1) * HALF], bank[q][:, 0:HALF],
                               ACT.Copy).then_inc(emb_sb, 1)
            act.wait_ge(ld_row, 112)
            act.activation(exp_a[:, :], rows8[:, 2 * HEADS:3 * HEADS], ACT.Exp).then_inc(expa_done, 1)

            act.sem_inc(nt_done, RING)
            for s in (bc_ev, s_ev):
                act.sem_inc(s, 1)
            act.wait_ge(ld_proj, 64)

            def norm_t(b, s):
                act.wait_ge(t_done, b + 1 + RING)
                act.wait_ge(s_mm, b + 1)
                for k in range(KD):
                    i = act.activation(nt[s][:, k, :], bank[s][:, k * P:k * P + LEN], ACT.Identity,
                                       bias=bet_t[:, k:k + 1], scale=gam_t[:, k:k + 1])
                i.then_inc(nt_done, 1)

            def keep_bc(b, s):
                act.wait_ge(bc_mm, b + 1)
                act.wait_ge(s_mm, b + 1)
                act.activation(bct[s][:, :], bank[2][:, 0:LEN], ACT.Identity, bias=b_bc[:, 0:1]).then_inc(bc_ev, 1)
                act.wait_ge(bc_ev, b + 1 + 1)
                act.activation(ct[s][:, :], bct[s][STATE:P, :], ACT.Copy).then_inc(c_ev, 1)

            def keep_scores(b, s):
                act.wait_ge(s_mm, b + 1 + RING)
                settle(act)
                act.activation(s_all[:, bass.ds(b * LEN, LEN)], bank[3][0:LEN, 0:LEN], ACT.Copy).then_inc(s_ev, 1)

            def gate_values(b, s):
                if s == 0 and not late(b):
                    silu(b)

            def silu(b):
                act.wait_ge(z_ev, b + 1 + 2)
                settle(act)
                z = sz_all[:, bass.ds(b * INNER, 2 * INNER)]
                act.activation(z, z, ACT.Silu).then_inc(sz_done, 1)

            skewed(act, [(0, keep_bc), (-1, norm_t), (2, gate_values), (0, keep_scores)])

            act.wait_ge(dm, 1)
            act.activation(t128[2][:, :], t128[0][:, :], ACT.Exp).then_inc(em, 1)
            act.wait_ge(dm, DM)
            act.activation(dec_all[:, :], t128[3][:, :], ACT.Exp, bias=rowmask[:, 0:1], scale=-1.0).then_inc(dec_done, 1)

            load_expert(0)
            for s in (tt_done, yt_done):
                act.sem_inc(s, 1)
            act.sem_inc(tc_done, RING)

            def keep_target(b, s):
                act.wait_ge(tg_done, b + 1)
                settle(act)
                act.activation(hn_all[:, cols(b)], tslot[s][:, :], ACT.Copy).then_inc(tc_done, 1)
                act.wait_ge(t2_mm, b + 1 + RING)
                act.wait_ge(l_mm, b + 1)
                act.activation(tt[s][:, :, :], bank[3][:, 0:KD * P].rearrange("p (k c) -> p k c", k=KD)[:, :, 0:LEN],
                               ACT.Copy).then_inc(tt_done, 1)

            def gated_t(b, s):
                act.wait_ge(t4_mm, b + 1 + RING)
                act.wait_ge(o_mm, b + 1)
                act.activation(yt[s][:, :, :], bank[1][:, :].rearrange("p (k c) -> p k c", k=KI)[:, :, 0:LEN],
                               ACT.Copy).then_inc(yt_done, 1)

            def slot_decays(b, s):
                act.wait_ge(b_mm, b + 1)
                settle(act)
                act.activation(decs[s][:, :], dec_all[:, cols(b, HEADS)], ACT.Copy).then_inc(decs_done, 1)

            def skip_values(b, s):
                act.wait_ge(ya_done, b + 1)
                settle(act)
                for h in range(HEADS):
                    i = act.activation(xsd[s][:, h * HEAD:(h + 1) * HEAD], xs_all[:, bass.ds(b * INNER + h * HEAD, HEAD)],
                                       ACT.Copy, scale=rows8[:, 3 * HEADS + h:3 * HEADS + h + 1])
                i.then_inc(xsd_done, 1)

            act.wait_ge(dec_done, 1)
            act.wait_ge(s_mm, BATCH + RING)
            act.wait_ge(z_mm, BATCH)
            act.wait_ge(xs_ev, BATCH + 1)

            def late_gates(b, s):
                if isinstance(b, int) and b == 0:
                    silu(BATCH - LATE)

            skewed(act, [(2, gated_t), (-1, slot_decays), (4, keep_target), (0, skip_values), (0, late_gates)])

            act.wait_ge(apart, BATCH)
            act.activation(t16[1][:, :], t16[0][:, :], ACT.Exp).then_inc(ratio_done, 1)

            act.wait_ge(l_mm, BATCH + RING)
            act.wait_ge(lg_done, BATCH + 1)
            act.wait_ge(y2_done, BATCH)
            act.wait_ge(pow_done, BATCH)
            for e in range(1, W_FIRST):
                load_expert(e)

            def load_next(i, s):
                if isinstance(i, int) and i + W_FIRST < EXPERTS:
                    load_expert(i + W_FIRST)

            act.sem_inc(h_ev, HALVES)

            def keep_hidden(half):
                def stage(i, s):
                    act.wait_ge(h_mm, i * HALVES + (half + 1 + HALVES * RING))
                    act.wait_ge(hc_mm, i * HALVES + HALVES)
                    act.activation(hrow[s][:, half * HH:(half + 1) * HH], bank[1 + half][:, :],
                                   ACT.Copy).then_inc(h_ev, 1)
                return stage

            skewed(act, [(0, keep_hidden(0)), (0, keep_hidden(1)), (0, load_next)], TILES, peel=EXPERTS - W_FIRST)

            shift = t16[0]
            for b in range(BATCH):
                if b % PER == 0:
                    act.wait_ge(tail_shift, b // PER + 1)
                at = slice(b * DIM, (b + 1) * DIM)
                act.activation(u_end[:, at], u_end[:, at], ACT.Identity, bias=shift[:, b:b + 1],
                               scale=rstd[:, b:b + 1]).then_inc(tail_norm, 1)

        @block.vector
        def _(dve):
            dve.wait_ge(ld_bias, 16)
            for i, rest in enumerate((bsrc, *bres)):
                dve.tensor_copy(bpart[i][:, :], rest[:, :]).then_inc(bias_step, 1)
                if i < 2:
                    dve.wait_ge(bias_step, 2 * i + 1)
                    dve.tensor_tensor(bres[i][:, :], rest[:, :], bpart[i][:, :], ALU.subtract).then_inc(bias_step, 1)
                    dve.wait_ge(bias_step, 2 * i + 2)

            dve.memset(mhalf[:, :], -0.5).then_inc(ln, 1)
            dve.memset(zeros[:, :], 0.0).then_inc(zero_set, 1)
            dve.memset(ones3[:, :], 1.0)
            dve.wait_ge(ld_h, 48)
            dve.tensor_tensor(posb[:, :], posb[:, :], tokb[:, :], ALU.add).then_inc(ln, 1)
            dve.wait_ge(ln, 2)
            for g in range(BATCH // 2):
                dve.wait_ge(img_t, g + 1)
                dve.tensor_tensor(h_all[0:IMG, 2 * g * DIM:(2 * g + 2) * DIM].rearrange("p (b c) -> p b c", b=2),
                                  bank[4 + g % 4][0:IMG, :].rearrange("p (b c) -> p b c", b=2),
                                  posb[:, :].unsqueeze(1).to_broadcast([IMG, 2, DIM]),
                                  ALU.add).then_inc(img_rows, 1)
            dve.wait_ge(img_rows, BATCH // 2)

            dve.wait_ge(ld_row, 112)
            dve.tensor_tensor(bdt[:, :], rows8[:, 0:HEADS], rows8[:, HEADS:2 * HEADS], ALU.add).then_inc(bdt_done, 1)
            dve.wait_ge(bdt_done, 1)
            for s in (xs_ev, z_ev):
                dve.sem_inc(s, 1)

            def moments(j, rows, b, s):
                settle(dve)
                dve.bn_stats(nst[j][s][:, :], rows[:, cols(b)]).then_inc(nst_done[j], 1)
                dve.wait_ge(nst_done[j], b + 1)
                settle(dve)
                dve.bn_aggr(nmv[j][s][:, :], nst[j][s][:, :]).then_inc(nag_done[j], 1)
                dve.wait_ge(nag_done[j], b + 1)
                dve.tensor_scalar(nve[j][s][:, :], nmv[j][s][:, 1:2], EPS, None, ALU.add).then_inc(nve_done[j], 1)

            def first_moments(b, s):
                moments(0, h_all, b, s)

            def first_norm(b, s):
                dve.wait_ge(npow_done[0], b + 1)
                dve.tensor_scalar(hn_all[:, cols(b)], h_all[:, cols(b)], nmv[0][s][:, 0:1], nrs[0][s][:, :],
                                  ALU.subtract, ALU.mult).then_inc(n1_done, 1)
                dve.wait_ge(n1_done, b + 1)
                moments(1, hn_all, b, s)

            def second_norm(b, s):
                dve.wait_ge(npow_done[1], b + 1)
                dve.wait_ge(t_done, b + 1)
                dve.tensor_scalar(nslot[s][:, :], hn_all[:, cols(b)], nmv[1][s][:, 0:1], nrs[1][s][:, :],
                                  ALU.subtract, ALU.mult).then_inc(ns_done, 1)

            def add_dt_bias(b, s):
                dve.wait_ge(dt_mm, b + 1)
                dve.tensor_tensor(dt_all[:, cols(b, HEADS)], bank[3][0:LEN, 256:256 + HEADS], bdt[:, :],
                                  ALU.add).then_inc(dt_ev, 1)

            def add_x_bias(b, s):
                if not late(b):
                    keep_x(b)

            def add_z_bias(b, s):
                if not late(b):
                    keep_z(b)

            def keep_x(b):
                if isinstance(b, int) and b == 0:
                    dve.wait_ge(bias_out, 48)
                dve.wait_ge(xs_mm, b + 1)
                dve.tensor_tensor(xs_all[:, cols(b, INNER)], bank[4][0:LEN, :], bx[:, :], ALU.add).then_inc(xs_ev, 1)

            def keep_z(b):
                dve.wait_ge(z_mm, b + 1)
                dve.tensor_tensor(sz_all[:, cols(b, INNER)], bank[5][0:LEN, :], bz[:, :], ALU.add).then_inc(z_ev, 1)

            skewed(dve, [(-2, second_norm), (0, add_dt_bias), (-4, first_moments), (0, add_x_bias),
                         (-3, first_norm), (0, add_z_bias)], peel=1)

            count = [0]

            def step(i):
                count[0] += 1
                i.then_inc(dm, 1)
                dve.wait_ge(dm, count[0])

            x, neg, e_, q, q2 = dt_all, t128[0], t128[2], t128[4], t128[5]
            dve.wait_ge(dt_ev, BATCH)
            step(dve.scalar_tensor_tensor(neg[:, :], x[:, :], -1.0, x[:, :], ALU.mult, ALU.min))
            step(dve.tensor_scalar(t128[1][:, :], x[:, :], 0.0, None, ALU.max))
            keep_x(BATCH - 2)
            dve.wait_ge(em, 1)
            step(dve.tensor_scalar(t128[3][:, :], e_[:, :], 2.0, None, ALU.add))
            step(dve.reciprocal(neg[:, :], t128[3][:, :]))
            step(dve.tensor_tensor(q[:, :], e_[:, :], neg[:, :], ALU.mult))
            step(dve.tensor_tensor(q2[:, :], q[:, :], q[:, :], ALU.mult))
            step(dve.tensor_scalar(t128[3][:, :], q2[:, :], 1.0 / 17, None, ALU.mult))
            for odd in range(15, 1, -2):
                step(dve.scalar_tensor_tensor(t128[3][:, :], t128[3][:, :], 1.0 / odd, q2[:, :], ALU.add, ALU.mult))
                if odd == 15:
                    keep_z(BATCH - 2)
            step(dve.scalar_tensor_tensor(t128[3][:, :], t128[3][:, :], 1.0, q[:, :], ALU.add, ALU.mult))
            step(dve.scalar_tensor_tensor(dt_all[:, :], t128[3][:, :], 2.0, t128[1][:, :], ALU.mult, ALU.add))
            dve.wait_ge(expa_done, 1)
            step(dve.tensor_tensor(t128[3][:, :].rearrange("p (b h) -> p b h", h=HEADS),
                                   dt_all[:, :].rearrange("p (b h) -> p b h", h=HEADS),
                                   exp_a[:, :].unsqueeze(1).to_broadcast([LEN, BATCH, HEADS]), ALU.mult))
            assert count[0] == DM
            keep_x(BATCH - 1)
            keep_z(BATCH - 1)

            dve.wait_ge(ld_ssm, 96)
            for s in (scan_done, h1_done, lg_done):
                dve.sem_inc(s, 1)
            dve.sem_inc(ya_done, RING)
            dve.wait_ge(s_ev, BATCH + 1)
            dve.wait_ge(res_done, BATCH)

            def scan(b, s):
                dve.wait_ge(b_mm, b + 1 + RING)
                dve.wait_ge(y_mm, b + 1)
                for h in range(HEADS // HPB):
                    at = slice(h * HPB * LEN, (h + 1) * HPB * LEN)
                    i = dve.tensor_tensor_scan(gm[s][:, at], pair[0:LEN, h, 0:HPB * LEN], delta[:, :], 0.0,
                                               ALU.mult, ALU.add)
                i.then_inc(scan_done, 1)

            def add_skip(b, s):
                dve.wait_ge(y_mm, b + 1 + RING)
                dve.wait_ge(xsd_done, b + 1)
                dve.wait_ge(t4_mm, b + 1)
                dve.tensor_tensor(yb[s][:, :], bank[0][0:LEN, :], xsd[s][:, :], ALU.add).then_inc(ya_done, 1)

            def weigh(b, s):
                dve.wait_ge(scan_done, b + 1 + 1)
                g3 = gm[s][:, :].rearrange("p (h t) -> p h t", h=HEADS)
                dve.tensor_tensor(g3, g3, s_all[:, bass.ds(b * LEN, LEN)].unsqueeze(1).to_broadcast([LEN, HEADS, LEN]),
                                  ALU.mult).then_inc(g_done, 1)

            def add_residual(b, s):
                dve.wait_ge(o_mm, b + 1 + RING)
                dve.tensor_tensor(h_all[:, cols(b)], bank[2][0:LEN, 0:DIM], h_all[:, cols(b)],
                                  ALU.add).then_inc(h1_done, 1)
                dve.wait_ge(h1_done, b + 1 + 1)
                settle(dve)
                dve.bn_stats(est[s][:, :], h_all[:, cols(b)]).then_inc(st_done, 1)
                dve.wait_ge(st_done, b + 1)
                settle(dve)
                dve.bn_aggr(emv[s][:, :], est[s][:, :]).then_inc(ag_done, 1)
                dve.wait_ge(ag_done, b + 1)
                dve.tensor_scalar(eve[s][:, :], emv[s][:, 1:2], EPS, None, ALU.add).then_inc(ve_done, 1)

            def add_router_bias(b, s):
                dve.wait_ge(l_mm, b + 1 + RING)
                dve.tensor_tensor(pair_logits[:, s * EXPERTS:(s + 1) * EXPERTS], bank[4][0:LEN, 0:EXPERTS],
                                  rows8[:, 4 * HEADS:5 * HEADS], ALU.add).then_inc(lg_done, 1)

            def norm_target(b, s):
                dve.wait_ge(pow_done, b + 1)
                dve.wait_ge(t2_mm, b + 1)
                dve.wait_ge(tc_done, b + 1)
                dve.tensor_scalar(tslot[s][:, :], h_all[:, cols(b)], emv[s][:, 0:1], ers[s][:, :],
                                  ALU.subtract, ALU.mult).then_inc(tg_done, 1)

            def routing(f):
                def stage(b, s):
                    if s == 0:
                        f(b)
                return stage

            def after(b, steps):
                dve.wait_ge(route, b * (R_STEPS // 2) + steps)

            def of_pair(t):
                return t[:, :].rearrange("p (b k e) -> p b k e", b=2, k=TOP)

            def of_choice(t):
                return t[:, :].rearrange("p (c e) -> p c e", e=EXPERTS)

            def of_expert(t):
                return t[:, :].rearrange("p (b e) -> p b e", e=EXPERTS)

            def find_largest(b):
                dve.wait_ge(lg_done, b + 2 + 1)
                settle(dve)
                for i in range(2):
                    at = slice(i * EXPERTS, (i + 1) * EXPERTS)
                    dve.max(mx8[:, at], pair_logits[:, at]).then_inc(route, 1)

            def find_experts(b):
                after(b, 2)
                settle(dve)
                for i in range(2):
                    at = slice(i * EXPERTS, (i + 1) * EXPERTS)
                    dve.max_index(ix8[:, at], mx8[:, at], pair_logits[:, at]).then_inc(route, 1)
                dve.tensor_tensor(t16[0][:, bass.ds(b, 2)], mx8[:, 1:16:8], mx8[:, 0:16:8], ALU.subtract
                                  ).then_inc(apart, 2)

            def convert_experts(b):
                after(b, 4)
                settle(dve)
                dve.tensor_copy(ixf[:, :].rearrange("p (b k) -> p b k", b=2),
                                ix8[:, :].rearrange("p (b k) -> p b k", b=2)[:, :, 0:TOP]).then_inc(route, 1)

            def mark_experts(b):
                after(b, 5)
                dve.tensor_tensor(of_choice(mask), of_choice(iota8),
                                  ixf[:, :].unsqueeze(2).to_broadcast([LEN, 2 * TOP, EXPERTS]), ALU.is_equal
                                  ).then_inc(route, 1)

            def pick_experts(b):
                after(b, 6)
                m = of_pair(mask)
                dve.tensor_tensor(of_expert(picks), m[:, :, 0, :], m[:, :, 1, :], ALU.add).then_inc(route, 1)

            def add_region(b):
                dve.wait_ge(rank_mm, b + 2)
                dve.tensor_tensor(of_expert(rank), bank[5][0:LEN, 0:2 * EXPERTS].rearrange("p (b e) -> p b e", b=2),
                                  small[:, REGION - 1 + TILES:].unsqueeze(1).to_broadcast([LEN, 2, EXPERTS]),
                                  ALU.add).then_inc(route, 1)

            def choose_places(b):
                after(b, R_PICKED + 1)
                dve.tensor_tensor(of_pair(ranked), of_pair(mask),
                                  of_expert(rank).unsqueeze(2).to_broadcast([LEN, 2, TOP, EXPERTS]), ALU.mult
                                  ).then_inc(route, 1)
                dve.tensor_tensor(seen[:, :], seen[:, :], picks[:, :], ALU.add).then_inc(seen_done, 2)

            def sum_places(b):
                after(b, R_PICKED + 2)
                dve.tensor_reduce(placef[:, :], of_choice(ranked), AXIS_X, ALU.add).then_inc(route, 1)

            def keep_places(b):
                after(b, R_PICKED + 3)
                settle(dve)
                dve.tensor_copy(place_of[:, bass.ds(b * TOP, 2 * TOP)], placef[:, :]).then_inc(place_done, 2)

            dve.memset(seen[:, :], 0.0).then_inc(seen_done, 2)
            skewed(dve, [(5, add_router_bias), (6, routing(find_largest)), (3, add_residual), (6, routing(find_experts)),
                         (0, scan), (6, routing(convert_experts)), (7, routing(add_region)),
                         (1, add_skip), (6, routing(mark_experts)), (7, routing(choose_places)),
                         (3, norm_target), (6, routing(pick_experts)), (7, routing(sum_places)),
                         (0, weigh), (7, routing(keep_places))])

            steps = [0]

            def step(i):
                steps[0] += 1
                i.then_inc(table_step, 1)
                dve.wait_ge(table_step, steps[0])

            count8, more8, tiles8, end8, free8 = r8
            dve.wait_ge(count_mm, 1)
            step(dve.tensor_copy(count8[:, :], bank[5][0:LEN, P:P + EXPERTS]))
            g = grid[:, 0:EXPERTS * (REGION - 1)].rearrange("p (e k) -> p e k", e=EXPERTS)
            step(dve.tensor_tensor(g, count8[:, :].unsqueeze(2).to_broadcast([LEN, EXPERTS, REGION - 1]),
                                   small[:, 0:REGION - 1].unsqueeze(1).to_broadcast([LEN, EXPERTS, REGION - 1]),
                                   ALU.is_gt))
            step(dve.tensor_reduce(more8[:, :], g, AXIS_X, ALU.add))
            step(dve.tensor_scalar(tiles8[:, :], more8[:, :], 1.0, None, ALU.add))
            step(dve.tensor_tensor_scan(end8[:, :], tiles8[:, :], zeros[0:LEN, 0:EXPERTS], 0.0, ALU.add, ALU.add))
            step(dve.tensor_scalar(free8[:, :], tiles8[:, :], -1.0, float(REGION), ALU.mult, ALU.add))
            passed, behind, where = row_f
            numbers = small[:, REGION - 1:REGION - 1 + TILES]
            g = grid[:, :].rearrange("p (t e) -> p t e", e=EXPERTS)
            step(dve.tensor_tensor(g, numbers.unsqueeze(2).to_broadcast([LEN, TILES, EXPERTS]),
                                   end8[:, :].unsqueeze(1).to_broadcast([LEN, TILES, EXPERTS]), ALU.is_ge))
            step(dve.tensor_reduce(passed[:, :], g, AXIS_X, ALU.add))
            step(dve.tensor_tensor(g, g, free8[:, :].unsqueeze(1).to_broadcast([LEN, TILES, EXPERTS]), ALU.mult))
            step(dve.tensor_reduce(behind[:, :], g, AXIS_X, ALU.add))
            step(dve.tensor_tensor(where[:, :], behind[:, :], numbers, ALU.add))
            step(dve.tensor_scalar(where[:, :], where[:, :], float(EXPERTS * REGION), None, ALU.min))
            step(dve.tensor_copy(tile_at[:, :], where[:, :]))
            step(dve.tensor_scalar(passed[:, :], passed[:, :], -1.0, EXPERTS - 1.0, ALU.mult, ALU.add))
            step(dve.tensor_scalar(passed[:, :], passed[:, :], 0.0, None, ALU.max))
            dve.tensor_copy(tile_slot[:, :], passed[:, :]).then_inc(table_done, 1)

            dve.wait_ge(ratio_done, 1)
            w1, w2 = t16[3], t16[2]
            step(dve.tensor_scalar(w2[:, :], t16[1][:, :], 1.0, None, ALU.add))
            step(dve.reciprocal(w1[:, :], w2[:, :]))
            step(dve.tensor_tensor(w2[:, :], t16[1][:, :], w1[:, :], ALU.mult))

            tokens = BATCH * TOP
            place_f, shift_f = t128[0][:, 0:tokens], t128[1][:, 0:tokens]
            dve.wait_ge(place_done, BATCH)
            step(dve.tensor_copy(place_f, place_of[:, :]))
            g = grid[:, 0:tokens * (EXPERTS - 1)].rearrange("p (t e) -> p t e", e=EXPERTS - 1)
            starts = small[:, REGION + TILES:]
            step(dve.tensor_tensor(g, place_f.unsqueeze(2).to_broadcast([LEN, tokens, EXPERTS - 1]),
                                   starts.unsqueeze(1).to_broadcast([LEN, tokens, EXPERTS - 1]), ALU.is_ge))
            step(dve.tensor_tensor(g, g, free8[:, 0:EXPERTS - 1].unsqueeze(1).to_broadcast([LEN, tokens, EXPERTS - 1]),
                                   ALU.mult))
            step(dve.tensor_reduce(shift_f, g, AXIS_X, ALU.add))
            step(dve.scalar_tensor_tensor(place_f, shift_f, -float(P), place_f, ALU.mult, ALU.add))
            step(dve.tensor_copy(listed_at[:, :], place_f))
            step(dve.tensor_scalar(in_tile[:, :], listed_at[:, :], P - 1, None, ALU.bitwise_and))
            step(dve.tensor_scalar(tile_no[:, :], listed_at[:, :], P.bit_length() - 1, None, ALU.logical_shift_right))
            step(dve.tensor_copy(place_f, in_tile[:, :]))
            step(dve.tensor_copy(shift_f, tile_no[:, :]))
            step(dve.scalar_tensor_tensor(place_f, place_f, float(TILES), shift_f, ALU.mult, ALU.add))
            dve.tensor_copy(listed_at[:, :], place_f).then_inc(listed, 1)

            for s, n in ((xc_ev, 1), (hc_ev, HALVES), (yr_ev, 1)):
                dve.sem_inc(s, n)
            dve.wait_ge(mixed, 1)

            def columns_x(i, s):
                dve.wait_ge(xc_mm, i + (1 + RING))
                dve.wait_ge(h_mm, i * HALVES + HALVES)
                dve.tensor_copy(xcol[s % RING][:, :, :], bank[0][:, 0:DIM].rearrange("p (k c) -> p k c", k=KD)
                                ).then_inc(xc_ev, 1)

            def columns_hidden(half):
                def stage(i, s):
                    dve.wait_ge(hc_mm, i * HALVES + (half + 1 + HALVES * RING))
                    dve.wait_ge(yr_mm, i + 1 + (Y_RING - RING))
                    if half == 0:
                        dve.wait_ge(b1_in, i * 16 + 32)
                    for k in range(KH):
                        at = half * KH + k
                        op = dve.tensor_scalar(hcol[s % RING][:, at, :], bank[3 + half][:, k * P:(k + 1) * P],
                                               b1col[s][:, at:at + 1], 0.0, ALU.add, ALU.max)
                    op.then_inc(hc_ev, 1)
                return stage

            def results(i, s):
                dve.wait_ge(yr_mm, i + (1 + Y_RING))
                dve.wait_ge(y_free, i + 1)
                dve.tensor_copy(yrow[s][:, :], bank[5][:, 0:DIM]).then_inc(yr_ev, 1)

            skewed(dve, [(1, columns_hidden(0)), (1, columns_hidden(1)), (-1, columns_x), (1, results)], TILES,
                   ring=Y_RING)

            shift = t16[0]
            at_tail = [0]
            dve.wait_ge(hb_done, 1)

            def tail_step(i):
                at_tail[0] += 1
                i.then_inc(tail, 1)

            def weigh_results(c):
                batches = range(c * PER, (c + 1) * PER)
                dve.wait_ge(back_in[c], 16 * TOP)
                for i, w in enumerate((w1, w2)):
                    for b in batches:
                        at = slice(b * DIM, (b + 1) * DIM)
                        tail_step(dve.scalar_tensor_tensor(u_end[:, at], back[i][:, at], w[:, b:b + 1], u_end[:, at],
                                                           ALU.mult, ALU.add))
                    dve.wait_ge(tail, at_tail[0])
                for b in batches:
                    tail_step(dve.bn_stats(stats[:, 6 * b:6 * b + 6], u_end[:, b * DIM:(b + 1) * DIM]))
                dve.wait_ge(tail, at_tail[0])
                for b in batches:
                    tail_step(dve.bn_aggr(mv[:, 2 * b:2 * b + 2], stats[:, 6 * b:6 * b + 6]))
                dve.wait_ge(tail, at_tail[0])
                dve.tensor_scalar(ve[:, c * PER:(c + 1) * PER], mv[:, 2 * c * PER + 1:2 * (c + 1) * PER:2], EPS, None,
                                  ALU.add).then_inc(tail_ve, 1)

            def shift_mean(c):
                dve.wait_ge(tail_pow, c + 1)
                at = slice(c * PER, (c + 1) * PER)
                dve.scalar_tensor_tensor(shift[:, at], mv[:, 2 * c * PER:2 * (c + 1) * PER:2], -1.0, rstd[:, at],
                                         ALU.mult, ALU.mult).then_inc(tail_shift, 1)

            for n in range(CHUNKS + 1):
                if n < CHUNKS:
                    weigh_results(n)
                if n > 0:
                    shift_mean(n - 1)
            finish(dve, CHUNKS - 1)

        @block.gpsimd
        def _(pool):
            pool.wait_ge(ln, 1)
            pool.wait_ge(ld_row, 112)

            def first_root(b, s):
                pool.wait_ge(nve_done[0], b + 1)
                pool.tensor_tensor(nrs[0][s][:, :], nve[0][s][:, :], mhalf[:, 0:1], ALU.pow).then_inc(npow_done[0], 1)

            def second_root(b, s):
                pool.wait_ge(nve_done[1], b + 1)
                pool.tensor_tensor(nrs[1][s][:, :], nve[1][s][:, :], mhalf[:, 0:1], ALU.pow).then_inc(npow_done[1], 1)

            def residual(b, s):
                h = h_all[:, cols(b)]
                pool.wait_ge(n1_done, b + 1)
                settle(pool)
                pool.tensor_tensor(h, h, hn_all[:, cols(b)], ALU.add).then_inc(res_sum, 1)
                pool.wait_ge(res_sum, b + 1)
                settle(pool)
                pool.tensor_tensor(h, h, bout[:, :], ALU.add).then_inc(res_done, 1)

            skewed(pool, [(-4, first_root), (-3, second_root), (-3, residual)])

            pool.wait_ge(dec_done, 1)
            pool.wait_ge(s_mm, BATCH + RING)
            pool.wait_ge(z_mm, BATCH)
            pool.wait_ge(sz_done, (BATCH - LATE) // 2)
            pool.wait_ge(xs_ev, BATCH + 1)

            def by_head(t):
                return t.rearrange("p (h c) -> p h c", h=HEADS)

            def prepare(b, s):
                pool.wait_ge(y_mm, b + 1)
                settle(pool)
                pool.tensor_tensor(by_head(dtx[s][:, :]), by_head(xs_all[:, cols(b, INNER)]),
                                   dt_all[:, cols(b, HEADS)].unsqueeze(2).to_broadcast([LEN, HEADS, HEAD]),
                                   ALU.mult).then_inc(prep_done, 1)

            def gate(b, s):
                if late(b):
                    pool.wait_ge(sz_done, BATCH // 2)
                pool.wait_ge(ya_done, b + 1 + RING)
                settle(pool)
                pool.tensor_tensor(yb[s][:, :], yb[s][:, :], sz_all[:, cols(b, INNER)], ALU.mult).then_inc(y2_done, 1)

            def inverse_root(b, s):
                pool.wait_ge(ve_done, b + 1)
                pool.tensor_tensor(ers[s][:, :], eve[s][:, :], mhalf[:, 0:1], ALU.pow).then_inc(pow_done, 1)

            def send_rows(b, s):
                pool.wait_ge(tc_done, b + 1 + RING)
                pool.wait_ge(place_done, b + 2 - b % 2)
                for i in range(TOP):
                    at = b * TOP + i
                    pool.indirect_dma_start(xg[:, :], bass.IndirectOffsetOnAxis(place_of[:, at:at + 1], 0),
                                            hn_all[:, b * DIM:(b + 1) * DIM], None).then_inc(placed, 16)

            pool.wait_ge(zero_out, 16)
            skewed(pool, [(0, prepare), (8, send_rows), (3, inverse_root), (1, gate)], peel=BATCH)

            pool.wait_ge(l_mm, BATCH + RING)
            pool.wait_ge(lg_done, BATCH + 1)
            pool.wait_ge(tt_done, BATCH + 1)
            pool.wait_ge(y2_done, BATCH)
            pool.wait_ge(pow_done, BATCH)
            pool.drain().then_inc(mixed, 1)

            pool.sem_inc(y_free, Y_RING)
            pool.wait_ge(ld_goals, 16)
            pool.wait_ge(unlisted, 16)
            pool.wait_ge(listed, 1)
            for j in range(BATCH * TOP):
                pool.indirect_dma_start(goal_list, bass.IndirectOffsetOnAxis(listed_at[:, j:j + 1], 0),
                                        goals[:, j // TOP + j % TOP * BATCH:j // TOP + j % TOP * BATCH + 1], None
                                        ).then_inc(goals_out, 16)
            pool.wait_ge(goals_out, 16 * BATCH * TOP)
            pool.dma_start(goal_of[:, :], goal_list.rearrange("(p t) o -> p (t o)", p=P)).then_inc(goals_in, 16)

            pool.wait_ge(goals_in, 16)
            for i in range(TILES):
                if i > 0:
                    pool.wait_ge(y_out, 16 * i)
                    pool.sem_inc(y_free, 1)
                pool.wait_ge(yr_ev, i + 2)
                pool.indirect_dma_start(yg, bass.IndirectOffsetOnAxis(goal_of[:, i:i + 1], 0),
                                        yrow[i % Y_RING][:, :], None).then_inc(y_out, 16)
                if i == 2 * REGION:
                    pool.wait_ge(yr_mm, i + 1 + Y_RING)
                    pool.wait_ge(kept, 32 * BATCH)
                    pool.dma_start(u_end[:, :], u_dram).then_inc(ends_in, 16)
                    pool.dma_start(h_end[:, :], h_dram).then_inc(ends_in, 16)
                    pool.wait_ge(ends_in, 32)
                    h3 = h_end[:, :].rearrange("p (b c) -> p b c", b=BATCH)
                    pool.tensor_tensor(h3, h3, fbet[:, :].unsqueeze(1).to_broadcast([LEN, BATCH, DIM]),
                                       ALU.add).then_inc(hb_done, 1)

            def deviation(c):
                at = slice(c * PER, (c + 1) * PER)
                pool.wait_ge(tail_ve, c + 1)
                pool.tensor_tensor(rstd[:, at], ve[:, at], mhalf[:, at], ALU.pow).then_inc(tail_pow, 1)

            for n in range(CHUNKS + 1):
                if n < CHUNKS:
                    deviation(n)
                if n > 1:
                    finish(pool, n - 2)


def kernel(x, txt, L0_tok_W, L0_tok_b, L0_tok_pos_embd, L0_attn_ln_gamma, L0_attn_ln_beta, L0_attn_W_in,
           L0_attn_b_in, L0_attn_A_log, L0_attn_D_skip, L0_attn_dt_bias, L0_attn_W_out, L0_attn_b_out, L0_ffn_Wr,
           L0_ffn_br, L0_ffn_W1, L0_ffn_b1, L0_ffn_W2, L0_ffn_b2, L0_ffn_gamma, L0_ffn_beta):
    import concourse.bacc as bacc
    from concourse.bass_utils import run_bass_kernel_spmd

    def tiles(w, k):
        return np.asarray(w).reshape(k, P, -1).transpose(1, 0, 2)

    side = 16
    per = 96 // side
    patches = np.asarray(x).reshape(BATCH, 3, per, side, per, side).transpose(1, 3, 5, 0, 2, 4)
    w1 = np.asarray(L0_ffn_W1).transpose(0, 2, 1).reshape(EXPERTS, KD, P, HIDDEN).transpose(0, 2, 1, 3)
    w2 = np.asarray(L0_ffn_W2).transpose(0, 2, 1).reshape(EXPERTS, KF, P, DIM).transpose(0, 2, 1, 3)
    b_in = np.asarray(L0_attn_b_in)
    eye = np.eye(P, dtype=np.float32)
    arrays = {
        "patch": tiles(patches.reshape(PATCH, BATCH * IMG), KP),
        "w_tok": tiles(np.asarray(L0_tok_W).T, KP),
        "txt": txt,
        "pos": np.asarray(L0_tok_pos_embd)[0],
        "tok_b": L0_tok_b,
        "w_in": tiles(L0_attn_W_in, KD),
        "w_out": tiles(L0_attn_W_out, KI),
        "wr": tiles(np.asarray(L0_ffn_Wr).T, KD),
        "b_bc": b_in[C_BC:C_DT].reshape(P, 1),
        "b_x": b_in[C_X:C_BC],
        "b_z": b_in[C_Z:C_X],
        "b_out": L0_attn_b_out,
        "gam_t": np.asarray(L0_attn_ln_gamma).reshape(KD, P).T,
        "bet_t": np.asarray(L0_attn_ln_beta).reshape(KD, P).T,
        "rows8": np.concatenate([b_in[C_DT:], np.asarray(L0_attn_dt_bias), np.asarray(L0_attn_A_log),
                                 np.asarray(L0_attn_D_skip), np.asarray(L0_ffn_br)]),
        "experts": np.concatenate([w1.reshape(EXPERTS, P, -1), w2.reshape(EXPERTS, P, -1)], axis=2),
        "b1": np.asarray(L0_ffn_b1)[::-1].reshape(EXPERTS, KF, P).transpose(0, 2, 1),
        "b2": np.asarray(L0_ffn_b2)[::-1].reshape(BIAS_ROWS, P),
        "f_gam": L0_ffn_gamma,
        "f_bet": L0_ffn_beta,
        "ident": eye,
        "delta": np.tile(eye[:LEN, :LEN], (1, HPB)),
        "iota8": np.tile(np.arange(EXPERTS, dtype=np.float32), (LEN, 2 * TOP)),
        "small": np.concatenate([P * np.arange(1, REGION), np.arange(TILES),
                                 REGION * P * np.arange(EXPERTS)]).astype(np.float32),
        "before": np.concatenate([np.triu(np.ones((LEN, LEN)), 1), np.ones((LEN, LEN))], axis=1).astype(np.float32),
        "rowmask": np.where(np.arange(LEN) == 0, -1e30, 0.0).astype(np.float32).reshape(LEN, 1),
    }
    goal = np.arange(TOP * BATCH * LEN, dtype=np.uint32).reshape(TOP * BATCH, LEN).T
    arrays["goals"] = goal
    arrays["unlisted"] = (TOP * TOK + np.arange(TILES * P, dtype=np.uint32)).reshape(TILES * P, 1)
    arrays = {f"in_{k}": np.ascontiguousarray(v) for k, v in arrays.items()}
    nc = bacc.Bacc("TRN2", target_bir_lowering=False, num_devices=1)
    d = {k[3:]: nc.dram_tensor(k, v.shape, U32 if v.dtype == np.uint32 else F32, kind="ExternalInput").ap()
         for k, v in arrays.items()}
    out = nc.dram_tensor("out", (BATCH, LEN, DIM), F32, kind="ExternalOutput").ap()
    build(nc, d, out)
    r = run_bass_kernel_spmd(nc, [arrays], core_ids=[0])
    return r.results[0]["out"]
```
